# Optimizing a Trainium2 kernel written in Bass

```python
import numpy as np
import jax
import jax.numpy as jnp

def _softmax(x, axis=-1):
    return jax.nn.softmax(x, axis=axis)

def _gelu(x):
    return jax.nn.gelu(x, approximate=True)

def _silu(x):
    return jax.nn.silu(x)

def _sigmoid(x):
    return jax.nn.sigmoid(x)

def _layernorm(x, axis=-1, eps=1e-05):
    m = jnp.mean(x, axis=axis, keepdims=True)
    v = jnp.var(x, axis=axis, keepdims=True)
    return (x - m) / jnp.sqrt(v + eps)

def _scatter_add(tgt, idx, src, axis=0):
    return tgt.at[idx].add(src)

def _segment_sum(src, seg, n):
    return jax.ops.segment_sum(src, seg, n)
kernel_name = 'mk_xattn_ffn_d1_seqx_r4_45e52d'

def setup_inputs(seed: int=0):
    np.random.seed(seed)
    _w = jnp.asarray

    def _rec_inputs():
        import jax
        import jax.numpy as jnp
        _rk = jax.random.key(seed)
        x = 7.22e-05 + 1 * jax.random.normal(jax.random.fold_in(_rk, 1), (16, 112, 1024), jnp.float32)
        _lenS = 112 - jax.random.randint(jax.random.fold_in(_rk, 7), (16,), 0, max(1, 112 // 4) + 1, jnp.int32)
        _lenS2 = 375 - jax.random.randint(jax.random.fold_in(_rk, 8), (16,), 0, max(1, 375 // 4) + 1, jnp.int32)
        _ctx_4096P = jax.random.normal(jax.random.fold_in(_rk, 11), (16, 16, 1024), jnp.float32)
        _ctx_4096c = jax.random.dirichlet(jax.random.fold_in(_rk, 511), 0.3 * jnp.ones((16,), jnp.float32), (16, 375))
        _ctx_4096t = jnp.einsum('bsk,bkd->bsd', _ctx_4096c, _ctx_4096P)
        _ctx_4096t = _ctx_4096t * jax.lax.rsqrt(jnp.mean(jnp.square(_ctx_4096t)) + 1e-12) * 0.953939
        ctx_4096 = 2.81802e-05 + 1.00001 * (_ctx_4096t + 0.3 * jax.random.normal(jax.random.fold_in(_rk, 611), (16, 375, 1024), jnp.float32))
        return (x, ctx_4096)
    x, ctx_4096 = _rec_inputs()

    def _L0_xattn_setup():
        import jax, jax.numpy as jnp
        import numpy as np
        HIDDEN = 1024
        N_HEADS = 32
        N_KV_HEADS = 8
        HEAD_DIM = HIDDEN // N_HEADS
        N_REP = N_HEADS // N_KV_HEADS
        EPS = 1e-05

        def _rmsnorm(x, w):
            xf = x.astype(jnp.float32)
            var = jnp.mean(xf * xf, axis=-1, keepdims=True)
            return (xf * jax.lax.rsqrt(var + EPS)).astype(x.dtype) * w
        key = jax.random.key(seed)
        ks = jax.random.split(key, 7)
        B, Q, K = (2, 256, 512)
        scale = 0.02
        return {'hidden_states': jax.random.normal(ks[0], (B, Q, HIDDEN), jnp.float32), 'encoder_hidden_states': jax.random.normal(ks[1], (B, K, HIDDEN), jnp.float32), 'wq': jax.random.normal(ks[2], (N_HEADS * HEAD_DIM, HIDDEN), jnp.float32) * scale, 'wk': jax.random.normal(ks[3], (N_KV_HEADS * HEAD_DIM, HIDDEN), jnp.float32) * scale, 'wv': jax.random.normal(ks[4], (N_KV_HEADS * HEAD_DIM, HIDDEN), jnp.float32) * scale, 'wo': jax.random.normal(ks[5], (HIDDEN, N_HEADS * HEAD_DIM), jnp.float32) * scale, 'ln_w': jnp.ones((HIDDEN,), jnp.float32)}
    _L0_xattn_all = _L0_xattn_setup()
    _L0_xattn_in = {k: v for k, v in _L0_xattn_all.items() if k in ('wq', 'wk', 'wv', 'wo', 'ln_w')}
    del _L0_xattn_all

    def _L0_ffn_setup():
        import jax, jax.numpy as jnp
        import numpy as np

        @jax.custom_vjp
        def ste_sign(w):
            return jnp.sign(w)

        def _ste_fwd(w):
            return (jnp.sign(w), w)

        def _ste_bwd(w, g):
            mask = ((w > -1) & (w < 1)).astype(g.dtype)
            return (g * mask,)
        ste_sign.defvjp(_ste_fwd, _ste_bwd)
        key = jax.random.key(seed)
        k = jax.random.split(key, 6)
        B, S, H, O, E = (4, 512, 1024, 1024, 8)
        return {'x': jax.random.normal(k[0], (B, S, H), dtype=jnp.float32), 'weight': jax.random.normal(k[1], (O, H), dtype=jnp.float32) * 0.02, 'bias': jax.random.normal(k[2], (O,), dtype=jnp.float32) * 0.02, 'gate_w': jax.random.normal(k[3], (E, H), dtype=jnp.float32) * 0.02, 'in_channel_scale': jax.random.normal(k[4], (E, H), dtype=jnp.float32), 'out_channel_scale': jax.random.normal(k[5], (E, O), dtype=jnp.float32)}
    _L0_ffn_all = _L0_ffn_setup()
    _L0_ffn_in = {k: v for k, v in _L0_ffn_all.items() if k in ('weight', 'bias', 'gate_w', 'in_channel_scale', 'out_channel_scale')}
    del _L0_ffn_all
    return {'x': x, 'ctx_4096': ctx_4096, 'L0_xattn_wq': _L0_xattn_in['wq'], 'L0_xattn_wk': _L0_xattn_in['wk'], 'L0_xattn_wv': _L0_xattn_in['wv'], 'L0_xattn_wo': _L0_xattn_in['wo'], 'L0_xattn_ln_w': _L0_xattn_in['ln_w'], 'L0_ffn_weight': _L0_ffn_in['weight'], 'L0_ffn_bias': _L0_ffn_in['bias'], 'L0_ffn_gate_w': _L0_ffn_in['gate_w'], 'L0_ffn_in_channel_scale': _L0_ffn_in['in_channel_scale'], 'L0_ffn_out_channel_scale': _L0_ffn_in['out_channel_scale']}

def reference(x, ctx_4096, L0_xattn_wq, L0_xattn_wk, L0_xattn_wv, L0_xattn_wo, L0_xattn_ln_w, L0_ffn_weight, L0_ffn_bias, L0_ffn_gate_w, L0_ffn_in_channel_scale, L0_ffn_out_channel_scale):
    import jax
    import jax.numpy as jnp

    def _L0_xattn_ref(hidden_states, encoder_hidden_states, wq, wk, wv, wo, ln_w):
        import jax, jax.numpy as jnp
        import numpy as np
        HIDDEN = 1024
        N_HEADS = 32
        N_KV_HEADS = 8
        HEAD_DIM = HIDDEN // N_HEADS
        N_REP = N_HEADS // N_KV_HEADS
        EPS = 1e-05

        def _rmsnorm(x, w):
            xf = x.astype(jnp.float32)
            var = jnp.mean(xf * xf, axis=-1, keepdims=True)
            return (xf * jax.lax.rsqrt(var + EPS)).astype(x.dtype) * w
        B, Qlen, _ = hidden_states.shape
        _, Klen, _ = encoder_hidden_states.shape
        x = _rmsnorm(hidden_states, ln_w)
        q = jnp.einsum('bqd,hd->bqh', x, wq).reshape(B, Qlen, N_HEADS, HEAD_DIM)
        k = jnp.einsum('bkd,hd->bkh', encoder_hidden_states, wk).reshape(B, Klen, N_KV_HEADS, HEAD_DIM)
        v = jnp.einsum('bkd,hd->bkh', encoder_hidden_states, wv).reshape(B, Klen, N_KV_HEADS, HEAD_DIM)
        q = q.transpose(0, 2, 1, 3)
        k = k.transpose(0, 2, 1, 3)
        v = v.transpose(0, 2, 1, 3)
        k = jnp.repeat(k, N_REP, axis=1)
        v = jnp.repeat(v, N_REP, axis=1)
        scores = jnp.einsum('bhqd,bhkd->bhqk', q, k) / np.sqrt(HEAD_DIM).astype(np.float32)
        attn = jax.nn.softmax(scores.astype(jnp.float32), axis=-1).astype(q.dtype)
        out = jnp.einsum('bhqk,bhkd->bhqd', attn, v)
        out = out.transpose(0, 2, 1, 3).reshape(B, Qlen, HIDDEN)
        return jnp.einsum('bqh,dh->bqd', out, wo)

    def _L0_ffn_ref(x, weight, bias, gate_w, in_channel_scale, out_channel_scale):
        import jax, jax.numpy as jnp
        import numpy as np

        @jax.custom_vjp
        def ste_sign(w):
            return jnp.sign(w)

        def _ste_fwd(w):
            return (jnp.sign(w), w)

        def _ste_bwd(w, g):
            mask = ((w > -1) & (w < 1)).astype(g.dtype)
            return (g * mask,)
        ste_sign.defvjp(_ste_fwd, _ste_bwd)
        B, S, H = x.shape
        xf = x.reshape(-1, H)
        router_logits = xf @ gate_w.T
        routing = jax.nn.softmax(router_logits.astype(jnp.float32), axis=1).astype(x.dtype)
        in_scale = routing @ in_channel_scale
        out_scale = routing @ out_channel_scale
        wb = ste_sign(weight)
        out = xf * in_scale @ wb.T * out_scale + bias
        return out.reshape(B, S, -1)
    x = x + _L0_xattn_ref(_layernorm(x, axis=-1), ctx_4096, L0_xattn_wq, L0_xattn_wk, L0_xattn_wv, L0_xattn_wo, L0_xattn_ln_w)
    x = x + _L0_ffn_ref(_layernorm(x, axis=-1), L0_ffn_weight, L0_ffn_bias, L0_ffn_gate_w, L0_ffn_in_channel_scale, L0_ffn_out_channel_scale)
    return x

_drawn_inputs = setup_inputs


def setup_inputs(seed=0):
    import zlib

    import numpy as np

    out = dict(_drawn_inputs(seed))
    spreads = {'L0_xattn_ln_w': (1.0, 0.6)}
    factors = {'L0_ffn_bias': 8.0}
    for name, (base, spread) in spreads.items():
        noise = np.random.default_rng([zlib.crc32(name.encode()), seed]).standard_normal(out[name].shape)
        drawn = base * np.exp(spread * noise) if base else spread * noise
        out[name] = jnp.asarray(drawn.astype(out[name].dtype))
    for name, factor in factors.items():
        out[name] = (out[name] * factor).astype(out[name].dtype)
    return out
```

```python
from contextlib import ExitStack

import numpy as np

import concourse.bass as bass
from concourse import mybir

F32 = mybir.dt.float32
F32R = mybir.dt.float32r
ALU = mybir.AluOpType
ACT = mybir.ActivationFunctionType
AX = mybir.AxisListType.X

P = 128
B, Q, D = 16, 112, 1024
K, KP = 375, 376
NH, NG, HD = 32, 8, 32
REP = NH // NG
NC = D // P
KC = 3
KCS = K // KC
T = B * Q
GB = 4
QG = GB * Q
NQG = B // GB
NE = 8
EPS = 1e-5
SCALE = float(HD) ** -0.5
VW = 2 * HD + 2
TT = 128
NT = T // TT
HALF = D // 2
EROWS = 72


def f(ap):
    return ap.bitcast(F32)


def phase_queries(nc, x, wq_t, ln_w, q_scr, ident):
    with ExitStack() as ctx:
        sb = lambda n, s, d=F32: ctx.enter_context(nc.sbuf_tensor(n, s, d))
        sem = lambda n: ctx.enter_context(nc.semaphore(n))
        w_raw = sb("q_w_raw", [P, 2, D])
        w_hi = sb("q_w_hi", [P, NC, D], F32R)
        w_lo = sb("q_w_lo", [P, NC, D], F32R)
        lnw = sb("q_lnw", [P, NC])
        x_in = sb("q_x_in", [Q, 2, D])
        x_n = sb("q_x_n", [Q, 2, D])
        stats = sb("q_stats", [Q, 2, 12])
        mv = sb("q_mv", [Q, 2, 2])
        rstd = sb("q_rstd", [Q, 2, 1])
        var = sb("q_var", [Q, 2, 1])
        half_pow = sb("q_half_pow", [Q, 1])
        xt_hi = [sb(f"q_xt_hi{i}", [P, NC, QG], F32R) for i in range(2)]
        xt_lo = [sb(f"q_xt_lo{i}", [P, NC, QG], F32R) for i in range(2)]
        q_hi = [sb(f"q_hi{i}", [P, QG], F32R) for i in range(4)]
        q_lo = [sb(f"q_lo{i}", [P, QG], F32R) for i in range(4)]
        xp = ctx.enter_context(nc.psum_tensor("q_xp", [P, 2, 512], F32))
        qp = [ctx.enter_context(nc.psum_tensor(f"q_qp{i}", [P, 512], F32)) for i in range(4)]

        lnw_in = sem("q_lnw_in")
        w_in = [sem(f"q_w_in{i}") for i in range(2)]
        whi_ready = sem("q_whi_ready")
        wlo_ready = sem("q_wlo_ready")
        xin = [sem(f"q_xin{i}") for i in range(2)]
        stat_step = sem("q_stat_step")
        var_ready = sem("q_var_ready")
        rstd_ready = sem("q_rstd_ready")
        xn_ready = sem("q_xn_ready")
        xp_ready = sem("q_xp_ready")
        xhi_ready = sem("q_xhi_ready")
        xlo_ready = sem("q_xlo_ready")
        q_mm = sem("q_mm")
        qhi_ready = sem("q_qhi_ready")
        qlo_ready = sem("q_qlo_ready")
        q_out = [sem(f"q_out{i}") for i in range(4)]
        const_ready = sem("q_const_ready")

        wq_v = wq_t.rearrange("(c p) h -> c p h", p=P)
        NOUT = 2 * REP * 16

        def batches_before(g):
            return {0: 0, 2: 1, 4: 2, 6: 3}.get(g)

        with nc.Block() as block:
            @block.sync
            def _(sp):
                sp.dma_start(lnw[:], ln_w).then_inc(lnw_in, 16)

                def load_x(b):
                    if b >= 2:
                        sp.wait_ge(xn_ready, b - 1)
                    sp.dma_start(x_in[:, b % 2, :], x[b]).then_inc(xin[b % 2], 16)

                def load_w(c):
                    if c >= 2:
                        sp.wait_ge(wlo_ready, c - 1)
                    sp.dma_start(w_raw[:, c % 2, :], wq_v[c]).then_inc(w_in[c % 2], 16)

                load_x(0)
                load_w(0)
                load_w(1)
                load_x(1)
                for c in range(2, NC):
                    load_w(c)
                    if c in (3, 5):
                        load_x(2 + (c - 3) // 2)

                def store_q(i):
                    g, grp = i % NG, i // NG
                    sp.wait_ge(qlo_ready, i + 1)
                    for hl, tile in ((0, q_hi), (1, q_lo)):
                        for r in range(REP):
                            src = f(tile[i % 4][HD * r:HD * r + HD, :]).rearrange("p (b t) -> p b t", b=GB)
                            dst = q_scr[hl, :, grp * GB:(grp + 1) * GB, g, r, :]
                            sp.dma_start(dst, src).then_inc(q_out[i % 4], 16)

                for i in range(NQG * NG):
                    nxt = batches_before(i % NG)
                    b = (i // NG + 1) * GB + (nxt if nxt is not None else 0)
                    if nxt is not None and b < B:
                        load_x(b)
                    store_q(i)
                for s in range(4):
                    sp.wait_ge(q_out[s], NOUT * (NQG * NG // 4))

            def steps():
                out = [("x", b) for b in range(GB)]
                for i in range(NQG * NG):
                    out.append(("q", i))
                    nxt = batches_before(i % NG)
                    b = (i // NG + 1) * GB + (nxt if nxt is not None else 0)
                    if nxt is not None and b < B:
                        out.append(("x", b))
                return out

            @block.gpsimd
            def _(pool):
                pool.wait_ge(const_ready, 1)
                for b in range(B):
                    pool.wait_ge(var_ready, b + 1)
                    if b >= 2:
                        pool.wait_ge(xn_ready, b - 1)
                    pool.tensor_tensor(rstd[:, b % 2, :], var[:, b % 2, :], half_pow[:], ALU.pow).then_inc(rstd_ready, 1)

            @block.vector
            def _(dve):
                dve.memset(half_pow[:], -0.5).then_inc(const_ready, 1)

                def normalise(b):
                    s = b % 2
                    dve.wait_ge(xin[s], 16 * (b // 2 + 1))
                    for h in range(2):
                        dve.bn_stats(stats[:, s, 6 * h:6 * h + 6], x_in[:, s, HALF * h:HALF * (h + 1)]).then_inc(stat_step, 1)
                    dve.wait_ge(stat_step, 3 * b + 2)
                    dve.bn_aggr(mv[:, s, :], stats[:, s, :]).then_inc(stat_step, 1)
                    dve.wait_ge(stat_step, 3 * b + 3)
                    dve.tensor_scalar(var[:, s, :], mv[:, s, 1:2], 1.0 + EPS, EPS * EPS, ALU.mult, ALU.add).then_inc(var_ready, 1)
                    dve.wait_ge(rstd_ready, b + 1)
                    if b >= 2:
                        dve.wait_ge(xp_ready, b - 1)
                    dve.tensor_scalar(x_n[:, s, :], x_in[:, s, :], mv[:, s, 0:1], rstd[:, s, :],
                                      ALU.subtract, ALU.mult).then_inc(xn_ready, 1)

                def split_w(c):
                    dve.wait_ge(whi_ready, c + 1)
                    dve.scalar_tensor_tensor(out=w_lo[:, c, :], in0=w_raw[:, c % 2, :], scalar=lnw[:, c:c + 1],
                                             in1=f(w_hi[:, c, :]), op0=ALU.mult, op1=ALU.subtract).then_inc(wlo_ready, 1)

                def split_x(b):
                    grp, t0 = b // GB, (b % GB) * Q
                    dve.wait_ge(xhi_ready, b + 1)
                    dst = xt_lo[grp % 2][:, :, t0:t0 + Q].rearrange("p (k c) t -> p k c t", k=2)
                    hi = f(xt_hi[grp % 2][:, :, t0:t0 + Q]).rearrange("p (k c) t -> p k c t", k=2)
                    src = xp[:, :, 0:4 * Q].rearrange("p k (c t) -> p k c t", c=4)
                    dve.tensor_tensor(dst, src, hi, ALU.subtract).then_inc(xlo_ready, 1)

                normalise(0)
                normalise(1)
                split_w(0)
                split_w(1)
                split_x(0)
                normalise(2)
                split_w(2)
                split_w(3)
                split_x(1)
                normalise(3)
                split_w(4)
                split_w(5)
                split_x(2)
                split_w(6)
                split_w(7)
                split_x(3)
                for kind, i in steps()[GB:]:
                    if kind == "x":
                        normalise(i)
                        split_x(i)
                    else:
                        dve.wait_ge(qhi_ready, i + 1)
                        if i >= 4:
                            dve.wait_ge(q_out[i % 4], NOUT * (i // 4))
                        dve.tensor_tensor(q_lo[i % 4][:], qp[i % 4][:, 0:QG], f(q_hi[i % 4][:]), ALU.subtract).then_inc(qlo_ready, 1)

            @block.scalar
            def _(act):
                def split_w(c):
                    act.wait_ge(w_in[c % 2], 16 * (c // 2 + 1))
                    act.activation(w_hi[:, c, :], w_raw[:, c % 2, :], ACT.Copy, scale=lnw[:, c:c + 1]).then_inc(whi_ready, 1)

                def split_x(b):
                    grp, t0 = b // GB, (b % GB) * Q
                    act.wait_ge(xp_ready, b + 1)
                    if grp >= 2:
                        act.wait_ge(q_mm, NG * (grp - 1))
                    dst = xt_hi[grp % 2][:, :, t0:t0 + Q].rearrange("p (k c) t -> p k c t", k=2)
                    src = xp[:, :, 0:4 * Q].rearrange("p k (c t) -> p k c t", c=4)
                    act.copy(dst, src).then_inc(xhi_ready, 1)

                act.wait_ge(lnw_in, 16)
                for c in range(NC):
                    split_w(c)
                    if c % 2:
                        split_x(c // 2)
                for kind, i in steps()[GB:]:
                    if kind == "x":
                        split_x(i)
                    else:
                        act.wait_ge(q_mm, i + 1)
                        if i >= 4:
                            act.wait_ge(q_out[i % 4], NOUT * (i // 4))
                        act.copy(q_hi[i % 4][:], qp[i % 4][:, 0:QG]).then_inc(qhi_ready, 1)

            @block.tensor
            def _(pe):
                for kind, i in steps():
                    if kind == "x":
                        pe.wait_ge(xn_ready, i + 1)
                        if i >= 1:
                            pe.wait_ge(xlo_ready, i)
                        for c in range(NC):
                            mm = pe.transpose(xp[:, c // 4, (c % 4) * Q:(c % 4 + 1) * Q],
                                              x_n[:, i % 2, c * P:(c + 1) * P], ident[0:Q, 0:Q])
                        mm.then_inc(xp_ready, 1)
                    else:
                        grp, g = i // NG, i % NG
                        if g == 0:
                            pe.wait_ge(xlo_ready, GB * (grp + 1))
                        if i >= 4:
                            pe.wait_ge(qlo_ready, i - 3)
                        for c in range(NC):
                            if i == 0:
                                pe.wait_ge(wlo_ready, c + 1)
                            wh, wl = w_hi[:, c, g * P:(g + 1) * P], w_lo[:, c, g * P:(g + 1) * P]
                            xh, xl = xt_hi[grp % 2][:, c, :], xt_lo[grp % 2][:, c, :]
                            out = qp[i % 4][:, 0:QG]
                            pe.matmul(out, wh, xh, start=(c == 0), stop=False)
                            pe.matmul(out, wh, xl, start=False, stop=False)
                            mm = pe.matmul(out, wl, xh, start=False, stop=(c == NC - 1))
                        mm.then_inc(q_mm, 1)


def phase_attention(nc, ctx_t, wkv_t, q_scr, o_scr, ident):
    with ExitStack() as ctx:
        sb = lambda n, s, d=F32: ctx.enter_context(nc.sbuf_tensor(n, s, d))
        ps = lambda n, s: ctx.enter_context(nc.psum_tensor(n, s, F32))
        sem = lambda n: ctx.enter_context(nc.semaphore(n))
        KV = 2 * NG * HD
        w_hi = sb("a_w_hi", [P, NC, KV], F32R)
        w_lo = sb("a_w_lo", [P, NC, KV], F32R)
        c_raw = sb("a_c_raw", [P, NC, KP])
        c_hi = [sb(f"a_c_hi{i}", [P, NC, KP], F32R) for i in range(2)]
        c_lo = [sb(f"a_c_lo{i}", [P, NC, KP], F32R) for i in range(2)]
        k_hi = sb("a_k_hi", [P, 2, KP], F32R)
        k_lo = sb("a_k_lo", [P, 2, KP], F32R)
        k_st = [sb(f"a_k_st{i}", [3 * HD + 2, NG, KP], F32R) for i in range(2)]
        q_st = [sb(f"a_q_st{i}", [3 * HD + 2, NG, REP * Q], F32R) for i in range(2)]
        v_st = [sb(f"a_v_st{i}", [KCS, KC, NG, VW], F32R) for i in range(2)]
        p_f = [sb(f"a_p_f{i}", [KCS, KC, REP * Q]) for i in range(2)]
        p_hi = [sb(f"a_p_hi{i}", [KCS, KC, REP * Q], F32R) for i in range(2)]
        p_lo = [sb(f"a_p_lo{i}", [KCS, KC, REP * Q], F32R) for i in range(2)]
        o_sb = [sb(f"a_o_sb{i}", [VW, REP * Q]) for i in range(2)]
        row_max = sb("a_row_max", [Q, 2, 16])
        neg_max = sb("a_neg_max", [Q, 2, 32])
        max_t = [sb(f"a_max_t{i}", [32, Q], F32R) for i in range(2)]
        a_ps = ps("a_ps", [P, 2, 512])
        b_ps = ps("b_ps", [P, 3, 512])
        o_ps = ps("o_ps", [P, 512])
        ring = [ps(f"a_ring{i}", [P, 512]) for i in range(2)]

        w_in = [sem(f"a_w_in{i}") for i in range(2)]
        w_hi_ready = sem("a_w_hi_ready")
        w_lo_ready = sem("a_w_lo_ready")
        c_in = sem("a_c_in")
        c_hi_ready = sem("a_c_hi_ready")
        c_lo_ready = sem("a_c_lo_ready")
        ones_ready = sem("a_ones_ready")
        v_mm = sem("a_v_mm")
        v_hi_ready = sem("a_v_hi_ready")
        v_lo_ready = sem("a_v_lo_ready")
        k_mm = sem("a_k_mm")
        k_hi_ready = sem("a_k_hi_ready")
        k_lo_ready = sem("a_k_lo_ready")
        k_in = [[sem(f"a_k_in{i}{c}") for c in range(2)] for i in range(2)]
        q_in = [[sem(f"a_q_in{i}{h}") for h in range(2)] for i in range(2)]
        a_mm = sem("a_a_mm")
        a_max = sem("a_a_max")
        neg_step = sem("a_neg_step")
        neg_ready = sem("a_neg_ready")
        t_mm = sem("a_t_mm")
        t_ready = sem("a_t_ready")
        shift_in = [sem(f"a_shift_in{h}") for h in range(2)]
        b_mm = sem("a_b_mm")
        exp_ready = sem("a_exp_ready")
        p_hi_ready = sem("a_p_hi_ready")
        p_lo_ready = sem("a_p_lo_ready")
        pv_mm = sem("a_pv_mm")
        o_ready = sem("a_o_ready")
        o_out = [sem(f"a_o_out{i}") for i in range(2)]
        waited = sem("a_waited")
        NKD = 12 * 16
        NQD = 3 * 16
        NSD = 2 * 16

        PEEL, LOOPS = 2, 5
        V_PIECES = 9

        def schedule(eng, emit):
            for n in range(-3, PEEL):
                emit(n, n, n % 2, 0)
            with eng.Fori(PEEL // 2, PEEL // 2 + LOOPS) as j:
                emit(None, 2 * j, 0, j)
                emit(None, 2 * j + 1, 1, j)
            for n in range(PEEL + 2 * LOOPS, B):
                emit(n, n, n % 2, 0)

        def on(static, ahead):
            return static is None or 0 <= static + ahead < B

        def pair(static, par, j, ahead):
            return (static + ahead) // 2 if static is not None else j + (par + ahead) // 2

        def w_raw(i):
            flat = c_raw[:].rearrange("p c k -> p (c k)")
            return flat[:, (i % 2) * 2 * KV:(i % 2 + 1) * 2 * KV].rearrange("p (c h) -> p c h", c=2)

        with nc.Block() as block:
            @block.sync
            def _(sp):
                for i in range(NC // 2):
                    if i >= 2:
                        sp.wait_ge(w_lo_ready, i - 1)
                    sp.dma_start(w_raw(i), wkv_t[2 * i:2 * i + 2].rearrange("c p h -> p c h")).then_inc(w_in[i % 2], 16)

                def load_q(b, par, h):
                    g0 = 4 * h
                    for rep, hl in enumerate((0, 1, 0)):
                        dst = f(q_st[par][HD * rep:HD * rep + HD, g0:g0 + 4, :])
                        src = q_scr[hl, :, b, g0:g0 + 4, :, :].rearrange("d g r t -> d g (r t)")
                        sp.dma_start(dst, src).then_inc(q_in[par][h], 16)

                def stack_k(par, c):
                    for rep, tile in enumerate((k_hi, k_hi, k_lo)):
                        for i in range(4):
                            sp.dma_start(f(k_st[par][HD * rep:HD * rep + HD, 4 * c + i, :]),
                                         f(tile[HD * i:HD * i + HD, c, :])).then_inc(k_in[par][c], 16)

                def shift(par, h):
                    for hl in range(2):
                        dst = f(q_st[par][96 + hl:97 + hl, 4 * h:4 * h + 4, :]).rearrange("p g (r t) -> p (g r) t", t=Q)
                        sp.dma_start(dst, f(max_t[h][16 * hl:16 * hl + 16, :])).then_inc(shift_in[h], 16)

                def store_o(b, g):
                    sp.dma_start(o_scr[:, g, :, b, :], o_sb[g % 2][:].rearrange("p (r t) -> p r t", r=REP)).then_inc(o_out[g % 2], 16)

                def emit(s, n, par, j):
                    for g in range(NG):
                        if g == 1 and on(s, 3):
                            if s == -3:
                                sp.wait_ge(w_lo_ready, NC // 2)
                            else:
                                sp.wait_ge(c_hi_ready, 2 * (n + 3))
                                sp.wait_ge(c_lo_ready, 2 * (n + 3))
                            sp.dma_start(c_raw[:], ctx_t[n + 3]).then_inc(c_in, 16)
                        if g == 2 and on(s, 0):
                            sp.wait_ge(t_ready, 2 * (n + 1))
                            shift(par, 1)
                        if g == 4 and on(s, 2):
                            if on(s, 0):
                                sp.wait_ge(b_mm, NG * n + 4)
                            load_q(n + 2, par, 0)
                        if g == 6 and on(s, 1):
                            sp.wait_ge(t_ready, 2 * (n + 1) + 1)
                            shift(1 - par, 0)
                        if g == 6 and on(s, 2):
                            sp.wait_ge(k_lo_ready, 2 * (n + 2) + 1)
                            stack_k(par, 0)
                        if g >= 2 and on(s, 0):
                            sp.wait_ge(o_ready, NG * n + g - 1)
                            store_o(n, g - 2)
                        if g < 2 and on(s, -1):
                            sp.wait_ge(o_ready, NG * n + g - 1)
                            store_o(n - 1, NG - 2 + g)
                    if on(s, 2):
                        sp.wait_ge(k_lo_ready, 2 * (n + 2) + 2)
                        sp.sem_inc(waited, 1)
                        if on(s, 0):
                            sp.wait_ge(b_mm, NG * (n + 1))
                        stack_k(par, 1)
                        load_q(n + 2, par, 1)

                schedule(sp, emit)
                for g in (NG - 2, NG - 1):
                    sp.wait_ge(o_ready, NG * (B - 1) + g + 1)
                    store_o(B - 1, g)
                for i in range(2):
                    sp.wait_ge(o_out[i], 16 * B * NG // 2)

            @block.tensor
            def _(pe):
                pe.wait_ge(w_lo_ready, NC // 2)
                pe.wait_ge(ones_ready, 4)

                def scores_rows(s, b, par, jj, g, p):
                    if p == 0 and g % 4 == 0:
                        pe.wait_ge(k_in[par][g // 4], NKD * (jj + 1))
                        pe.wait_ge(q_in[par][g // 4], NQD * (jj + 1))
                    if s is None or s > 0 or g > 0 or p > 0:
                        pe.wait_ge(a_max, 16 * b + 2 * g + p)
                    for i in range(2):
                        r = 2 * p + i
                        mm = pe.matmul(a_ps[0:Q, i, 0:KP], q_st[par][0:96, g, r * Q:(r + 1) * Q],
                                       k_st[par][0:96, g, :], start=True, stop=True)
                    mm.then_inc(a_mm, 1)

                def scores_cols(s, b, par, g):
                    if g % 4 == 0:
                        pe.wait_ge(shift_in[g // 4], NSD * (b + 1))
                    if s is None or s > 0 or g > 0:
                        pe.wait_ge(exp_ready, NG * b + g)
                    for c in range(KC):
                        mm = pe.matmul(b_ps[0:KCS, c, 0:REP * Q], k_st[par][:, g, c * KCS:(c + 1) * KCS],
                                       q_st[par][:, g, :], start=True, stop=True)
                    mm.then_inc(b_mm, 1)

                def pv(s, b, par, g):
                    pe.wait_ge(p_lo_ready, NG * b + g + 1)
                    if g % NG == 0:
                        pe.wait_ge(v_lo_ready, KC * (b + 1))
                    if s is None or s > 0 or g > 0:
                        pe.wait_ge(o_ready, NG * b + g)
                    for c in range(KC):
                        w = v_st[par][:, c, g, :]
                        pe.matmul(o_ps[0:VW, 0:REP * Q], w, p_hi[g % 2][:, c, :], start=(c == 0), stop=False)
                        mm = pe.matmul(o_ps[0:VW, 0:REP * Q], w, p_lo[g % 2][:, c, :], start=False, stop=(c == KC - 1))
                    mm.then_inc(pv_mm, 1)

                def max_turn(s, b, h):
                    pe.wait_ge(neg_ready, 2 * b + h + 1)
                    pe.transpose(ring[h][0:32, 0:Q], neg_max[:, h, :], ident[0:Q, 0:Q]).then_inc(t_mm, 1)

                def kv_piece(s, n, par, i):
                    if i < V_PIECES:
                        if not on(s, 1):
                            return
                        job, part = divmod(i, 3)
                        bank = ring[(0, 1, 0)[job]]
                        cpar = 1 - par
                        if part == 0 and job == 0:
                            pe.wait_ge(k_lo_ready, 2 * (n + 2))
                        if part == 0 and job == 1 and on(s, 0):
                            pe.wait_ge(t_ready, 2 * n + 2)
                        if part == 0 and job == 2:
                            pe.wait_ge(v_lo_ready, KC * (n + 1) + 1)
                        for st in range(8 * part, 8 * part + 8):
                            c, pas = divmod(st, 3)
                            a = (c_hi, c_lo, c_hi)[pas][cpar][:, c, job * KCS:(job + 1) * KCS]
                            w = (w_hi, w_hi, w_lo)[pas][:, c, NG * HD:]
                            mm = pe.matmul(bank[0:KCS, 0:NG * HD], a, w, start=(st == 0), stop=(st == 23))
                        if part == 2:
                            mm.then_inc(v_mm, 1)
                    elif i < V_PIECES + 6:
                        if not on(s, 2):
                            return
                        job, part = divmod(i - V_PIECES, 3)
                        bank = ring[(1, 0)[job]]
                        if part == 0 and job == 0:
                            pe.wait_ge(c_lo_ready, 2 * (n + 3))
                            pe.wait_ge(c_hi_ready, 2 * (n + 3))
                            if on(s, 1):
                                pe.wait_ge(v_lo_ready, KC * (n + 1) + 2)
                        if part == 0 and job == 1 and on(s, 1):
                            pe.wait_ge(t_ready, 2 * (n + 1) + 1)
                        for st in range(8 * part, 8 * part + 8):
                            c, pas = divmod(st, 3)
                            a = (c_hi, c_lo, c_hi)[pas][par][:, c, :]
                            w = (w_hi, w_hi, w_lo)[pas][:, c, job * P:(job + 1) * P]
                            mm = pe.matmul(bank[:, 0:KP], w, a, start=(st == 0), stop=(st == 23))
                        if part == 2:
                            mm.then_inc(k_mm, 1)

                def emit(s, n, par, j):
                    for g in range(NG):
                        if on(s, 1):
                            scores_rows(None if s is None else s + 1, n + 1, 1 - par, pair(s, par, j, 1), g, 0)
                        if g == 1 and on(s, 0):
                            pe.wait_ge(k_lo_ready, 2 * (n + 2) if on(s, 1) else 2 * B)
                            if not on(s, 2):
                                pe.wait_ge(v_lo_ready, KC * B if not on(s, 1) else KC * (n + 1))
                            max_turn(s, n, 1)
                        if g == 5 and on(s, 1):
                            pe.wait_ge(v_lo_ready, KC * (n + 2))
                            max_turn(s, n + 1, 0)
                        if on(s, 0):
                            scores_cols(s, n, par, g)
                        if g >= 2 and on(s, 0):
                            pv(s, n, par, g - 2)
                        if g < 2 and on(s, -1):
                            pv(None if s is None else s - 1, n - 1, 1 - par, NG - 2 + g)
                        kv_piece(s, n, par, 2 * g)
                        if on(s, 1):
                            scores_rows(None if s is None else s + 1, n + 1, 1 - par, pair(s, par, j, 1), g, 1)
                        kv_piece(s, n, par, 2 * g + 1)

                schedule(pe, emit)
                pv(B - 1, B - 1, (B - 1) % 2, NG - 2)
                pv(B - 1, B - 1, (B - 1) % 2, NG - 1)

            @block.vector
            def _(dve):
                for i in range(2):
                    dve.memset(f(k_st[i][96:98, :, :]), 1.0).then_inc(ones_ready, 1)
                    dve.memset(f(v_st[i][:, :, :, 2 * HD:VW]), 1.0).then_inc(ones_ready, 1)
                for i in range(NC // 2):
                    dve.wait_ge(w_hi_ready, i + 1)
                    dve.tensor_tensor(w_lo[:, 2 * i:2 * i + 2, :], w_raw(i), f(w_hi[:, 2 * i:2 * i + 2, :]),
                                      ALU.subtract).then_inc(w_lo_ready, 1)

                def row_maxima(b, g, p):
                    dve.wait_ge(a_mm, 16 * b + 2 * g + p + 1)
                    dve.tensor_reduce(row_max[:, g // 4, (g % 4) * 4 + 2 * p:(g % 4) * 4 + 2 * p + 2],
                                      a_ps[0:Q, :, 0:K], AX, ALU.max).then_inc(a_max, 1)

                def negate(s, b, h):
                    dve.wait_ge(a_max, 16 * b + 8 * h + 8)
                    if s is None or s > 0:
                        dve.wait_ge(t_mm, 2 * b + h - 1)
                    dve.tensor_scalar(neg_max[:, h, 0:16].bitcast(F32R), row_max[:, h, :], -1.0, None, ALU.mult).then_inc(neg_step, 1)
                    dve.wait_ge(neg_step, 2 * b + h + 1)
                    dve.scalar_tensor_tensor(out=neg_max[:, h, 16:32], in0=row_max[:, h, :], scalar=-1.0,
                                             in1=neg_max[:, h, 0:16], op0=ALU.mult, op1=ALU.subtract).then_inc(neg_ready, 1)

                def take_turned(s, b, h):
                    dve.wait_ge(t_mm, 2 * b + h + 1)
                    if s is None or s > 0:
                        dve.wait_ge(shift_in[h], NSD * b)
                    dve.tensor_copy(max_t[h][:], ring[h][0:32, 0:Q]).then_inc(t_ready, 1)

                def split_p(s, b, g):
                    dve.wait_ge(exp_ready, NG * b + g + 1)
                    if s is None or s > 0 or g >= 2:
                        dve.wait_ge(pv_mm, NG * b + g - 1)
                    dve.tensor_copy(p_hi[g % 2][:], p_f[g % 2][:]).then_inc(p_hi_ready, 1)

                def split_v(b, par, job):
                    dve.wait_ge(v_hi_ready, KC * b + job + 1)
                    src = ring[(0, 1, 0)[job]][0:KCS, 0:NG * HD].rearrange("p (g d) -> p g d", g=NG)
                    dve.tensor_tensor(v_st[par][:, job, :, HD:2 * HD], src, f(v_st[par][:, job, :, 0:HD]),
                                      ALU.subtract).then_inc(v_lo_ready, 1)

                def split_k(s, b, par, jj, job):
                    dve.wait_ge(k_hi_ready, 2 * b + job + 1)
                    dve.tensor_tensor(k_lo[:, job, :], ring[(1, 0)[job]][:, 0:KP], f(k_hi[:, job, :]),
                                      ALU.subtract).then_inc(k_lo_ready, 1)

                def split_ctx(b, par, h):
                    dve.wait_ge(c_hi_ready, 2 * b + h + 1)
                    cs = slice(4 * h, 4 * h + 4)
                    dve.tensor_tensor(c_lo[par][:, cs, :], c_raw[:, cs, :], f(c_hi[par][:, cs, :]), ALU.subtract).then_inc(c_lo_ready, 1)

                def emit(s, n, par, j):
                    for g in range(NG):
                        if on(s, 1):
                            row_maxima(n + 1, g, 0)
                        if g == 1 and on(s, 0):
                            take_turned(s, n, 1)
                        if g == 5 and on(s, 1):
                            take_turned(None if s is None else s + 1, n + 1, 0)
                        if g >= 1 and on(s, 0):
                            split_p(s, n, g - 1)
                        if g == 0 and on(s, -1):
                            split_p(None if s is None else s - 1, n - 1, NG - 1)
                        if on(s, 1):
                            row_maxima(n + 1, g, 1)
                            if g == 3:
                                negate(None if s is None else s + 1, n + 1, 0)
                            if g == 7:
                                negate(None if s is None else s + 1, n + 1, 1)
                            if g in (1, 2, 4):
                                split_v(n + 1, 1 - par, (1, 2, 4).index(g))
                        if g in (5, 7) and on(s, 2):
                            split_k(s, n + 2, par, 0, (5, 7).index(g))
                        if g in (5, 6) and on(s, 3):
                            split_ctx(n + 3, 1 - par, g - 5)

                schedule(dve, emit)
                split_p(B - 1, B - 1, NG - 1)

            @block.gpsimd
            def _(pool):
                def emit(s, n, par, j):
                    for g in range(NG):
                        if on(s, 0):
                            pool.wait_ge(p_hi_ready, NG * n + g + 1)
                            pool.tensor_tensor(p_lo[g % 2][:], p_f[g % 2][:], f(p_hi[g % 2][:]), ALU.subtract).then_inc(p_lo_ready, 1)

                schedule(pool, emit)

            @block.scalar
            def _(act):
                for i in range(NC // 2):
                    act.wait_ge(w_in[i % 2], 16 * (i // 2 + 1))
                    act.copy(w_hi[:, 2 * i:2 * i + 2, :], w_raw(i)).then_inc(w_hi_ready, 1)
                act.wait_ge(w_lo_ready, NC // 2)

                def exponentials(s, b, g):
                    act.wait_ge(b_mm, NG * b + g + 1)
                    if s is None or s > 0 or g >= 2:
                        act.wait_ge(p_lo_ready, NG * b + g - 1)
                    act.activation(p_f[g % 2][:], b_ps[0:KCS, :, 0:REP * Q], ACT.Exp, scale=SCALE).then_inc(exp_ready, 1)

                def take_o(s, b, g):
                    act.wait_ge(pv_mm, NG * b + g + 1)
                    if s is None or s > 0 or g >= 2:
                        act.wait_ge(o_out[g % 2], 16 * (NG // 2 * b + g // 2))
                    act.copy(o_sb[g % 2][:], o_ps[0:VW, 0:REP * Q]).then_inc(o_ready, 1)

                def take_v(s, b, par, job):
                    act.wait_ge(v_mm, KC * b + job + 1)
                    if s is None or s >= 2:
                        act.wait_ge(pv_mm, NG * (b - 1))
                    src = ring[(0, 1, 0)[job]][0:KCS, 0:NG * HD].rearrange("p (g d) -> p g d", g=NG)
                    act.copy(v_st[par][:, job, :, 0:HD], src).then_inc(v_hi_ready, 1)

                def take_k(s, b, par, jj, job):
                    act.wait_ge(k_mm, 2 * b + job + 1)
                    if s is None or s >= 1:
                        act.wait_ge(k_in[1 - par][job], NKD * jj)
                    act.copy(k_hi[:, job, :], ring[(1, 0)[job]][:, 0:KP]).then_inc(k_hi_ready, 1)

                def split_ctx(s, b, par, h):
                    act.wait_ge(c_in, 16 * (b + 1))
                    if s is None or s >= 2:
                        act.wait_ge(v_mm, KC * (b - 1))
                    cs = slice(4 * h, 4 * h + 4)
                    act.copy(c_hi[par][:, cs, :], c_raw[:, cs, :]).then_inc(c_hi_ready, 1)

                def emit(s, n, par, j):
                    ahead = lambda k: None if s is None else s + k
                    for g in range(NG):
                        if on(s, 0):
                            exponentials(s, n, g)
                        if g >= 2 and on(s, 0):
                            take_o(s, n, g - 2)
                        if g < 2 and on(s, -1):
                            take_o(ahead(-1), n - 1, NG - 2 + g)
                        if g in (1, 2, 4) and on(s, 1):
                            take_v(ahead(1), n + 1, 1 - par, (1, 2, 4).index(g))
                        if g in (5, 7) and on(s, 2):
                            take_k(ahead(2), n + 2, par, pair(s, par, j, 3), (5, 7).index(g))
                        if g in (5, 6) and on(s, 3):
                            split_ctx(ahead(3), n + 3, 1 - par, g - 5)

                schedule(act, emit)
                take_o(B - 1, B - 1, NG - 2)
                take_o(B - 1, B - 1, NG - 1)


def phase_output(nc, x, wo_t, wf_t, bias, gate_t, in_scale, out_scale, o_scr, out, ident):
    with ExitStack() as ctx:
        sb = lambda n, s, d=F32: ctx.enter_context(nc.sbuf_tensor(n, s, d))
        ps = lambda n, s: ctx.enter_context(nc.psum_tensor(n, s, F32))
        sem = lambda n: ctx.enter_context(nc.semaphore(n))
        two = range(2)
        wo_hi = sb("o_wo_hi", [P, NC, D], F32R)
        wo_lo = sb("o_wo_lo", [P, NC, D], F32R)
        sign = sb("o_sign", [P, NC, D], F32R)
        gate = sb("o_gate", [P, NC, NE])
        s_raw = sb("o_s_raw", [EROWS, D])
        s_in = sb("o_s_in", [EROWS, D], F32R)
        s_out = sb("o_s_out", [EROWS, D], F32R)
        bias_b = sb("o_bias", [P, D])
        a_t = [sb(f"o_a_t{i}", [P, NC, TT]) for i in two]
        b_t = sb("o_b_t", [P, NC, TT])
        d_t = sb("o_d_t", [P, NC, TT])
        a_hi = sb("o_a_hi", [P, NC, TT], F32R)
        a_lo = sb("o_a_lo", [P, NC, TT], F32R)
        x_in = [sb(f"o_x_in{i}", [TT, D]) for i in two]
        x1 = [sb(f"o_x1{i}", [TT, D]) for i in two]
        x1b = [sb(f"o_x1b{i}", [TT, D]) for i in two]
        x_n = sb("o_x_n", [TT, D])
        x_t = [sb(f"o_x_t{i}", [P, NC, TT]) for i in two]
        xs = sb("o_xs", [P, NC, TT])
        xs_hi = sb("o_xs_hi", [P, NC, TT], F32R)
        xs_lo = sb("o_xs_lo", [P, NC, TT], F32R)
        osc = sb("o_osc", [TT, D])
        y = sb("o_y", [TT, D])
        y_out = sb("o_y_out", [TT, D])
        stats = sb("o_stats", [TT, 12])
        mv = sb("o_mv", [TT, 2])
        var = sb("o_var", [TT, 1])
        rstd = sb("o_rstd", [TT, 1])
        half_pow = sb("o_half_pow", [TT, 1])
        lg_t = sb("o_lg_t", [NE, TT])
        neg = sb("o_neg", [TT, 1])
        ex = sb("o_ex", [TT, NE])
        den = sb("o_den", [TT, 1])
        rden = sb("o_rden", [TT, 1])
        route = sb("o_route", [TT, EROWS])
        route_t = sb("o_route_t", [EROWS, TT], F32R)
        w_ps = ps("o_w_ps", [P, 2, HALF])
        x_ps = ps("o_x_ps", [P, 2, HALF])
        f_ps = ps("o_f_ps", [P, 2, HALF])
        o_ps = ps("o_o_ps", [P, HALF])
        s_ps = ps("o_s_ps", [P, HALF])

        names = """w_hi_ready w_lo_ready neg_w_ready sign_ready small_in zero_ready scale_hi scale_ready
            sum_ready rec_ready at_ready ahi_ready alo_ready w_mm x1_ready stat_step var_ready rstd_ready
            xn_ready x1b_ready xt_mm xt_ready lg_mm lg_ready lt_mm neg_ready ex_ready rden_ready route_hi
            route_ready rt_mm rt_ready is_mm xs_ready xshi_ready xslo_ready os_mm osc_ready f_mm y_ready
            yout_ready const_ready waited_sp waited_pe waited_dve""".split()
        S = {k: sem("o_" + k) for k in names}
        w_in = [sem(f"o_w_in{i}") for i in two]
        scales_in = [sem(f"o_scales_in{i}") for i in two]
        at_in = sem("o_at_in")
        xin = [sem(f"o_xin{i}") for i in two]
        out_done = sem("o_out_done")
        wo_v, wf_v = (w.rearrange("(c p) h -> c p h", p=P) for w in (wo_t, wf_t))
        W_CHUNKS = 2 * NC

        PEEL, LOOPS = 3, 5

        def schedule(eng, emit):
            for n in range(-1, PEEL):
                emit(n, n, n % 2)
            with eng.Fori(PEEL // 2, PEEL // 2 + LOOPS) as j:
                emit(None, 2 * j + 1, 1)
                emit(None, 2 * j + 2, 0)
            for n in range(PEEL + 2 * LOOPS, NT + 2):
                emit(n, n, n % 2)

        def on(static, ahead):
            return static is None or 0 <= static + ahead < NT

        def past(static, ahead, least):
            return static is None or static + ahead >= least

        def slot(static, n, par, ahead):
            return (static + ahead) // 2 if static is not None else None

        flat = lambda ap: ap.rearrange("p k c -> p (k c)")
        chunks = lambda ap: ap.rearrange("p k (c t) -> p (k c) t", c=NC // 2)

        with nc.Block() as block:
            @block.sync
            def _(sp):
                sp.dma_start(gate[:], gate_t).then_inc(S["small_in"], 16)
                sp.dma_start(bias_b[:], bias.rearrange("(a d) -> a d", a=1).broadcast_to([P, D])).then_inc(S["small_in"], 16)

                def load_w(c):
                    if c >= NC + 2:
                        sp.wait_ge(S["sign_ready"], c - NC - 1)
                    elif c >= 2:
                        sp.wait_ge(S["w_lo_ready"], c - 1)
                    sp.dma_start(x1[c % 2][:], (wo_v if c < NC else wf_v)[c % NC]).then_inc(w_in[c % 2], 16)

                def load_scales(i, src):
                    if i == 0:
                        sp.wait_ge(S["zero_ready"], 1)
                    else:
                        sp.wait_ge(S["scale_ready"], 1)
                    for r in range(3):
                        sp.dma_start(s_raw[32 * r:32 * r + NE, :], src).then_inc(scales_in[i], 16)

                def emit(s, n, par):
                    if on(s, 1):
                        if past(s, 0, 0):
                            sp.wait_ge(S["at_ready"], n + 1)
                            sp.sem_inc(S["waited_sp"], 1)
                        if past(s, -1, 0):
                            sp.wait_ge(S["alo_ready"], n)
                        t0 = (n + 1) * TT
                        for r in range(REP):
                            rows = slice(HD * r, HD * r + HD)
                            sp.dma_start(a_t[1 - par][rows, :, :], o_scr[0:HD, :, r, bass.ds(t0, TT)]).then_inc(at_in, 16)
                            sp.dma_start(b_t[rows, :, :], o_scr[HD:2 * HD, :, r, bass.ds(t0, TT)]).then_inc(at_in, 16)
                            sp.dma_start(d_t[rows, :, :], o_scr[2 * HD:2 * HD + 1, :, r, bass.ds(t0, TT)]
                                         .broadcast_to([HD, NC, TT])).then_inc(at_in, 16)
                        if past(s, -1, 0):
                            sp.wait_ge(S["x1_ready"], 2 * n)
                        sp.dma_start(x_in[1 - par][:], x[bass.ds(t0, TT), :]).then_inc(xin[1 - par], 16)
                    if on(s, -2):
                        sp.wait_ge(S["yout_ready"], 2 * (n - 1))
                        sp.dma_start(out[bass.ds((n - 2) * TT, TT), :], y_out[:]).then_inc(out_done, 16)

                for c in range(W_CHUNKS):
                    load_w(c)
                    if c == 1:
                        load_scales(0, in_scale)
                    if c == 5:
                        load_scales(1, out_scale)
                schedule(sp, emit)
                sp.wait_ge(out_done, 16 * NT)

            @block.gpsimd
            def _(pool):
                pool.wait_ge(S["const_ready"], 1)
                pool.wait_ge(S["small_in"], 2 * 16)

                def emit(s, n, par):
                    if on(s, 1):
                        pool.wait_ge(S["ahi_ready"], n + 2)
                        if past(s, 0, 0):
                            pool.wait_ge(S["w_mm"], 2 * n + 2)
                        pool.tensor_tensor(a_lo[:], a_t[1 - par][:], f(a_hi[:]), ALU.subtract).then_inc(S["alo_ready"], 1)
                    if on(s, -2):
                        pool.wait_ge(S["xshi_ready"], n - 1)
                        pool.tensor_tensor(xs_lo[:], xs[:], f(xs_hi[:]), ALU.subtract).then_inc(S["xslo_ready"], 1)
                    if on(s, 0):
                        pool.wait_ge(S["var_ready"], n + 1)
                        pool.tensor_tensor(rstd[:], var[:], half_pow[:], ALU.pow).then_inc(S["rstd_ready"], 1)
                    if on(s, -2):
                        for h in range(2):
                            hs = slice(HALF * h, HALF * (h + 1))
                            pool.wait_ge(S["y_ready"], 2 * (n - 2) + h + 1)
                            if past(s, -2, 1):
                                pool.wait_ge(out_done, 16 * (n - 2))
                            pool.tensor_tensor(y_out[:, hs], y[:, hs], x1b[par][:, hs], ALU.add).then_inc(S["yout_ready"], 1)
                    if on(s, 0):
                        pool.wait_ge(S["x1_ready"], 2 * n + 2)
                        if past(s, 0, 2):
                            pool.wait_ge(S["yout_ready"], 2 * (n - 1))
                        pool.tensor_tensor(x1b[par][:], x1[par][:], bias_b[:], ALU.add).then_inc(S["x1b_ready"], 1)

                schedule(pool, emit)

            @block.tensor
            def _(pe):
                def wo(s, n, par, h):
                    if h == 0:
                        pe.wait_ge(S["alo_ready"], n + 1)
                    if past(s, 0, 1):
                        pe.wait_ge(S["x1_ready"], 2 * n - 1 + h)
                    hs = slice(HALF * h, HALF * (h + 1))
                    for c in range(NC):
                        pe.matmul(w_ps[:, h, :], a_hi[:, c, :], wo_hi[:, c, hs], start=(c == 0), stop=False)
                        pe.matmul(w_ps[:, h, :], a_hi[:, c, :], wo_lo[:, c, hs], start=False, stop=False)
                        mm = pe.matmul(w_ps[:, h, :], a_lo[:, c, :], wo_hi[:, c, hs], start=False, stop=(c == NC - 1))
                    mm.then_inc(S["w_mm"], 1)

                def turn_routes(s, m):
                    pe.wait_ge(S["route_ready"], m + 1)
                    pe.transpose(s_ps[0:EROWS, 0:TT], route[:], ident[:]).then_inc(S["rt_mm"], 1)

                def scale_in(s, m):
                    pe.wait_ge(S["rt_ready"], m + 1)
                    pe.wait_ge(S["xt_ready"], m + 1)
                    for c in range(NC):
                        mm = pe.matmul(x_ps[:, c // 4, (c % 4) * TT:(c % 4 + 1) * TT], s_in[:, c * P:(c + 1) * P],
                                       route_t[:], start=True, stop=True)
                    mm.then_inc(S["is_mm"], 1)

                def scale_out(s, m, h):
                    if not (h == 0 and s is not None and s == 2):
                        pe.wait_ge(S["osc_ready"], 2 * m + h)
                    pe.matmul(o_ps[:], route_t[:], s_out[:, HALF * h:HALF * (h + 1)], start=True, stop=True).then_inc(S["os_mm"], 1)

                def turn_x(s, m):
                    pe.wait_ge(S["xn_ready"], m + 1)
                    if s is None or s >= 2:
                        pe.wait_ge(S["xs_ready"], m)
                    for c in range(NC):
                        mm = pe.transpose(x_ps[:, c // 4, (c % 4) * TT:(c % 4 + 1) * TT], x_n[:, c * P:(c + 1) * P], ident[:])
                    mm.then_inc(S["xt_mm"], 1)

                def logits(s, m, par):
                    pe.wait_ge(S["xt_ready"], m + 1)
                    if s is None or s >= 2:
                        pe.wait_ge(S["rt_ready"], m)
                    for c in range(NC):
                        mm = pe.matmul(s_ps[0:NE, 0:TT], gate[:, c, :], x_t[par][:, c, :], start=(c == 0), stop=(c == NC - 1))
                    mm.then_inc(S["lg_mm"], 1)

                def ffn(s, m, h):
                    if h == 0:
                        pe.wait_ge(S["xslo_ready"], m + 1)
                    if s is None or s > 2:
                        pe.wait_ge(S["y_ready"], 2 * m - 1 + h)
                    hs = slice(HALF * h, HALF * (h + 1))
                    for c in range(NC):
                        pe.matmul(f_ps[:, h, :], xs_hi[:, c, :], sign[:, c, hs], start=(c == 0), stop=False)
                        mm = pe.matmul(f_ps[:, h, :], xs_lo[:, c, :], sign[:, c, hs], start=False, stop=(c == NC - 1))
                    mm.then_inc(S["f_mm"], 1)

                def turn_logits(s, m):
                    pe.wait_ge(S["lg_ready"], m + 1)
                    pe.sem_inc(S["waited_pe"], 1)
                    pe.transpose(s_ps[0:TT, 0:NE], lg_t[:], ident[0:NE, 0:NE]).then_inc(S["lt_mm"], 1)

                def emit(s, n, par):
                    if on(s, -2):
                        turn_routes(s, n - 2)
                    if on(s, 0):
                        wo(s, n, par, 0)
                    if on(s, -2):
                        scale_in(s, n - 2)
                        scale_out(s, n - 2, 0)
                    if on(s, 0):
                        wo(s, n, par, 1)
                    if on(s, -1):
                        turn_x(s, n - 1)
                    if on(s, -2):
                        scale_out(s, n - 2, 1)
                        ffn(s, n - 2, 0)
                    if on(s, -1):
                        logits(s, n - 1, 1 - par)
                    if on(s, -2):
                        ffn(s, n - 2, 1)
                    if on(s, -1):
                        turn_logits(s, n - 1)

                pe.wait_ge(S["w_lo_ready"], NC)
                pe.wait_ge(S["sign_ready"], NC)
                pe.wait_ge(S["scale_ready"], 2)
                pe.wait_ge(S["small_in"], 2 * 16)
                schedule(pe, emit)

            @block.scalar
            def _(act):
                for c in range(NC):
                    act.wait_ge(w_in[c % 2], 16 * (c // 2 + 1))
                    act.copy(wo_hi[:, c, :], x1[c % 2][:]).then_inc(S["w_hi_ready"], 1)
                    if c == 1 or c == 5:
                        act.wait_ge(scales_in[c // 4], 3 * 16)
                        if c == 5:
                            act.wait_ge(S["scale_ready"], 1)
                        act.copy((s_in if c == 1 else s_out)[:], s_raw[:]).then_inc(S["scale_hi"], 1)

                def emit(s, n, par):
                    if on(s, 1):
                        act.wait_ge(S["at_ready"], n + 2)
                        if past(s, 0, 0):
                            act.wait_ge(S["w_mm"], 2 * n + 2)
                            act.wait_ge(S["alo_ready"], n + 1)
                        act.copy(a_hi[:], a_t[1 - par][:]).then_inc(S["ahi_ready"], 1)
                    if on(s, -2):
                        act.wait_ge(S["os_mm"], 2 * (n - 2) + 1)
                        if past(s, -2, 1):
                            act.wait_ge(S["y_ready"], 2 * (n - 2))
                        act.copy(osc[:, 0:HALF], o_ps[:]).then_inc(S["osc_ready"], 1)
                        act.wait_ge(S["xs_ready"], n - 1)
                        if past(s, -2, 1):
                            act.wait_ge(S["f_mm"], 2 * (n - 2))
                        act.copy(xs_hi[:], xs[:]).then_inc(S["xshi_ready"], 1)
                    if on(s, -1):
                        act.wait_ge(S["xt_mm"], n)
                        act.copy(x_t[1 - par][:], chunks(x_ps[:])).then_inc(S["xt_ready"], 1)
                    if on(s, -2):
                        act.wait_ge(S["os_mm"], 2 * (n - 2) + 2)
                        act.copy(osc[:, HALF:D], o_ps[:]).then_inc(S["osc_ready"], 1)
                    if on(s, -1):
                        act.wait_ge(S["lg_mm"], n)
                        act.copy(lg_t[:], s_ps[0:NE, 0:TT]).then_inc(S["lg_ready"], 1)
                        act.wait_ge(S["neg_ready"], n)
                        act.activation(ex[:], s_ps[0:TT, 0:NE], ACT.Exp, bias=neg[:], accum_out=den[:]).then_inc(S["ex_ready"], 1)

                schedule(act, emit)

            @block.vector
            def _(dve):
                dve.memset(half_pow[:], -0.5).then_inc(S["const_ready"], 1)
                dve.memset(route[:], 0.0).then_inc(S["const_ready"], 1)
                dve.memset(s_raw[:], 0.0).then_inc(S["zero_ready"], 1)

                def split_scales(i):
                    st = (s_in, s_out)[i]
                    dve.wait_ge(S["scale_hi"], i + 1)
                    dve.tensor_tensor(st[64:EROWS, :], s_raw[64:EROWS, :], f(st[64:EROWS, :]), ALU.subtract).then_inc(S["scale_ready"], 1)

                for c in range(NC):
                    dve.wait_ge(S["w_hi_ready"], c + 1)
                    dve.tensor_tensor(wo_lo[:, c, :], x1[c % 2][:], f(wo_hi[:, c, :]), ALU.subtract).then_inc(S["w_lo_ready"], 1)
                    if c == 1:
                        split_scales(0)
                    if c == 5:
                        split_scales(1)
                for c in range(NC):
                    dve.wait_ge(w_in[c % 2], 16 * ((NC + c) // 2 + 1))
                    if c >= 1:
                        dve.wait_ge(S["sign_ready"], c)
                    dve.tensor_scalar(y[:], x1[c % 2][:], 0.0, None, ALU.is_lt).then_inc(S["neg_w_ready"], 1)
                    dve.wait_ge(S["neg_w_ready"], c + 1)
                    dve.scalar_tensor_tensor(out=sign[:, c, :], in0=x1[c % 2][:], scalar=0.0, in1=y[:],
                                             op0=ALU.is_gt, op1=ALU.subtract).then_inc(S["sign_ready"], 1)

                def combine(s, m, par):
                    dve.wait_ge(at_in, 3 * REP * 16 * (m + 1))
                    dve.tensor_tensor(a_t[par][:], a_t[par][:], b_t[:], ALU.add).then_inc(S["sum_ready"], 1)
                    dve.reciprocal(d_t[:], d_t[:]).then_inc(S["rec_ready"], 1)

                def normalise_a(s, m, par):
                    dve.wait_ge(S["rec_ready"], m + 1)
                    dve.wait_ge(S["sum_ready"], m + 1)
                    dve.tensor_tensor(a_t[par][:], a_t[par][:], d_t[:], ALU.mult).then_inc(S["at_ready"], 1)

                def add_x(s, m, par, jj, h):
                    hs = slice(HALF * h, HALF * (h + 1))
                    dve.wait_ge(S["w_mm"], 2 * m + h + 1)
                    if h == 0:
                        if s is None:
                            dve.wait_ge(xin[par], jj)
                        else:
                            dve.wait_ge(xin[par], 16 * (s // 2 + 1))
                        if past(s, 0, 2):
                            dve.wait_ge(S["x1b_ready"], m - 1)
                    dve.tensor_tensor(x1[par][:, hs], w_ps[:, h, :], x_in[par][:, hs], ALU.add).then_inc(S["x1_ready"], 1)

                def normalise(s, m, par):
                    if past(s, 0, 1):
                        dve.wait_ge(S["xt_mm"], m)
                    for h in range(2):
                        dve.wait_ge(S["x1_ready"], 2 * m + h + 1)
                        dve.bn_stats(stats[:, 6 * h:6 * h + 6], x1[par][:, HALF * h:HALF * (h + 1)]).then_inc(S["stat_step"], 1)
                    dve.wait_ge(S["stat_step"], 3 * m + 2)
                    dve.sem_inc(S["waited_dve"], 1)
                    dve.bn_aggr(mv[:], stats[:]).then_inc(S["stat_step"], 1)
                    dve.wait_ge(S["stat_step"], 3 * m + 3)
                    dve.tensor_scalar(var[:], mv[:, 1:2], 1.0, EPS, ALU.mult, ALU.add).then_inc(S["var_ready"], 1)
                    dve.wait_ge(S["rstd_ready"], m + 1)
                    dve.tensor_scalar(x_n[:], x1[par][:], mv[:, 0:1], rstd[:], ALU.subtract, ALU.mult).then_inc(S["xn_ready"], 1)

                def scale_x(s, m, par):
                    dve.wait_ge(S["is_mm"], m + 1)
                    if past(s, -2, 1):
                        dve.wait_ge(S["xslo_ready"], m)
                    dve.tensor_tensor(xs[:], chunks(x_ps[:]), x_t[par][:], ALU.mult).then_inc(S["xs_ready"], 1)

                def scale_y(s, m, h):
                    hs = slice(HALF * h, HALF * (h + 1))
                    dve.wait_ge(S["f_mm"], 2 * m + h + 1)
                    dve.wait_ge(S["osc_ready"], 2 * m + h + 1)
                    if past(s, -2, 1):
                        dve.wait_ge(S["yout_ready"], 2 * m - 1 + h)
                    dve.tensor_tensor(y[:, hs], f_ps[:, h, :], osc[:, hs], ALU.mult).then_inc(S["y_ready"], 1)

                def routing(s, m):
                    dve.wait_ge(S["lt_mm"], m + 1)
                    dve.tensor_reduce(neg[:], s_ps[0:TT, 0:NE], AX, ALU.max, negate=True).then_inc(S["neg_ready"], 1)
                    dve.wait_ge(S["ex_ready"], m + 1)
                    dve.reciprocal(rden[:], den[:]).then_inc(S["rden_ready"], 1)
                    dve.wait_ge(S["rden_ready"], m + 1)
                    for k in (0, 64):
                        dve.tensor_scalar(route[:, k:k + NE].bitcast(F32R), ex[:], rden[:], None, ALU.mult).then_inc(S["route_hi"], 1)
                    dve.wait_ge(S["route_hi"], 2 * m + 2)
                    dve.scalar_tensor_tensor(out=route[:, 32:32 + NE], in0=ex[:], scalar=rden[:],
                                             in1=route[:, 0:NE], op0=ALU.mult, op1=ALU.subtract).then_inc(S["route_ready"], 1)

                def emit(s, n, par):
                    if on(s, 1):
                        combine(s, n + 1, 1 - par)
                    if on(s, -2):
                        dve.wait_ge(S["rt_mm"], n - 1)
                        dve.tensor_copy(route_t[:], s_ps[0:EROWS, 0:TT]).then_inc(S["rt_ready"], 1)
                    if on(s, 1):
                        normalise_a(s, n + 1, 1 - par)
                    if on(s, 0):
                        jj = None if s is not None else (8 * n + 16 if par == 0 else 8 * n + 8)
                        add_x(s, n, par, jj, 0)
                    if on(s, -2):
                        scale_x(s, n - 2, par)
                    if on(s, 0):
                        add_x(s, n, par, None if s is not None else jj, 1)
                        normalise(s, n, par)
                    if on(s, -2):
                        scale_y(s, n - 2, 0)
                        scale_y(s, n - 2, 1)
                    if on(s, -1):
                        routing(s, n - 1)

                schedule(dve, emit)


def build(nc, x, ctx_t, wq_t, wkv_t, wo_t, ln_w, wf_t, bias, gate_t, in_scale, out_scale, out):
    q_scr = nc.dram_tensor("q_scratch", (2, HD, B, NG, REP, Q), F32).ap()
    o_scr = nc.dram_tensor("o_scratch", (VW, NG, REP, B, Q), F32).ap()
    with ExitStack() as ctx:
        ident = ctx.enter_context(nc.sbuf_tensor("ident", [P, P], F32))
        zeroed = ctx.enter_context(nc.semaphore("ident_zeroed"))
        with nc.Block() as block:
            @block.gpsimd
            def _(pool):
                pool.memset(ident[:], 0.0).then_inc(zeroed, 1)
                pool.wait_ge(zeroed, 1)
                pool.affine_select(out=ident[:], in_=ident[:], compare_op=ALU.not_equal, fill=1.0, base=0,
                                   pattern=[[-1, P]], channel_multiplier=1).then_inc(zeroed, 1)
                pool.wait_ge(zeroed, 2)
        phase_queries(nc, x, wq_t, ln_w, q_scr, ident)
        phase_attention(nc, ctx_t, wkv_t, q_scr, o_scr, ident)
        phase_output(nc, x.rearrange("b q d -> (b q) d"), wo_t, wf_t, bias, gate_t, in_scale, out_scale,
                     o_scr.rearrange("v g r b q -> v g r (b q)"), out, ident)


def kernel(x, ctx_4096, L0_xattn_wq, L0_xattn_wk, L0_xattn_wv, L0_xattn_wo, L0_xattn_ln_w, L0_ffn_weight,
           L0_ffn_bias, L0_ffn_gate_w, L0_ffn_in_channel_scale, L0_ffn_out_channel_scale):
    import concourse.bacc as bacc
    from concourse.bass_utils import run_bass_kernel_spmd

    lay = lambda a: np.ascontiguousarray(a)
    ctx = np.zeros((B, NC, P, KP), np.float32)
    ctx[:, :, :, :K] = np.asarray(ctx_4096).transpose(0, 2, 1).reshape(B, NC, P, K)
    wkv = np.concatenate([np.asarray(L0_xattn_wk).T, np.asarray(L0_xattn_wv).T], axis=1)
    arrays = {
        "x": lay(x),
        "ctx_t": lay(ctx.transpose(0, 2, 1, 3)),
        "wq_t": lay(np.asarray(L0_xattn_wq).T),
        "wkv_t": lay(wkv.reshape(NC, P, 2 * NG * HD)),
        "wo_t": lay(np.asarray(L0_xattn_wo).T),
        "ln_w": lay(np.asarray(L0_xattn_ln_w).reshape(NC, P).T),
        "wf_t": lay(np.asarray(L0_ffn_weight).T),
        "bias": lay(L0_ffn_bias),
        "gate_t": lay(np.asarray(L0_ffn_gate_w).T.reshape(NC, P, NE).transpose(1, 0, 2)),
        "in_scale": lay(L0_ffn_in_channel_scale),
        "out_scale": lay(L0_ffn_out_channel_scale),
    }
    nc = bacc.Bacc("TRN2", target_bir_lowering=False, num_devices=1)
    args = [nc.dram_tensor(f"in_{n}", a.shape, mybir.dt.from_np(a.dtype), kind="ExternalInput").ap()
            for n, a in arrays.items()]
    out = nc.dram_tensor("out", (T, D), F32, kind="ExternalOutput").ap()
    build(nc, *args, out)
    got = run_bass_kernel_spmd(nc, [{f"in_{n}": a for n, a in arrays.items()}], core_ids=[0])
    return got.results[0]["out"].reshape(B, Q, D)
```

```python
from contextlib import ExitStack

import numpy as np

import concourse.bass as bass
from concourse import mybir

F32 = mybir.dt.float32
F32R = mybir.dt.float32r
ALU = mybir.AluOpType
ACT = mybir.ActivationFunctionType
AX = mybir.AxisListType.X

P = 128
B, Q, D = 16, 112, 1024
K, KP = 375, 376
NH, NG, HD = 32, 8, 32
REP = NH // NG
NC = D // P
KC = 3
KCS = K // KC
T = B * Q
GB = 4
QG = GB * Q
NQG = B // GB
NE = 8
EPS = 1e-5
SCALE = float(HD) ** -0.5
VW = 2 * HD + 2
TT = 128
NT = T // TT
HALF = D // 2
EROWS = 72


def f(ap):
    return ap.bitcast(F32)


def phase_queries(nc, x, wq_t, ln_w, wkv_t, ctx_t, q_scr, ident, kv_hi, kv_lo, c_raw, c_in):
    with ExitStack() as ctx:
        sb = lambda n, s, d=F32: ctx.enter_context(nc.sbuf_tensor(n, s, d))
        sem = lambda n: ctx.enter_context(nc.semaphore(n))
        w_raw = sb("q_w_raw", [P, 2, D])
        c_flat = c_raw[:].rearrange("p c k -> p (c k)")
        raw = [w_raw[:, 0, :], w_raw[:, 1, :], c_flat[:, 0:D], c_flat[:, D:2 * D]]
        w_hi = sb("q_w_hi", [P, NC, D], F32R)
        w_lo = sb("q_w_lo", [P, NC, D], F32R)
        lnw = sb("q_lnw", [P, NC])
        x_in = sb("q_x_in", [Q, 2, D])
        x_n = sb("q_x_n", [Q, 2, D])
        stats = sb("q_stats", [Q, 2, 12])
        mv = sb("q_mv", [Q, 2, 2])
        rstd = sb("q_rstd", [Q, 2, 1])
        var = sb("q_var", [Q, 2, 1])
        half_pow = sb("q_half_pow", [Q, 1])
        xt_hi = [sb(f"q_xt_hi{i}", [P, NC, QG], F32R) for i in range(2)]
        xt_lo = [sb(f"q_xt_lo{i}", [P, NC, QG], F32R) for i in range(2)]
        q_hi = [sb(f"q_hi{i}", [P, QG], F32R) for i in range(4)]
        q_lo = [sb(f"q_lo{i}", [P, QG], F32R) for i in range(4)]
        xp = ctx.enter_context(nc.psum_tensor("q_xp", [P, 2, 512], F32))
        qp = [ctx.enter_context(nc.psum_tensor(f"q_qp{i}", [P, 512], F32)) for i in range(4)]

        lnw_in = sem("q_lnw_in")
        w_in = [sem(f"q_w_in{i}") for i in range(4)]
        whi_ready = sem("q_whi_ready")
        wlo_ready = sem("q_wlo_ready")
        xin = [sem(f"q_xin{i}") for i in range(2)]
        stat_step = sem("q_stat_step")
        var_ready = sem("q_var_ready")
        rstd_ready = sem("q_rstd_ready")
        xn_ready = sem("q_xn_ready")
        xp_ready = sem("q_xp_ready")
        xhi_ready = sem("q_xhi_ready")
        xlo_ready = sem("q_xlo_ready")
        q_mm = sem("q_mm")
        qhi_ready = sem("q_qhi_ready")
        qlo_ready = sem("q_qlo_ready")
        q_out = [sem(f"q_out{i}") for i in range(4)]
        const_ready = sem("q_const_ready")

        wq_v = wq_t.rearrange("(c p) h -> c p h", p=P)
        NOUT = 2 * REP * 16

        NW = NC + NC // 2

        def kv_piece(i):
            return slice(2 * i, 2 * i + 2)

        with nc.Block() as block:
            @block.sync
            def _(sp):
                sp.dma_start(lnw[:], ln_w).then_inc(lnw_in, 16)

                def load_w(i):
                    if i >= 4:
                        sp.wait_ge(wlo_ready, i - 3)
                    if i < NC:
                        sp.dma_start(raw[i % 4], wq_v[i]).then_inc(w_in[i % 4], 16)
                    else:
                        sp.dma_start(raw[i % 4].rearrange("p (c h) -> p c h", c=2),
                                     wkv_t[kv_piece(i - NC)].rearrange("c p h -> p c h")).then_inc(w_in[i % 4], 16)

                for i in range(NW):
                    load_w(i)
                sp.wait_ge(wlo_ready, NW)
                sp.dma_start(c_raw[:], ctx_t[0]).then_inc(c_in, 16)

                def store_q(i):
                    g, grp = i % NG, i // NG
                    sp.wait_ge(qlo_ready, i + 1)
                    for hl, tile in ((0, q_hi), (1, q_lo)):
                        for r in range(REP):
                            src = f(tile[i % 4][HD * r:HD * r + HD, :]).rearrange("p (b t) -> p b t", b=GB)
                            dst = q_scr[hl, :, grp * GB:(grp + 1) * GB, g, r, :]
                            sp.dma_start(dst, src).then_inc(q_out[i % 4], 16)

                for i in range(NQG * NG):
                    store_q(i)
                for s in range(4):
                    sp.wait_ge(q_out[s], NOUT * (NQG * NG // 4))

            def steps():
                out = []
                for i in range(NQG * NG):
                    b = (i // NG + 1) * GB + i % NG // 2
                    out.append(("q", i))
                    if b < B:
                        out.append(("nx"[i % 2], b))
                return out

            @block.gpsimd
            def _(pool):
                def load_x(b):
                    pool.dma_start(x_in[:, b % 2, :], x[b]).then_inc(xin[b % 2], 16)

                load_x(0)
                load_x(1)
                pool.wait_ge(const_ready, 1)
                for b in range(B):
                    pool.wait_ge(var_ready, b + 1)
                    if b >= 2:
                        pool.wait_ge(xn_ready, b - 1)
                    pool.tensor_tensor(rstd[:, b % 2, :], var[:, b % 2, :], half_pow[:], ALU.pow).then_inc(rstd_ready, 1)
                    if b + 2 < B:
                        pool.wait_ge(xn_ready, b + 1)
                        load_x(b + 2)

            @block.vector
            def _(dve):
                dve.memset(half_pow[:], -0.5).then_inc(const_ready, 1)

                def normalise(b):
                    s = b % 2
                    dve.wait_ge(xin[s], 16 * (b // 2 + 1))
                    for h in range(2):
                        dve.bn_stats(stats[:, s, 6 * h:6 * h + 6], x_in[:, s, HALF * h:HALF * (h + 1)]).then_inc(stat_step, 1)
                    dve.wait_ge(stat_step, 3 * b + 2)
                    dve.bn_aggr(mv[:, s, :], stats[:, s, :]).then_inc(stat_step, 1)
                    dve.wait_ge(stat_step, 3 * b + 3)
                    dve.tensor_scalar(var[:, s, :], mv[:, s, 1:2], 1.0 + EPS, EPS * EPS, ALU.mult, ALU.add).then_inc(var_ready, 1)
                    dve.wait_ge(rstd_ready, b + 1)
                    if b >= 2:
                        dve.wait_ge(xp_ready, b - 1)
                    dve.tensor_scalar(x_n[:, s, :], x_in[:, s, :], mv[:, s, 0:1], rstd[:, s, :],
                                      ALU.subtract, ALU.mult).then_inc(xn_ready, 1)

                def split_w(i):
                    dve.wait_ge(whi_ready, i + 1)
                    if i < NC:
                        dve.scalar_tensor_tensor(out=w_lo[:, i, :], in0=raw[i % 4], scalar=lnw[:, i:i + 1],
                                                 in1=f(w_hi[:, i, :]), op0=ALU.mult, op1=ALU.subtract).then_inc(wlo_ready, 1)
                    else:
                        cs = kv_piece(i - NC)
                        dve.tensor_tensor(kv_lo[:, cs, :], raw[i % 4].rearrange("p (c h) -> p c h", c=2),
                                          f(kv_hi[:, cs, :]), ALU.subtract).then_inc(wlo_ready, 1)

                def split_x(b):
                    grp, t0 = b // GB, (b % GB) * Q
                    dve.wait_ge(xhi_ready, b + 1)
                    dst = xt_lo[grp % 2][:, :, t0:t0 + Q].rearrange("p (k c) t -> p k c t", k=2)
                    hi = f(xt_hi[grp % 2][:, :, t0:t0 + Q]).rearrange("p (k c) t -> p k c t", k=2)
                    src = xp[:, :, 0:4 * Q].rearrange("p k (c t) -> p k c t", c=4)
                    dve.tensor_tensor(dst, src, hi, ALU.subtract).then_inc(xlo_ready, 1)

                normalise(0)
                split_w(0)
                split_w(1)
                normalise(1)
                split_x(0)
                split_w(2)
                split_w(3)
                normalise(2)
                split_x(1)
                split_w(4)
                split_w(5)
                normalise(3)
                split_x(2)
                split_w(6)
                split_w(7)
                split_x(3)
                for kind, i in steps():
                    if kind == "n":
                        normalise(i)
                    elif kind == "x":
                        split_x(i)
                    else:
                        dve.wait_ge(qhi_ready, i + 1)
                        if i >= 4:
                            dve.wait_ge(q_out[i % 4], NOUT * (i // 4))
                        dve.tensor_tensor(q_lo[i % 4][:], qp[i % 4][:, 0:QG], f(q_hi[i % 4][:]), ALU.subtract).then_inc(qlo_ready, 1)
                        if i < NW - NC:
                            split_w(NC + i)

            @block.scalar
            def _(act):
                def split_w(i):
                    act.wait_ge(w_in[i % 4], 16 * (i // 4 + 1))
                    if i < NC:
                        act.activation(w_hi[:, i, :], raw[i % 4], ACT.Copy, scale=lnw[:, i:i + 1]).then_inc(whi_ready, 1)
                    else:
                        act.copy(kv_hi[:, kv_piece(i - NC), :],
                                 raw[i % 4].rearrange("p (c h) -> p c h", c=2)).then_inc(whi_ready, 1)

                def split_x(b):
                    grp, t0 = b // GB, (b % GB) * Q
                    act.wait_ge(xp_ready, b + 1)
                    if grp >= 2:
                        act.wait_ge(q_mm, NG * (grp - 1))
                    dst = xt_hi[grp % 2][:, :, t0:t0 + Q].rearrange("p (k c) t -> p k c t", k=2)
                    src = xp[:, :, 0:4 * Q].rearrange("p k (c t) -> p k c t", c=4)
                    act.copy(dst, src).then_inc(xhi_ready, 1)

                act.wait_ge(lnw_in, 16)
                for c in range(NC):
                    split_w(c)
                    if c % 2:
                        split_x(c // 2)
                for kind, i in steps():
                    if kind == "x":
                        split_x(i)
                    elif kind == "q":
                        act.wait_ge(q_mm, i + 1)
                        if i >= 4:
                            act.wait_ge(q_out[i % 4], NOUT * (i // 4))
                        act.copy(q_hi[i % 4][:], qp[i % 4][:, 0:QG]).then_inc(qhi_ready, 1)
                        if i < NW - NC:
                            split_w(NC + i)

            @block.tensor
            def _(pe):
                for kind, i in [("x", b) for b in range(GB)] + steps():
                    if kind == "x":
                        pe.wait_ge(xn_ready, i + 1)
                        if i >= 1:
                            pe.wait_ge(xlo_ready, i)
                        for c in range(NC):
                            mm = pe.transpose(xp[:, c // 4, (c % 4) * Q:(c % 4 + 1) * Q],
                                              x_n[:, i % 2, c * P:(c + 1) * P], ident[0:Q, 0:Q])
                        mm.then_inc(xp_ready, 1)
                    elif kind == "q":
                        grp, g = i // NG, i % NG
                        if g == 0:
                            pe.wait_ge(xlo_ready, GB * (grp + 1))
                        if i >= 4:
                            pe.wait_ge(qlo_ready, i - 3)
                        for c in range(NC):
                            if i == 0:
                                pe.wait_ge(wlo_ready, c + 1)
                            wh, wl = w_hi[:, c, g * P:(g + 1) * P], w_lo[:, c, g * P:(g + 1) * P]
                            xh, xl = xt_hi[grp % 2][:, c, :], xt_lo[grp % 2][:, c, :]
                            out = qp[i % 4][:, 0:QG]
                            pe.matmul(out, wh, xh, start=(c == 0), stop=False)
                            pe.matmul(out, wh, xl, start=False, stop=False)
                            mm = pe.matmul(out, wl, xh, start=False, stop=(c == NC - 1))
                        mm.then_inc(q_mm, 1)


def phase_attention(nc, ctx_t, q_scr, o_scr, ident, w_hi, w_lo, c_raw, c_in):
    with ExitStack() as ctx:
        sb = lambda n, s, d=F32: ctx.enter_context(nc.sbuf_tensor(n, s, d))
        ps = lambda n, s: ctx.enter_context(nc.psum_tensor(n, s, F32))
        sem = lambda n: ctx.enter_context(nc.semaphore(n))
        c_hi = [sb(f"a_c_hi{i}", [P, NC, KP], F32R) for i in range(2)]
        c_lo = [sb(f"a_c_lo{i}", [P, NC, KP], F32R) for i in range(2)]
        k_hi = sb("a_k_hi", [P, 2, KP], F32R)
        k_lo = sb("a_k_lo", [P, 2, KP], F32R)
        k_st = [sb(f"a_k_st{i}", [3 * HD + 2, NG, KP], F32R) for i in range(2)]
        q_st = [sb(f"a_q_st{i}", [3 * HD + 2, NG, REP * Q], F32R) for i in range(2)]
        v_st = [sb(f"a_v_st{i}", [KCS, KC, NG, VW], F32R) for i in range(2)]
        p_f = [sb(f"a_p_f{i}", [KCS, KC, REP * Q]) for i in range(2)]
        p_hi = [sb(f"a_p_hi{i}", [KCS, KC, REP * Q], F32R) for i in range(2)]
        p_lo = [sb(f"a_p_lo{i}", [KCS, KC, REP * Q], F32R) for i in range(2)]
        o_sb = [sb(f"a_o_sb{i}", [VW, REP * Q]) for i in range(2)]
        row_max = sb("a_row_max", [Q, 2, 16])
        neg_max = sb("a_neg_max", [Q, 2, 32])
        max_t = [sb(f"a_max_t{i}", [32, Q], F32R) for i in range(2)]
        a_ps = ps("a_ps", [P, 2, 512])
        b_ps = ps("b_ps", [P, 3, 512])
        o_ps = ps("o_ps", [P, 512])
        ring = [ps(f"a_ring{i}", [P, 512]) for i in range(2)]

        c_hi_ready = sem("a_c_hi_ready")
        c_lo_ready = sem("a_c_lo_ready")
        ones_ready = sem("a_ones_ready")
        v_mm = sem("a_v_mm")
        v_hi_ready = sem("a_v_hi_ready")
        v_lo_ready = sem("a_v_lo_ready")
        k_mm = sem("a_k_mm")
        k_hi_ready = sem("a_k_hi_ready")
        k_lo_ready = sem("a_k_lo_ready")
        k_in = [[sem(f"a_k_in{i}{c}") for c in range(2)] for i in range(2)]
        q_in = [[sem(f"a_q_in{i}{h}") for h in range(2)] for i in range(2)]
        a_mm = sem("a_a_mm")
        a_max = sem("a_a_max")
        neg_step = sem("a_neg_step")
        neg_ready = sem("a_neg_ready")
        t_mm = sem("a_t_mm")
        t_ready = sem("a_t_ready")
        shift_in = [sem(f"a_shift_in{h}") for h in range(2)]
        b_mm = sem("a_b_mm")
        exp_ready = sem("a_exp_ready")
        p_hi_ready = sem("a_p_hi_ready")
        p_lo_ready = sem("a_p_lo_ready")
        pv_mm = sem("a_pv_mm")
        o_ready = sem("a_o_ready")
        o_out = [sem(f"a_o_out{i}") for i in range(2)]
        waited = sem("a_waited")
        NKD = 12 * 16
        NQD = 3 * 16
        NSD = 2 * 16

        PEEL, LOOPS = 2, 5

        def schedule(eng, emit):
            for n in range(-3, PEEL):
                emit(n, n, n % 2, 0)
            with eng.Fori(PEEL // 2, PEEL // 2 + LOOPS) as j:
                emit(None, 2 * j, 0, j)
                emit(None, 2 * j + 1, 1, j)
            for n in range(PEEL + 2 * LOOPS, B):
                emit(n, n, n % 2, 0)

        def on(static, ahead):
            return static is None or 0 <= static + ahead < B

        def pair(static, par, j, ahead):
            return (static + ahead) // 2 if static is not None else j + (par + ahead) // 2

        def ctx_splits(s, g):
            if s == -3:
                return [(g, 3)] if g < 4 else []
            q, k = {6: (0, 3), 7: (1, 3), 0: (2, 2), 1: (3, 2)}.get(g, (0, None))
            return [(q, k)] if k is not None and on(s, k) and not (s == -2 and k == 2) else []

        def v_batch(s, n):
            if s == -2:
                return 0
            return n + 1 if on(s, 1) and s != -1 else None

        def v_bank(par, job):
            return ring[(par, par, 1 - par)[job]]

        def k_bank(par, job):
            return ring[(1 - par, par)[job]]

        with nc.Block() as block:
            @block.sync
            def _(sp):
                def load_q(b, par, h):
                    g0 = 4 * h
                    for rep, hl in enumerate((0, 1, 0)):
                        dst = f(q_st[par][HD * rep:HD * rep + HD, g0:g0 + 4, :])
                        src = q_scr[hl, :, b, g0:g0 + 4, :, :].rearrange("d g r t -> d g (r t)")
                        sp.dma_start(dst, src).then_inc(q_in[par][h], 16)

                def stack_k(par, c):
                    for rep, tile in enumerate((k_hi, k_hi, k_lo)):
                        for i in range(4):
                            sp.dma_start(f(k_st[par][HD * rep:HD * rep + HD, 4 * c + i, :]),
                                         f(tile[HD * i:HD * i + HD, c, :])).then_inc(k_in[par][c], 16)

                def shift(par, h):
                    for hl in range(2):
                        dst = f(q_st[par][96 + hl:97 + hl, 4 * h:4 * h + 4, :]).rearrange("p g (r t) -> p (g r) t", t=Q)
                        sp.dma_start(dst, f(max_t[h][16 * hl:16 * hl + 16, :])).then_inc(shift_in[h], 16)

                def store_o(b, g):
                    sp.dma_start(o_scr[:, g, :, b, :], o_sb[g % 2][:].rearrange("p (r t) -> p r t", r=REP)).then_inc(o_out[g % 2], 16)

                def emit(s, n, par, j):
                    for g in range(NG):
                        if g >= 2 and on(s, 0):
                            sp.wait_ge(o_ready, NG * n + g - 1)
                            store_o(n, g - 2)
                        if g < 2 and on(s, -1):
                            sp.wait_ge(o_ready, NG * n + g - 1)
                            store_o(n - 1, NG - 2 + g)
                        if g == 0 and on(s, 1):
                            if on(s, -1):
                                sp.wait_ge(b_mm, NG * n)
                            load_q(n + 1, 1 - par, 1)
                            sp.wait_ge(k_lo_ready, 2 * (n + 1) + 2)
                            stack_k(1 - par, 1)
                        if g == 2 and on(s, 3) and s != -3:
                            sp.wait_ge(c_hi_ready, 4 * (n + 3))
                            sp.wait_ge(c_lo_ready, 4 * (n + 3))
                            sp.dma_start(c_raw[:], ctx_t[n + 3]).then_inc(c_in, 16)
                        if g == 1 and on(s, 0):
                            sp.wait_ge(t_ready, 2 * (n + 1))
                            shift(par, 1)
                        if g == 4 and on(s, 2):
                            if on(s, 0):
                                sp.wait_ge(b_mm, NG * n + 4)
                            load_q(n + 2, par, 0)
                            sp.wait_ge(k_lo_ready, 2 * (n + 2) + 1)
                            stack_k(par, 0)
                        if g == 6 and on(s, 1):
                            sp.wait_ge(t_ready, 2 * (n + 1) + 1)
                            shift(1 - par, 0)

                schedule(sp, emit)
                for g in (NG - 2, NG - 1):
                    sp.wait_ge(o_ready, NG * (B - 1) + g + 1)
                    store_o(B - 1, g)
                for i in range(2):
                    sp.wait_ge(o_out[i], 16 * B * NG // 2)

            @block.tensor
            def _(pe):
                def scores_rows(s, b, par, jj, g, p):
                    if p == 0 and g % 4 == 0:
                        pe.wait_ge(k_in[par][g // 4], NKD * (jj + 1))
                        pe.wait_ge(q_in[par][g // 4], NQD * (jj + 1))
                    if s is None or s > 0 or g > 0 or p > 0:
                        pe.wait_ge(a_max, 16 * b + 2 * g + p)
                    for i in range(2):
                        r = 2 * p + i
                        mm = pe.matmul(a_ps[0:Q, i, 0:KP], q_st[par][0:96, g, r * Q:(r + 1) * Q],
                                       k_st[par][0:96, g, :], start=True, stop=True)
                    mm.then_inc(a_mm, 1)

                def scores_cols(s, b, par, g):
                    if g % 4 == 0:
                        pe.wait_ge(shift_in[g // 4], NSD * (b + 1))
                    if s is None or s > 0 or g > 0:
                        pe.wait_ge(exp_ready, NG * b + g)
                    for c in range(KC):
                        mm = pe.matmul(b_ps[0:KCS, c, 0:REP * Q], k_st[par][:, g, c * KCS:(c + 1) * KCS],
                                       q_st[par][:, g, :], start=True, stop=True)
                    mm.then_inc(b_mm, 1)

                def pv(s, b, par, g):
                    pe.wait_ge(p_lo_ready, NG * b + g + 1)
                    if g % NG == 0:
                        pe.wait_ge(v_lo_ready, KC * (b + 1))
                    if s is None or s > 0 or g > 0:
                        pe.wait_ge(o_ready, NG * b + g)
                    for c in range(KC):
                        w = v_st[par][:, c, g, :]
                        pe.matmul(o_ps[0:VW, 0:REP * Q], w, p_hi[g % 2][:, c, :], start=(c == 0), stop=False)
                        mm = pe.matmul(o_ps[0:VW, 0:REP * Q], w, p_lo[g % 2][:, c, :], start=False, stop=(c == KC - 1))
                    mm.then_inc(pv_mm, 1)

                def max_turn(s, b, h, bank):
                    pe.wait_ge(neg_ready, 2 * b + h + 1)
                    pe.transpose(bank[0:32, 0:Q], neg_max[:, h, :], ident[0:Q, 0:Q]).then_inc(t_mm, 1)

                def v_part(s, n, par, job, part):
                    b = v_batch(s, n)
                    if b is None:
                        return
                    if part == 0:
                        if job == 0 and s == 0:
                            pe.wait_ge(k_lo_ready, 2 * (n + 1) + 1)
                        elif job == 0 and s != -2:
                            pe.wait_ge(v_lo_ready, KC * b)
                        if job == 1:
                            pe.wait_ge(v_lo_ready, KC * b + 1)
                        if job == 2 and on(s, 2):
                            pe.wait_ge(k_lo_ready, 2 * (n + 2) + 1)
                        elif job == 2:
                            pe.wait_ge(t_ready, 2 * n + 2)
                    cpar = 0 if s == -2 else 1 - par
                    for st in range(8 * part, 8 * part + 8):
                        c, pas = divmod(st, 3)
                        if s == -2 and job == 0 and st % 6 == 0:
                            pe.wait_ge(c_lo_ready, c // 2 + 1)
                        a = (c_hi, c_lo, c_hi)[pas][cpar][:, c, job * KCS:(job + 1) * KCS]
                        w = (w_hi, w_hi, w_lo)[pas][:, c, NG * HD:]
                        mm = pe.matmul(v_bank(par, job)[0:KCS, 0:NG * HD], a, w, start=(st == 0), stop=(st == 23))
                    if part == 2:
                        mm.then_inc(v_mm, 1)

                def k_part(s, n, par, job, part):
                    if not on(s, 2):
                        return
                    if part == 0 and job == 0:
                        pe.wait_ge(c_lo_ready, 4 * (n + 3))
                        if on(s, 0):
                            pe.wait_ge(t_ready, 2 * n + 2)
                        elif s == -1:
                            pe.wait_ge(k_lo_ready, 2)
                    if part == 0 and job == 1:
                        if on(s, 1):
                            pe.wait_ge(t_ready, 2 * (n + 1) + 1)
                        else:
                            pe.wait_ge(v_lo_ready, 2)
                    for st in range(8 * part, 8 * part + 8):
                        c, pas = divmod(st, 3)
                        a = (c_hi, c_lo, c_hi)[pas][par][:, c, :]
                        w = (w_hi, w_hi, w_lo)[pas][:, c, job * P:(job + 1) * P]
                        mm = pe.matmul(k_bank(par, job)[:, 0:KP], w, a, start=(st == 0), stop=(st == 23))
                    if part == 2:
                        mm.then_inc(k_mm, 1)

                def kv_piece(s, n, par, i):
                    for first, part_of, job in ((0, v_part, 0), (4, k_part, 0), (7, v_part, 1),
                                                (10, v_part, 2), (13, k_part, 1)):
                        if first <= i < first + 3:
                            part_of(s, n, par, job, i - first)

                def emit(s, n, par, j):
                    if s == -1:
                        pe.wait_ge(ones_ready, 4)
                    for g in range(NG):
                        if on(s, 1):
                            scores_rows(None if s is None else s + 1, n + 1, 1 - par, pair(s, par, j, 1), g, 0)
                        if g == 1 and on(s, 0):
                            pe.wait_ge(k_lo_ready, 2 * (n + 2) if on(s, 1) else 2 * B)
                            pe.wait_ge(t_ready, 2 * n + 1)
                            max_turn(s, n, 1, ring[1 - par])
                        if g == 6 and on(s, 1):
                            pe.wait_ge(v_lo_ready, KC if s == -1 else KC * (n + 1) + 2)
                            max_turn(s, n + 1, 0, ring[par])
                        if on(s, 0):
                            scores_cols(s, n, par, g)
                        if g >= 2 and on(s, 0):
                            pv(s, n, par, g - 2)
                        if g < 2 and on(s, -1):
                            pv(None if s is None else s - 1, n - 1, 1 - par, NG - 2 + g)
                        kv_piece(s, n, par, 2 * g)
                        if on(s, 1):
                            scores_rows(None if s is None else s + 1, n + 1, 1 - par, pair(s, par, j, 1), g, 1)
                        kv_piece(s, n, par, 2 * g + 1)

                schedule(pe, emit)
                pv(B - 1, B - 1, (B - 1) % 2, NG - 2)
                pv(B - 1, B - 1, (B - 1) % 2, NG - 1)

            @block.vector
            def _(dve):
                for i in range(2):
                    dve.memset(f(v_st[i][:, :, :, 2 * HD:VW]), 1.0).then_inc(ones_ready, 1)

                def row_maxima(b, g, p):
                    dve.wait_ge(a_mm, 16 * b + 2 * g + p + 1)
                    dve.tensor_reduce(row_max[:, g // 4, (g % 4) * 4 + 2 * p:(g % 4) * 4 + 2 * p + 2],
                                      a_ps[0:Q, :, 0:K], AX, ALU.max).then_inc(a_max, 1)

                def negate(s, b, h):
                    dve.wait_ge(a_max, 16 * b + 8 * h + 8)
                    if s is None or s > 0:
                        dve.wait_ge(t_mm, 2 * b + h - 1)
                    dve.tensor_scalar(neg_max[:, h, 0:16].bitcast(F32R), row_max[:, h, :], -1.0, None, ALU.mult).then_inc(neg_step, 1)
                    dve.wait_ge(neg_step, 2 * b + h + 1)
                    dve.scalar_tensor_tensor(out=neg_max[:, h, 16:32], in0=row_max[:, h, :], scalar=-1.0,
                                             in1=neg_max[:, h, 0:16], op0=ALU.mult, op1=ALU.subtract).then_inc(neg_ready, 1)

                def take_turned(s, b, h, bank):
                    dve.wait_ge(t_mm, 2 * b + h + 1)
                    if s is None or s > 0:
                        dve.wait_ge(shift_in[h], NSD * b)
                    dve.tensor_copy(max_t[h][:], bank[0:32, 0:Q]).then_inc(t_ready, 1)

                def split_p(s, b, g):
                    dve.wait_ge(exp_ready, NG * b + g + 1)
                    if s is None or s > 0 or g >= 2:
                        dve.wait_ge(pv_mm, NG * b + g - 1)
                    dve.tensor_copy(p_hi[g % 2][:], p_f[g % 2][:]).then_inc(p_hi_ready, 1)

                def split_v(s, n, par, job):
                    b = v_batch(s, n)
                    if b is not None:
                        v = v_st[0 if s == -2 else 1 - par]
                        dve.wait_ge(v_hi_ready, KC * b + job + 1)
                        src = v_bank(par, job)[0:KCS, 0:NG * HD].rearrange("p (g d) -> p g d", g=NG)
                        dve.tensor_tensor(v[:, job, :, HD:2 * HD], src, f(v[:, job, :, 0:HD]),
                                          ALU.subtract).then_inc(v_lo_ready, 1)

                def split_k(b, bank, job):
                    dve.wait_ge(k_hi_ready, 2 * b + job + 1)
                    dve.tensor_tensor(k_lo[:, job, :], bank[:, 0:KP], f(k_hi[:, job, :]),
                                      ALU.subtract).then_inc(k_lo_ready, 1)

                def split_ctx(b, par, h):
                    dve.wait_ge(c_hi_ready, 4 * b + h + 1)
                    cs = slice(2 * h, 2 * h + 2)
                    dve.tensor_tensor(c_lo[par][:, cs, :], c_raw[:, cs, :], f(c_hi[par][:, cs, :]), ALU.subtract).then_inc(c_lo_ready, 1)

                def emit(s, n, par, j):
                    for g in range(NG):
                        if g == 0 and s == -1:
                            split_k(n + 1, k_bank(1 - par, 1), 1)
                        if on(s, 1):
                            row_maxima(n + 1, g, 0)
                        if g == 0 and on(s, 1) and s != -1:
                            split_k(n + 1, k_bank(1 - par, 1), 1)
                        if g == 1 and on(s, 0):
                            take_turned(s, n, 1, ring[1 - par])
                        if g == 6 and on(s, 1):
                            take_turned(None if s is None else s + 1, n + 1, 0, ring[par])
                        if g == 5:
                            split_v(s, n, par, 1)
                        if on(s, 0):
                            split_p(s, n, g)
                        if on(s, 1):
                            row_maxima(n + 1, g, 1)
                            if g == 3:
                                negate(None if s is None else s + 1, n + 1, 0)
                            if g == 7:
                                negate(None if s is None else s + 1, n + 1, 1)
                        if g == 1:
                            split_v(s, n, par, 0)
                        if g == 3 and on(s, 2):
                            split_k(n + 2, k_bank(par, 0), 0)
                        if g == 6:
                            split_v(s, n, par, 2)
                        for q, k in ctx_splits(s, g):
                            split_ctx(n + k, (par + k) % 2, q)

                schedule(dve, emit)

            @block.gpsimd
            def _(pool):
                for i in range(2):
                    pool.memset(f(k_st[i][96:98, :, :]), 1.0).then_inc(ones_ready, 1)

                def emit(s, n, par, j):
                    for g in range(NG):
                        if on(s, 0):
                            pool.wait_ge(p_hi_ready, NG * n + g + 1)
                            pool.tensor_tensor(p_lo[g % 2][:], p_f[g % 2][:], f(p_hi[g % 2][:]), ALU.subtract).then_inc(p_lo_ready, 1)

                schedule(pool, emit)

            @block.scalar
            def _(act):
                def exponentials(s, b, g):
                    act.wait_ge(b_mm, NG * b + g + 1)
                    if s is None or s > 0 or g >= 2:
                        act.wait_ge(p_lo_ready, NG * b + g - 1)
                    act.activation(p_f[g % 2][:], b_ps[0:KCS, :, 0:REP * Q], ACT.Exp, scale=SCALE).then_inc(exp_ready, 1)

                def take_o(s, b, g):
                    act.wait_ge(pv_mm, NG * b + g + 1)
                    if s is None or s > 0 or g >= 2:
                        act.wait_ge(o_out[g % 2], 16 * (NG // 2 * b + g // 2))
                    act.copy(o_sb[g % 2][:], o_ps[0:VW, 0:REP * Q]).then_inc(o_ready, 1)

                def take_v(s, n, par, job):
                    b = v_batch(s, n)
                    if b is not None:
                        act.wait_ge(v_mm, KC * b + job + 1)
                        if s is None or s >= 1:
                            act.wait_ge(pv_mm, NG * (b - 1))
                        src = v_bank(par, job)[0:KCS, 0:NG * HD].rearrange("p (g d) -> p g d", g=NG)
                        act.copy(v_st[0 if s == -2 else 1 - par][:, job, :, 0:HD], src).then_inc(v_hi_ready, 1)

                def take_k(s, b, par, jj, job):
                    act.wait_ge(k_mm, 2 * b + job + 1)
                    if s is None or s >= 1:
                        act.wait_ge(k_in[1 - par][job], NKD * jj)
                    act.copy(k_hi[:, job, :], k_bank(par, job)[:, 0:KP]).then_inc(k_hi_ready, 1)

                def split_ctx(s, b, par, h):
                    act.wait_ge(c_in, 16 * (b + 1))
                    if s is None or s >= 2:
                        act.wait_ge(v_mm, KC * (b - 1))
                    cs = slice(2 * h, 2 * h + 2)
                    act.copy(c_hi[par][:, cs, :], c_raw[:, cs, :]).then_inc(c_hi_ready, 1)

                def emit(s, n, par, j):
                    ahead = lambda k: None if s is None else s + k
                    for g in range(NG):
                        if on(s, 0):
                            exponentials(s, n, g)
                        if g >= 2 and on(s, 0):
                            take_o(s, n, g - 2)
                        if g < 2 and on(s, -1):
                            take_o(ahead(-1), n - 1, NG - 2 + g)
                        if g in (1, 4, 6):
                            take_v(s, n, par, (1, 4, 6).index(g))
                        if g in (3, 7) and on(s, 2):
                            take_k(ahead(2), n + 2, par, pair(s, par, j, 3), (3, 7).index(g))
                        for q, k in ctx_splits(s, g):
                            split_ctx(ahead(k), n + k, (par + k) % 2, q)

                schedule(act, emit)
                take_o(B - 1, B - 1, NG - 2)
                take_o(B - 1, B - 1, NG - 1)


def phase_output(nc, x, wo_t, wf_t, bias, gate_t, in_scale, out_scale, o_scr, r_scr, out, ident):
    with ExitStack() as ctx:
        sb = lambda n, s, d=F32: ctx.enter_context(nc.sbuf_tensor(n, s, d))
        ps = lambda n, s: ctx.enter_context(nc.psum_tensor(n, s, F32))
        sem = lambda n: ctx.enter_context(nc.semaphore(n))
        two = range(2)
        wo_hi = sb("o_wo_hi", [P, NC, D], F32R)
        wo_lo = sb("o_wo_lo", [P, NC, D], F32R)
        sign = sb("o_sign", [P, NC, D], F32R)
        gate = sb("o_gate", [P, NC, NE])
        s_in = sb("o_s_in", [EROWS, D], F32R)
        s_out = sb("o_s_out", [EROWS, D], F32R)
        bias_b = sb("o_bias", [P, D])
        a_t = [sb(f"o_a_t{i}", [P, NC, TT]) for i in two]
        b_t = sb("o_b_t", [P, NC, TT])
        r_t = sb("o_r_t", [P, NC, TT])
        den_all = sb("o_den_all", [P, NH * T // P])
        a_hi = [sb(f"o_a_hi{i}", [P, NC, TT], F32R) for i in two]
        a_lo = [sb(f"o_a_lo{i}", [P, NC, TT], F32R) for i in two]
        x_in = [sb(f"o_x_in{i}", [TT, D]) for i in two]
        x1 = [sb(f"o_x1{i}", [TT, D]) for i in two]
        s_raw = x1[1][0:EROWS, :]
        x1b = [sb(f"o_x1b{i}", [TT, D]) for i in two]
        x_n = sb("o_x_n", [TT, D])
        x_t = [sb(f"o_x_t{i}", [P, NC, TT]) for i in two]
        xs = sb("o_xs", [P, NC, TT])
        xs_hi = sb("o_xs_hi", [P, NC, TT], F32R)
        xs_lo = sb("o_xs_lo", [P, NC, TT], F32R)
        osc = sb("o_osc", [TT, D])
        y = sb("o_y", [TT, D])
        y_out = sb("o_y_out", [TT, D])
        stats = sb("o_stats", [TT, 12])
        mv = sb("o_mv", [TT, 2])
        var = sb("o_var", [TT, 1])
        rstd = sb("o_rstd", [TT, 1])
        half_pow = sb("o_half_pow", [TT, 1])
        lg_t = sb("o_lg_t", [NE, TT])
        neg = sb("o_neg", [TT, 1])
        ex = sb("o_ex", [TT, NE])
        den = sb("o_den", [TT, 1])
        rden = sb("o_rden", [TT, 1])
        route = sb("o_route", [TT, EROWS])
        route_t = sb("o_route_t", [EROWS, TT], F32R)
        w_ps = ps("o_w_ps", [P, 2, HALF])
        x_ps = ps("o_x_ps", [P, 2, HALF])
        f_ps = ps("o_f_ps", [P, 2, HALF])
        o_ps = ps("o_o_ps", [P, HALF])
        s_ps = ps("o_s_ps", [P, HALF])

        names = """w_hi_ready w_lo_ready neg_w_ready sign_ready small_in zero_ready scale_hi scale_ready
            sum_ready den_in den_rec r_out at_ready ahi_ready alo_ready w_mm x1_ready stat_step var_ready rstd_ready
            xn_ready x1b_ready xt_mm xt_ready lg_mm lg_ready lt_mm neg_ready ex_ready rden_ready route_hi
            route_ready rt_mm rt_ready is_mm xs_ready xshi_ready xslo_ready os_mm osc_ready f_mm y_ready
            yout_ready const_ready waited_sp waited_pe waited_dve""".split()
        S = {k: sem("o_" + k) for k in names}
        w_in = [sem(f"o_w_in{i}") for i in range(NC)]
        scales_in = [sem(f"o_scales_in{i}") for i in two]
        at_in = sem("o_at_in")
        xin = [sem(f"o_xin{i}") for i in two]
        out_done = sem("o_out_done")
        wo_v, wf_v = (w.rearrange("(c p) h -> c p h", p=P) for w in (wo_t, wf_t))
        flat3 = lambda t: t[:].rearrange("p c t -> p (c t)")
        raw = [x1b[0][:], x1b[1][:], y[:], y_out[:], flat3(xs), flat3(x_t[0]), flat3(x_t[1]), osc[:]]

        PEEL, LOOPS = 3, 5

        def schedule(eng, emit, first=-1):
            for n in range(first, PEEL):
                emit(n, n, n % 2)
            with eng.Fori(PEEL // 2, PEEL // 2 + LOOPS) as j:
                emit(None, 2 * j + 1, 1)
                emit(None, 2 * j + 2, 0)
            for n in range(PEEL + 2 * LOOPS, NT + 2):
                emit(n, n, n % 2)

        def on(static, ahead):
            return static is None or 0 <= static + ahead < NT

        def past(static, ahead, least):
            return static is None or static + ahead >= least

        def slot(static, n, par, ahead):
            return (static + ahead) // 2 if static is not None else None

        r_den = o_scr[2 * HD:2 * HD + 1].rearrange("a g r t -> (a g r t)").rearrange("(p n) -> p n", p=P)
        r_flat = r_scr.rearrange("a g r t -> (a g r t)").rearrange("(p n) -> p n", p=P)
        chunks = lambda ap: ap.rearrange("p k (c t) -> p (k c) t", c=NC // 2)

        with nc.Block() as block:
            @block.sync
            def _(sp):
                sp.dma_start(gate[:], gate_t).then_inc(S["small_in"], 16)
                sp.dma_start(bias_b[:], bias.rearrange("(a d) -> a d", a=1).broadcast_to([P, D])).then_inc(S["small_in"], 16)

                def load_w(c):
                    if c >= NC:
                        sp.wait_ge(S["w_lo_ready"], c - NC + 1)
                    sp.dma_start(raw[c % NC], (wo_v if c < NC else wf_v)[c % NC]).then_inc(w_in[c % NC], 16)

                def load_scales(i, src):
                    if i == 0:
                        sp.wait_ge(S["zero_ready"], 1)
                    else:
                        sp.wait_ge(S["scale_ready"], 1)
                    for r in range(3):
                        sp.dma_start(s_raw[32 * r:32 * r + NE, :], src).then_inc(scales_in[i], 16)

                def emit(s, n, par):
                    if on(s, 1):
                        if past(s, 0, 0):
                            sp.wait_ge(S["at_ready"], n + 1)
                            sp.sem_inc(S["waited_sp"], 1)
                        if past(s, -1, 0):
                            sp.wait_ge(S["alo_ready"], n)
                        t0 = (n + 1) * TT
                        for r in range(REP):
                            rows = slice(HD * r, HD * r + HD)
                            sp.dma_start(a_t[1 - par][rows, :, :], o_scr[0:HD, :, r, bass.ds(t0, TT)]).then_inc(at_in, 16)
                            sp.dma_start(b_t[rows, :, :], o_scr[HD:2 * HD, :, r, bass.ds(t0, TT)]).then_inc(at_in, 16)
                            sp.dma_start(r_t[rows, :, :], r_scr[:, :, r, bass.ds(t0, TT)]
                                         .broadcast_to([HD, NC, TT])).then_inc(at_in, 16)
                        if past(s, -1, 0):
                            sp.wait_ge(S["x1_ready"], 2 * n)
                        sp.dma_start(x_in[1 - par][:], x[bass.ds(t0, TT), :]).then_inc(xin[1 - par], 16)

                sp.dma_start(den_all[:], r_den).then_inc(S["den_in"], 16)
                for c in range(NC):
                    load_w(c)
                    if c == 1:
                        load_scales(0, in_scale)
                        sp.wait_ge(S["den_rec"], 1)
                        sp.dma_start(r_flat, den_all[:]).then_inc(S["r_out"], 16)
                    if c == 5:
                        sp.wait_ge(S["r_out"], 16)
                        emit(-1, -1, 1)
                load_scales(1, out_scale)
                for c in range(NC, 2 * NC):
                    load_w(c)
                schedule(sp, emit, 0)

            @block.gpsimd
            def _(pool):
                pool.wait_ge(S["const_ready"], 1)
                pool.wait_ge(S["small_in"], 2 * 16)

                def emit(s, n, par):
                    if on(s, 1):
                        pool.wait_ge(S["ahi_ready"], n + 2)
                        if past(s, 0, 1):
                            pool.wait_ge(S["w_mm"], 2 * n)
                        pool.tensor_tensor(a_lo[1 - par][:], a_t[1 - par][:], f(a_hi[1 - par][:]),
                                           ALU.subtract).then_inc(S["alo_ready"], 1)
                    if on(s, 0):
                        pool.wait_ge(S["var_ready"], n + 1)
                        pool.tensor_tensor(rstd[:], var[:], half_pow[:], ALU.pow).then_inc(S["rstd_ready"], 1)
                    if on(s, -2):
                        for h in range(2):
                            hs = slice(HALF * h, HALF * (h + 1))
                            pool.wait_ge(S["y_ready"], 2 * (n - 2) + h + 1)
                            if h == 0 and past(s, -2, 1):
                                pool.wait_ge(out_done, 16 * (n - 2))
                            pool.tensor_tensor(y_out[:, hs], y[:, hs], x1b[par][:, hs], ALU.add).then_inc(S["yout_ready"], 1)
                        pool.wait_ge(S["yout_ready"], 2 * (n - 1))
                        pool.dma_start(out[bass.ds((n - 2) * TT, TT), :], y_out[:]).then_inc(out_done, 16)
                    if on(s, 0):
                        pool.wait_ge(S["x1_ready"], 2 * n + 2)
                        if past(s, 0, 2):
                            pool.wait_ge(S["yout_ready"], 2 * (n - 1))
                        pool.tensor_tensor(x1b[par][:], x1[par][:], bias_b[:], ALU.add).then_inc(S["x1b_ready"], 1)

                schedule(pool, emit)
                pool.wait_ge(out_done, 16 * NT)

            @block.tensor
            def _(pe):
                def wo(s, n, par, h, between=None):
                    if h == 0:
                        pe.wait_ge(S["alo_ready"], n + 1)
                    if past(s, 0, 1):
                        pe.wait_ge(S["x1_ready"], 2 * n - 1 + h)
                    hs = slice(HALF * h, HALF * (h + 1))
                    for c in range(NC):
                        if c == NC // 2 and between:
                            between()
                        if s == 0 and h == 0:
                            pe.wait_ge(S["w_lo_ready"], c + 1)
                        pe.matmul(w_ps[:, h, :], a_hi[par][:, c, :], wo_hi[:, c, hs], start=(c == 0), stop=False)
                        pe.matmul(w_ps[:, h, :], a_hi[par][:, c, :], wo_lo[:, c, hs], start=False, stop=False)
                        mm = pe.matmul(w_ps[:, h, :], a_lo[par][:, c, :], wo_hi[:, c, hs], start=False, stop=(c == NC - 1))
                    mm.then_inc(S["w_mm"], 1)

                def turn_routes(s, m):
                    pe.wait_ge(S["route_ready"], m + 1)
                    pe.transpose(s_ps[0:EROWS, 0:TT], route[:], ident[:]).then_inc(S["rt_mm"], 1)

                def scale_in(s, m):
                    pe.wait_ge(S["rt_ready"], m + 1)
                    pe.wait_ge(S["xt_ready"], m + 1)
                    for c in range(NC):
                        mm = pe.matmul(x_ps[:, c // 4, (c % 4) * TT:(c % 4 + 1) * TT], s_in[:, c * P:(c + 1) * P],
                                       route_t[:], start=True, stop=True)
                    mm.then_inc(S["is_mm"], 1)

                def scale_out(s, m, h):
                    if not (h == 0 and s is not None and s == 2):
                        pe.wait_ge(S["osc_ready"], 2 * m + h)
                    pe.matmul(o_ps[:], route_t[:], s_out[:, HALF * h:HALF * (h + 1)], start=True, stop=True).then_inc(S["os_mm"], 1)

                def turn_x(s, m):
                    pe.wait_ge(S["xn_ready"], m + 1)
                    if s is None or s >= 2:
                        pe.wait_ge(S["xs_ready"], m)
                    for c in range(NC):
                        mm = pe.transpose(x_ps[:, c // 4, (c % 4) * TT:(c % 4 + 1) * TT], x_n[:, c * P:(c + 1) * P], ident[:])
                    mm.then_inc(S["xt_mm"], 1)

                def logits(s, m, par):
                    pe.wait_ge(S["xt_ready"], m + 1)
                    if s is None or s >= 2:
                        pe.wait_ge(S["rt_ready"], m)
                    for c in range(NC):
                        mm = pe.matmul(s_ps[0:NE, 0:TT], gate[:, c, :], x_t[par][:, c, :], start=(c == 0), stop=(c == NC - 1))
                    mm.then_inc(S["lg_mm"], 1)

                def ffn(s, m, h, between=None):
                    if h == 0:
                        pe.wait_ge(S["xslo_ready"], m + 1)
                    if s is None or s > 2:
                        pe.wait_ge(S["y_ready"], 2 * m - 1 + h)
                    hs = slice(HALF * h, HALF * (h + 1))
                    for c in range(NC):
                        if c == NC // 2 and between:
                            between()
                        if s == 2 and h == 0:
                            pe.wait_ge(S["sign_ready"], c + 1)
                        pe.matmul(f_ps[:, h, :], xs_hi[:, c, :], sign[:, c, hs], start=(c == 0), stop=False)
                        mm = pe.matmul(f_ps[:, h, :], xs_lo[:, c, :], sign[:, c, hs], start=False, stop=(c == NC - 1))
                    mm.then_inc(S["f_mm"], 1)

                def turn_logits(s, m):
                    pe.wait_ge(S["lg_ready"], m + 1)
                    pe.sem_inc(S["waited_pe"], 1)
                    pe.transpose(s_ps[0:TT, 0:NE], lg_t[:], ident[0:NE, 0:NE]).then_inc(S["lt_mm"], 1)

                def emit(s, n, par):
                    routes = (lambda: turn_routes(s, n - 2)) if on(s, -2) else None
                    turned = (lambda: turn_logits(s, n - 1)) if on(s, -1) else None
                    if on(s, 0):
                        wo(s, n, par, 0, routes)
                    elif routes:
                        routes()
                    if on(s, -2):
                        if s == 2:
                            pe.wait_ge(S["scale_ready"], 2)
                        scale_in(s, n - 2)
                        scale_out(s, n - 2, 0)
                    if on(s, 0):
                        wo(s, n, par, 1)
                    if on(s, -1):
                        turn_x(s, n - 1)
                    if on(s, -2):
                        scale_out(s, n - 2, 1)
                        ffn(s, n - 2, 0)
                    if on(s, -1):
                        logits(s, n - 1, 1 - par)
                    if on(s, -2):
                        ffn(s, n - 2, 1, turned)
                    elif turned:
                        turned()

                pe.wait_ge(S["small_in"], 2 * 16)
                schedule(pe, emit)

            @block.scalar
            def _(act):
                for c in range(NC):
                    act.wait_ge(w_in[c], 16)
                    act.copy(wo_hi[:, c, :], raw[c]).then_inc(S["w_hi_ready"], 1)
                    if c == 1:
                        act.wait_ge(scales_in[0], 3 * 16)
                        act.copy(s_in[:], s_raw).then_inc(S["scale_hi"], 1)

                def emit(s, n, par):
                    if on(s, 1):
                        act.wait_ge(S["at_ready"], n + 2)
                        if past(s, 0, 1):
                            act.wait_ge(S["w_mm"], 2 * n)
                            act.wait_ge(S["alo_ready"], n)
                        act.copy(a_hi[1 - par][:], a_t[1 - par][:]).then_inc(S["ahi_ready"], 1)
                    if on(s, -2):
                        act.wait_ge(S["os_mm"], 2 * (n - 2) + 1)
                        if past(s, -2, 1):
                            act.wait_ge(S["y_ready"], 2 * (n - 2))
                        act.copy(osc[:, 0:HALF], o_ps[:]).then_inc(S["osc_ready"], 1)
                        act.wait_ge(S["xs_ready"], n - 1)
                        if past(s, -2, 1):
                            act.wait_ge(S["f_mm"], 2 * (n - 2))
                        act.copy(xs_hi[:], xs[:]).then_inc(S["xshi_ready"], 1)
                    if on(s, -1):
                        act.wait_ge(S["xt_mm"], n)
                        act.copy(x_t[1 - par][:], chunks(x_ps[:])).then_inc(S["xt_ready"], 1)
                    if on(s, -2):
                        act.wait_ge(S["os_mm"], 2 * (n - 2) + 2)
                        act.copy(osc[:, HALF:D], o_ps[:]).then_inc(S["osc_ready"], 1)
                    if on(s, -1):
                        act.wait_ge(S["lg_mm"], n)
                        act.copy(lg_t[:], s_ps[0:NE, 0:TT]).then_inc(S["lg_ready"], 1)
                        act.wait_ge(S["neg_ready"], n)
                        act.activation(ex[:], s_ps[0:TT, 0:NE], ACT.Exp, bias=neg[:], accum_out=den[:]).then_inc(S["ex_ready"], 1)

                act.wait_ge(scales_in[1], 3 * 16)
                act.copy(s_out[:], s_raw).then_inc(S["scale_hi"], 1)
                emit(-1, -1, 1)
                for c in range(NC):
                    act.wait_ge(w_in[c], 32)
                    act.activation(sign[:, c, :], raw[c], ACT.Sign).then_inc(S["sign_ready"], 1)
                schedule(act, emit, 0)

            @block.vector
            def _(dve):
                dve.memset(half_pow[:], -0.5).then_inc(S["const_ready"], 1)
                dve.memset(route[:], 0.0).then_inc(S["const_ready"], 1)
                dve.memset(s_raw, 0.0).then_inc(S["zero_ready"], 1)

                def split_scales(i):
                    st = (s_in, s_out)[i]
                    dve.wait_ge(S["scale_hi"], i + 1)
                    dve.tensor_tensor(st[64:EROWS, :], s_raw[64:EROWS, :], f(st[64:EROWS, :]), ALU.subtract).then_inc(S["scale_ready"], 1)

                def combine(s, m, par):
                    dve.wait_ge(at_in, 3 * REP * 16 * (m + 1))
                    dve.tensor_tensor(a_t[par][:], a_t[par][:], b_t[:], ALU.add).then_inc(S["sum_ready"], 1)

                def normalise_a(s, m, par):
                    dve.wait_ge(S["sum_ready"], m + 1)
                    dve.tensor_tensor(a_t[par][:], a_t[par][:], r_t[:], ALU.mult).then_inc(S["at_ready"], 1)

                def add_x(s, m, par, jj, h):
                    hs = slice(HALF * h, HALF * (h + 1))
                    dve.wait_ge(S["w_mm"], 2 * m + h + 1)
                    if h == 0:
                        if s is None:
                            dve.wait_ge(xin[par], jj)
                        else:
                            dve.wait_ge(xin[par], 16 * (s // 2 + 1))
                        if past(s, 0, 2):
                            dve.wait_ge(S["x1b_ready"], m - 1)
                    dve.tensor_tensor(x1[par][:, hs], w_ps[:, h, :], x_in[par][:, hs], ALU.add).then_inc(S["x1_ready"], 1)

                def normalise(s, m, par):
                    if past(s, 0, 1):
                        dve.wait_ge(S["xt_mm"], m)
                    for h in range(2):
                        dve.wait_ge(S["x1_ready"], 2 * m + h + 1)
                        dve.bn_stats(stats[:, 6 * h:6 * h + 6], x1[par][:, HALF * h:HALF * (h + 1)]).then_inc(S["stat_step"], 1)
                    dve.wait_ge(S["stat_step"], 3 * m + 2)
                    dve.sem_inc(S["waited_dve"], 1)
                    dve.bn_aggr(mv[:], stats[:]).then_inc(S["stat_step"], 1)
                    dve.wait_ge(S["stat_step"], 3 * m + 3)
                    dve.tensor_scalar(var[:], mv[:, 1:2], 1.0, EPS, ALU.mult, ALU.add).then_inc(S["var_ready"], 1)
                    dve.wait_ge(S["rstd_ready"], m + 1)
                    dve.tensor_scalar(x_n[:], x1[par][:], mv[:, 0:1], rstd[:], ALU.subtract, ALU.mult).then_inc(S["xn_ready"], 1)

                def scale_x(s, m, par):
                    dve.wait_ge(S["is_mm"], m + 1)
                    if past(s, -2, 1):
                        dve.wait_ge(S["xslo_ready"], m)
                    dve.tensor_tensor(xs[:], chunks(x_ps[:]), x_t[par][:], ALU.mult).then_inc(S["xs_ready"], 1)
                    dve.wait_ge(S["xshi_ready"], m + 1)
                    dve.tensor_tensor(xs_lo[:], xs[:], f(xs_hi[:]), ALU.subtract).then_inc(S["xslo_ready"], 1)

                def scale_y(s, m, h):
                    hs = slice(HALF * h, HALF * (h + 1))
                    dve.wait_ge(S["f_mm"], 2 * m + h + 1)
                    dve.wait_ge(S["osc_ready"], 2 * m + h + 1)
                    if past(s, -2, 1):
                        dve.wait_ge(S["yout_ready"], 2 * m - 1 + h)
                    dve.tensor_tensor(y[:, hs], f_ps[:, h, :], osc[:, hs], ALU.mult).then_inc(S["y_ready"], 1)

                def routing(s, m):
                    dve.wait_ge(S["lt_mm"], m + 1)
                    dve.tensor_reduce(neg[:], s_ps[0:TT, 0:NE], AX, ALU.max, negate=True).then_inc(S["neg_ready"], 1)
                    dve.wait_ge(S["ex_ready"], m + 1)
                    dve.reciprocal(rden[:], den[:]).then_inc(S["rden_ready"], 1)
                    dve.wait_ge(S["rden_ready"], m + 1)
                    for k in (0, 64):
                        dve.tensor_scalar(route[:, k:k + NE].bitcast(F32R), ex[:], rden[:], None, ALU.mult).then_inc(S["route_hi"], 1)
                    dve.wait_ge(S["route_hi"], 2 * m + 2)
                    dve.scalar_tensor_tensor(out=route[:, 32:32 + NE], in0=ex[:], scalar=rden[:],
                                             in1=route[:, 0:NE], op0=ALU.mult, op1=ALU.subtract).then_inc(S["route_ready"], 1)

                def emit(s, n, par):
                    if on(s, 1):
                        combine(s, n + 1, 1 - par)
                    if on(s, -2):
                        dve.wait_ge(S["rt_mm"], n - 1)
                        dve.tensor_copy(route_t[:], s_ps[0:EROWS, 0:TT]).then_inc(S["rt_ready"], 1)
                    if on(s, 1):
                        normalise_a(s, n + 1, 1 - par)
                    if on(s, 0):
                        jj = None if s is not None else (8 * n + 16 if par == 0 else 8 * n + 8)
                        add_x(s, n, par, jj, 0)
                    if on(s, -2):
                        scale_x(s, n - 2, par)
                    if on(s, 0):
                        add_x(s, n, par, jj, 1)
                        normalise(s, n, par)
                    if on(s, -2):
                        scale_y(s, n - 2, 0)
                    if on(s, -1):
                        routing(s, n - 1)
                    if on(s, -2):
                        scale_y(s, n - 2, 1)

                dve.wait_ge(S["den_in"], 16)
                dve.reciprocal(den_all[:], den_all[:]).then_inc(S["den_rec"], 1)
                for c in range(NC):
                    if c == 6:
                        emit(-1, -1, 1)
                    dve.wait_ge(S["w_hi_ready"], c + 1)
                    dve.tensor_tensor(wo_lo[:, c, :], raw[c], f(wo_hi[:, c, :]), ALU.subtract).then_inc(S["w_lo_ready"], 1)
                    if c == 1:
                        split_scales(0)
                split_scales(1)
                schedule(dve, emit, 0)


def build(nc, x, ctx_t, wq_t, wkv_t, wo_t, ln_w, wf_t, bias, gate_t, in_scale, out_scale, out):
    q_scr = nc.dram_tensor("q_scratch", (2, HD, B, NG, REP, Q), F32).ap()
    o_scr = nc.dram_tensor("o_scratch", (VW, NG, REP, B, Q), F32).ap()
    r_scr = nc.dram_tensor("r_scratch", (1, NG, REP, T), F32).ap()
    with ExitStack() as ctx:
        ident = ctx.enter_context(nc.sbuf_tensor("ident", [P, P], F32))
        zeroed = ctx.enter_context(nc.semaphore("ident_zeroed"))
        with nc.Block() as block:
            @block.gpsimd
            def _(pool):
                pool.memset(ident[:], 0.0).then_inc(zeroed, 1)
                pool.wait_ge(zeroed, 1)
                pool.affine_select(out=ident[:], in_=ident[:], compare_op=ALU.not_equal, fill=1.0, base=0,
                                   pattern=[[-1, P]], channel_multiplier=1).then_inc(zeroed, 1)
                pool.wait_ge(zeroed, 2)
        with (nc.sbuf_tensor("kv_hi", [P, NC, 2 * NG * HD], F32R) as kv_hi,
              nc.sbuf_tensor("kv_lo", [P, NC, 2 * NG * HD], F32R) as kv_lo,
              nc.sbuf_tensor("c_raw", [P, NC, KP], F32) as c_raw):
            c_in = ctx.enter_context(nc.semaphore("c_in"))
            phase_queries(nc, x, wq_t, ln_w, wkv_t, ctx_t, q_scr, ident, kv_hi, kv_lo, c_raw, c_in)
            phase_attention(nc, ctx_t, q_scr, o_scr, ident, kv_hi, kv_lo, c_raw, c_in)
        phase_output(nc, x.rearrange("b q d -> (b q) d"), wo_t, wf_t, bias, gate_t, in_scale, out_scale,
                     o_scr.rearrange("v g r b q -> v g r (b q)"), r_scr, out, ident)


def kernel(x, ctx_4096, L0_xattn_wq, L0_xattn_wk, L0_xattn_wv, L0_xattn_wo, L0_xattn_ln_w, L0_ffn_weight,
           L0_ffn_bias, L0_ffn_gate_w, L0_ffn_in_channel_scale, L0_ffn_out_channel_scale):
    import concourse.bacc as bacc
    from concourse.bass_utils import run_bass_kernel_spmd

    lay = lambda a: np.ascontiguousarray(a)
    ctx = np.zeros((B, NC, P, KP), np.float32)
    ctx[:, :, :, :K] = np.asarray(ctx_4096).transpose(0, 2, 1).reshape(B, NC, P, K)
    wkv = np.concatenate([np.asarray(L0_xattn_wk).T, np.asarray(L0_xattn_wv).T], axis=1)
    arrays = {
        "x": lay(x),
        "ctx_t": lay(ctx.transpose(0, 2, 1, 3)),
        "wq_t": lay(np.asarray(L0_xattn_wq).T),
        "wkv_t": lay(wkv.reshape(NC, P, 2 * NG * HD)),
        "wo_t": lay(np.asarray(L0_xattn_wo).T),
        "ln_w": lay(np.asarray(L0_xattn_ln_w).reshape(NC, P).T),
        "wf_t": lay(np.asarray(L0_ffn_weight).T),
        "bias": lay(L0_ffn_bias),
        "gate_t": lay(np.asarray(L0_ffn_gate_w).T.reshape(NC, P, NE).transpose(1, 0, 2)),
        "in_scale": lay(L0_ffn_in_channel_scale),
        "out_scale": lay(L0_ffn_out_channel_scale),
    }
    nc = bacc.Bacc("TRN2", target_bir_lowering=False, num_devices=1)
    args = [nc.dram_tensor(f"in_{n}", a.shape, mybir.dt.from_np(a.dtype), kind="ExternalInput").ap()
            for n, a in arrays.items()]
    out = nc.dram_tensor("out", (T, D), F32, kind="ExternalOutput").ap()
    build(nc, *args, out)
    got = run_bass_kernel_spmd(nc, [{f"in_{n}": a for n, a in arrays.items()}], core_ids=[0])
    return got.results[0]["out"].reshape(B, Q, D)
```

```python
from contextlib import ExitStack

import numpy as np

import concourse.bass as bass
from concourse import mybir

F32 = mybir.dt.float32
F32R = mybir.dt.float32r
ALU = mybir.AluOpType
ACT = mybir.ActivationFunctionType
AX = mybir.AxisListType.X

P = 128
B, Q, D = 16, 112, 1024
K, KP = 375, 376
NH, NG, HD = 32, 8, 32
REP = NH // NG
NC = D // P
KC = 3
KCS = K // KC
T = B * Q
GB = 4
NOUT = 2 * REP * 16
QG = GB * Q
NQG = B // GB
NE = 8
EPS = 1e-5
SCALE = float(HD) ** -0.5
VW = 2 * HD + 2
TT = 128
NT = T // TT
HALF = D // 2
OB = 4
NDB = B - 2
EROWS = 72


def f(ap):
    return ap.bitcast(F32)


def ctx_view(spare):
    return spare[:, 0:NC * KP].rearrange("p (c k) -> p c k", c=NC)


def phase_queries(nc, x, wq_t, ln_w, wkv_t, ctx_t, q_scr, ident, kv_hi, kv_lo, spare, c_in, c_ready, xc, p_bufs, q_out):
    with ExitStack() as ctx:
        sb = lambda n, s, d=F32: ctx.enter_context(nc.sbuf_tensor(n, s, d))
        sem = lambda n: ctx.enter_context(nc.semaphore(n))
        w_raw = sb("q_w_raw", [P, 2, D])
        raw = [w_raw[:, 0, :], w_raw[:, 1, :], spare[:, 0:D], spare[:, D:2 * D]]
        w_hi = sb("q_w_hi", [P, NC, D], F32R)
        w_lo = sb("q_w_lo", [P, NC, D], F32R)
        lnw = sb("q_lnw", [P, NC])
        x_in = sb("q_x_in", [Q, 2, D])
        x_n = sb("q_x_n", [Q, 2, D])
        stats = sb("q_stats", [Q, 2, 12])
        mv = sb("q_mv", [Q, 2, 2])
        rstd = sb("q_rstd", [Q, 2, 1])
        var = sb("q_var", [Q, 2, 1])
        half_pow = sb("q_half_pow", [Q, 1])
        xt_hi = [xc[0], sb("q_xt_hi1", [P, NC, QG], F32R)]
        xt_lo = [xc[1], sb("q_xt_lo1", [P, NC, QG], F32R)]
        ring = [t[:, i, :] for t in p_bufs for i in range(KC)]
        q_hi, q_lo = ring[0:4], ring[4:8]
        c_raw = ctx_view(spare)
        c_parts = [ctx_view(t[:].rearrange("p c t -> p (c t)")) for t in xc]
        xp = ctx.enter_context(nc.psum_tensor("q_xp", [P, 2, 512], F32))
        qp = [ctx.enter_context(nc.psum_tensor(f"q_qp{i}", [P, 512], F32)) for i in range(4)]

        lnw_in = sem("q_lnw_in")
        w_in = [sem(f"q_w_in{i}") for i in range(4)]
        wscaled = sem("q_wscaled")
        whi_ready = sem("q_whi_ready")
        wlo_ready = [sem(f"q_wlo_ready{i}") for i in range(2)]
        xin = [sem(f"q_xin{i}") for i in range(2)]
        stat_step = sem("q_stat_step")
        var_ready = sem("q_var_ready")
        rstd_ready = sem("q_rstd_ready")
        xn_ready = sem("q_xn_ready")
        xp_ready = sem("q_xp_ready")
        xhi_ready = sem("q_xhi_ready")
        xlo_ready = sem("q_xlo_ready")
        q_mm = sem("q_mm")
        qhi_ready = sem("q_qhi_ready")
        qlo_ready = sem("q_qlo_ready")
        const_ready = sem("q_const_ready")

        wq_v = wq_t.rearrange("(c p) h -> c p h", p=P)
        NW = NC + NC // 2
        KV_STEPS = (5, 7, 9, 11)

        def kv_piece(i):
            return slice(2 * i, 2 * i + 2)

        with nc.Block() as block:
            @block.sync
            def _(sp):
                sp.dma_start(lnw[:], ln_w).then_inc(lnw_in, 16)

                def load_w(i):
                    if i >= 4:
                        sp.wait_ge(wlo_ready[i % 2], i // 2 - 1)
                    if i < NC:
                        sp.dma_start(raw[i % 4], wq_v[i]).then_inc(w_in[i % 4], 16)
                    else:
                        sp.dma_start(raw[i % 4].rearrange("p (c h) -> p c h", c=2),
                                     wkv_t[kv_piece(i - NC)].rearrange("c p h -> p c h")).then_inc(w_in[i % 4], 16)

                for i in range(NW):
                    load_w(i)

                def store_q(i):
                    g, grp = i % NG, i // NG
                    sp.wait_ge(qlo_ready, i + 1)
                    for hl, tile in ((0, q_hi), (1, q_lo)):
                        for r in range(REP):
                            src = f(tile[i % 4][HD * r:HD * r + HD, :]).rearrange("p (b t) -> p b t", b=GB)
                            dst = q_scr[hl, :, grp * GB:(grp + 1) * GB, g, r, :]
                            sp.dma_start(dst, src).then_inc(q_out[i % 4], 16)

                for i in range(NQG * NG):
                    store_q(i)
                    if i == KV_STEPS[-1]:
                        for w in wlo_ready:
                            sp.wait_ge(w, NW // 2)
                        sp.dma_start(ctx_view(spare), ctx_t[0]).then_inc(c_in, 16)

            def steps():
                out = []
                for i in range(NQG * NG):
                    b = (i // NG + 1) * GB + i % NG // 2
                    if b < B:
                        out.append(("nx"[i % 2], b))
                    out.append(("q", i))
                return out

            @block.gpsimd
            def _(pool):
                def load_x(b):
                    pool.dma_start(x_in[:, b % 2, :], x[b]).then_inc(xin[b % 2], 16)

                load_x(0)
                load_x(1)
                pool.wait_ge(const_ready, 1)
                for b in range(B):
                    pool.wait_ge(var_ready, b + 1)
                    if b >= 2:
                        pool.wait_ge(xn_ready, b - 1)
                    pool.tensor_tensor(rstd[:, b % 2, :], var[:, b % 2, :], half_pow[:], ALU.pow).then_inc(rstd_ready, 1)
                    if b + 2 < B:
                        pool.wait_ge(xn_ready, b + 1)
                        load_x(b + 2)
                    if b < NC // 2:
                        pool.wait_ge(whi_ready, 2 * b + 1)
                        pool.tensor_tensor(w_lo[:, 2 * b, :], raw[2 * b % 4], f(w_hi[:, 2 * b, :]),
                                           ALU.subtract).then_inc(wlo_ready[0], 1)

            @block.vector
            def _(dve):
                dve.memset(half_pow[:], -0.5).then_inc(const_ready, 1)

                def normalise(b, between=None):
                    s = b % 2
                    dve.wait_ge(xin[s], 16 * (b // 2 + 1))
                    for h in range(2):
                        dve.bn_stats(stats[:, s, 6 * h:6 * h + 6], x_in[:, s, HALF * h:HALF * (h + 1)]).then_inc(stat_step, 1)
                    dve.wait_ge(stat_step, 3 * b + 2)
                    dve.bn_aggr(mv[:, s, :], stats[:, s, :]).then_inc(stat_step, 1)
                    dve.wait_ge(stat_step, 3 * b + 3)
                    dve.tensor_scalar(var[:, s, :], mv[:, s, 1:2], 1.0 + EPS, EPS * EPS, ALU.mult, ALU.add).then_inc(var_ready, 1)
                    if between:
                        between()
                    dve.wait_ge(rstd_ready, b + 1)
                    if b >= 2:
                        dve.wait_ge(xp_ready, b - 1)
                    dve.tensor_scalar(x_n[:, s, :], x_in[:, s, :], mv[:, s, 0:1], rstd[:, s, :],
                                      ALU.subtract, ALU.mult).then_inc(xn_ready, 1)

                def split_w(i):
                    dve.wait_ge(whi_ready, i + 1)
                    if i < NC:
                        dve.scalar_tensor_tensor(out=w_lo[:, i, :], in0=raw[i % 4], scalar=lnw[:, i:i + 1],
                                                 in1=f(w_hi[:, i, :]), op0=ALU.mult, op1=ALU.subtract).then_inc(wlo_ready[1], 1)
                    else:
                        cs = kv_piece(i - NC)
                        dve.tensor_tensor(kv_lo[:, cs, :], raw[i % 4].rearrange("p (c h) -> p c h", c=2),
                                          f(kv_hi[:, cs, :]), ALU.subtract).then_inc(wlo_ready[i % 2], 1)

                def split_x(b):
                    grp, t0 = b // GB, (b % GB) * Q
                    dve.wait_ge(xhi_ready, b + 1)
                    dst = xt_lo[grp % 2][:, :, t0:t0 + Q].rearrange("p (k c) t -> p k c t", k=2)
                    hi = f(xt_hi[grp % 2][:, :, t0:t0 + Q]).rearrange("p (k c) t -> p k c t", k=2)
                    src = xp[:, :, 0:4 * Q].rearrange("p k (c t) -> p k c t", c=4)
                    dve.tensor_tensor(dst, src, hi, ALU.subtract).then_inc(xlo_ready, 1)

                for b in range(GB):
                    normalise(b, (lambda: split_w(2 * b - 1)) if b else None)
                    if b:
                        split_x(b - 1)
                split_w(NC - 1)
                split_x(GB - 1)
                for kind, i in steps():
                    if kind == "n":
                        normalise(i)
                    elif kind == "x":
                        split_x(i)
                    else:
                        if i in KV_STEPS:
                            split_w(NC + KV_STEPS.index(i))
                        dve.wait_ge(qhi_ready, i + 1)
                        if i >= 4:
                            dve.wait_ge(q_out[i % 4], NOUT * (i // 4))
                        dve.tensor_tensor(q_lo[i % 4], qp[i % 4][:, 0:QG], f(q_hi[i % 4]), ALU.subtract).then_inc(qlo_ready, 1)
                        if i > NG * (NQG - 1) and i <= NG * (NQG - 1) + 4:
                            q = i - NG * (NQG - 1) - 1
                            cs = slice(2 * q, 2 * q + 2)
                            dve.wait_ge(c_ready[0], q + 1)
                            dve.tensor_tensor(c_parts[1][:, cs, :], c_raw[:, cs, :], f(c_parts[0][:, cs, :]),
                                              ALU.subtract).then_inc(c_ready[1], 1)

            @block.scalar
            def _(act):
                def split_w(i):
                    act.wait_ge(w_in[i % 4], 16 * (i // 4 + 1))
                    if i < NC and i % 2 == 0:
                        act.activation(raw[i % 4], raw[i % 4], ACT.Copy, scale=lnw[:, i:i + 1]).then_inc(wscaled, 1)
                        act.wait_ge(wscaled, i // 2 + 1)
                        act.copy(w_hi[:, i, :], raw[i % 4]).then_inc(whi_ready, 1)
                    elif i < NC:
                        act.activation(w_hi[:, i, :], raw[i % 4], ACT.Copy, scale=lnw[:, i:i + 1]).then_inc(whi_ready, 1)
                    else:
                        act.copy(kv_hi[:, kv_piece(i - NC), :],
                                 raw[i % 4].rearrange("p (c h) -> p c h", c=2)).then_inc(whi_ready, 1)

                def split_x(b):
                    grp, t0 = b // GB, (b % GB) * Q
                    act.wait_ge(xp_ready, b + 1)
                    if grp >= 2:
                        act.wait_ge(q_mm, NG * (grp - 1))
                    dst = xt_hi[grp % 2][:, :, t0:t0 + Q].rearrange("p (k c) t -> p k c t", k=2)
                    src = xp[:, :, 0:4 * Q].rearrange("p k (c t) -> p k c t", c=4)
                    act.copy(dst, src).then_inc(xhi_ready, 1)

                act.wait_ge(lnw_in, 16)
                for c in range(NC):
                    split_w(c)
                    if c % 2:
                        split_x(c // 2)
                for kind, i in steps():
                    if kind == "x":
                        split_x(i)
                    elif kind == "q":
                        if i in KV_STEPS:
                            split_w(NC + KV_STEPS.index(i))
                        act.wait_ge(q_mm, i + 1)
                        if i >= 4:
                            act.wait_ge(q_out[i % 4], NOUT * (i // 4))
                        act.copy(q_hi[i % 4], qp[i % 4][:, 0:QG]).then_inc(qhi_ready, 1)
                        if i > NG * (NQG - 1) and i <= NG * (NQG - 1) + 4:
                            q = i - NG * (NQG - 1) - 1
                            cs = slice(2 * q, 2 * q + 2)
                            act.wait_ge(c_in, 16)
                            act.copy(c_parts[0][:, cs, :], c_raw[:, cs, :]).then_inc(c_ready[0], 1)

            @block.tensor
            def _(pe):
                def products(i, c, cols):
                    grp, g = i // NG, i % NG
                    wh, wl = w_hi[:, c, g * P:(g + 1) * P], w_lo[:, c, g * P:(g + 1) * P]
                    xh, xl = xt_hi[grp % 2][:, c, cols], xt_lo[grp % 2][:, c, cols]
                    out = qp[i % 4][:, cols]
                    pe.matmul(out, wh, xh, start=(c == 0), stop=False)
                    pe.matmul(out, wh, xl, start=False, stop=False)
                    return pe.matmul(out, wl, xh, start=False, stop=(c == NC - 1))

                first, second = slice(0, QG // 2), slice(QG // 2, QG)

                def first_half(c):
                    pe.wait_ge(wlo_ready[c % 2], c // 2 + 1)
                    if c == 0:
                        pe.wait_ge(xlo_ready, 2)
                    for i in range(4):
                        products(i, c, first)

                order = [("x", 0), ("x", 1), ("x", 2)] + [("h", c) for c in range(NC // 2)] + [("x", 3)]
                order += [("h", c) for c in range(NC // 2, NC)] + steps()
                for kind, i in order:
                    if kind == "h":
                        first_half(i)
                    elif kind == "x":
                        pe.wait_ge(xn_ready, i + 1)
                        if i >= 1:
                            pe.wait_ge(xlo_ready, i)
                        for c in range(NC):
                            mm = pe.transpose(xp[:, c // 4, (c % 4) * Q:(c % 4 + 1) * Q],
                                              x_n[:, i % 2, c * P:(c + 1) * P], ident[0:Q, 0:Q])
                        mm.then_inc(xp_ready, 1)
                    elif kind == "q":
                        grp, g = i // NG, i % NG
                        if g == 0:
                            pe.wait_ge(xlo_ready, GB * (grp + 1))
                        if i >= 4:
                            pe.wait_ge(qlo_ready, i - 3)
                        for c in range(NC):
                            mm = products(i, c, second if i < 4 else slice(0, QG))
                        mm.then_inc(q_mm, 1)


def tile_views(spare):
    return [spare[:, i * D:(i + 1) * D].rearrange("p (c t) -> p c t", c=NC) for i in range(3)]


def load_attention(sp, views, o_scr, r_scr, t0, at_in, reps=range(REP)):
    a, b, r1 = views
    for r in reps:
        rows = slice(HD * r, HD * r + HD)
        sp.dma_start(a[rows, :, :], o_scr[0:HD, :, r, bass.ds(t0, TT)]).then_inc(at_in, 16)
        sp.dma_start(b[rows, :, :], o_scr[HD:2 * HD, :, r, bass.ds(t0, TT)]).then_inc(at_in, 16)
        sp.dma_start(r1[rows, :, :], r_scr[:, :, r, bass.ds(t0, TT)].broadcast_to([HD, NC, TT])).then_inc(at_in, 16)


def denominators(scr, row, b0, b1):
    toks = scr[row:row + 1, :, :, b0 * Q:b1 * Q]
    return toks.rearrange("a g r (s t) -> (a g r) s t", s=4)


def phase_attention(nc, ctx_t, q_scr, o_scr, ident, w_hi, w_lo, wo_raw, spare, c_in, c_ready, xc, p_bufs, q_out,
                    wo_t, r_scr, w_in, at_in):
    with ExitStack() as ctx:
        sb = lambda n, s, d=F32: ctx.enter_context(nc.sbuf_tensor(n, s, d))
        ps = lambda n, s: ctx.enter_context(nc.psum_tensor(n, s, F32))
        sem = lambda n: ctx.enter_context(nc.semaphore(n))
        c_raw = ctx_view(spare)
        first_hi, first_lo = (ctx_view(t[:].rearrange("p c t -> p (c t)")) for t in xc)
        c_hi = [first_hi, sb("a_c_hi1", [P, NC, KP], F32R)]
        c_lo = [first_lo, sb("a_c_lo1", [P, NC, KP], F32R)]
        k_hi = sb("a_k_hi", [P, 2, KP], F32R)
        k_lo = sb("a_k_lo", [P, 2, KP], F32R)
        k_st = [sb(f"a_k_st{i}", [3 * HD + 2, NG, KP], F32R) for i in range(2)]
        q_st = [sb(f"a_q_st{i}", [3 * HD + 2, NG, REP * Q], F32R) for i in range(2)]
        v_st = [sb(f"a_v_st{i}", [KCS, KC, NG, VW], F32R) for i in range(2)]
        p_f = [sb(f"a_p_f{i}", [KCS, KC, REP * Q]) for i in range(2)]
        p_hi = [t[0:KCS] for t in p_bufs[0:2]]
        p_lo = [p_bufs[2][0:KCS], sb("a_p_lo1", [KCS, KC, REP * Q], F32R)]
        o_sb = [sb(f"a_o_sb{i}", [VW, REP * Q]) for i in range(OB)]
        row_max = sb("a_row_max", [Q, 2, 16])
        neg_max = sb("a_neg_max", [Q, 2, 32])
        max_t = [sb(f"a_max_t{i}", [32, Q], F32R) for i in range(2)]
        a_ps = ps("a_ps", [P, 2, 512])
        b_ps = ps("b_ps", [P, 3, 512])
        o_ps = ps("o_ps", [P, 512])
        ring = [ps(f"a_ring{i}", [P, 512]) for i in range(2)]

        c_hi_ready, c_lo_ready = c_ready
        ones_ready = sem("a_ones_ready")
        v_mm = sem("a_v_mm")
        v_hi_ready = sem("a_v_hi_ready")
        v_lo_ready = sem("a_v_lo_ready")
        k_mm = sem("a_k_mm")
        k_hi_ready = sem("a_k_hi_ready")
        k_lo_ready = sem("a_k_lo_ready")
        k_in = [[sem(f"a_k_in{i}{c}") for c in range(2)] for i in range(2)]
        q_in = [[sem(f"a_q_in{i}{h}") for h in range(2)] for i in range(2)]
        a_mm = sem("a_a_mm")
        a_max = sem("a_a_max")
        neg_step = sem("a_neg_step")
        neg_ready = sem("a_neg_ready")
        t_mm = sem("a_t_mm")
        t_ready = sem("a_t_ready")
        shift_in = [sem(f"a_shift_in{h}") for h in range(2)]
        b_mm = sem("a_b_mm")
        exp_ready = sem("a_exp_ready")
        p_hi_ready = sem("a_p_hi_ready")
        p_lo_ready = sem("a_p_lo_ready")
        p_lo_rest = sem("a_p_lo_rest")
        pv_mm = sem("a_pv_mm")
        o_ready = sem("a_o_ready")
        o_out = [sem(f"a_o_out{i}") for i in range(OB)]
        den_in = sem("a_den_in")
        den_rec = sem("a_den_rec")
        r_out = sem("a_r_out")
        NKD = 12 * 16
        NQD = 3 * 16
        NSD = 2 * 16

        PEEL, LOOPS = 2, 5

        def schedule(eng, emit):
            for n in range(-2, PEEL):
                emit(n, n, n % 2, 0)
            with eng.Fori(PEEL // 2, PEEL // 2 + LOOPS) as j:
                emit(None, 2 * j, 0, j)
                emit(None, 2 * j + 1, 1, j)
            for n in range(PEEL + 2 * LOOPS, B):
                emit(n, n, n % 2, 0)

        def on(static, ahead):
            return static is None or 0 <= static + ahead < B

        def pair(static, par, j, ahead):
            return (static + ahead) // 2 if static is not None else j + (par + ahead) // 2

        def ctx_splits(s, g):
            q, k = {6: (0, 3), 7: (1, 3), 0: (2, 2), 1: (3, 2)}.get(g, (0, None))
            return [(q, k)] if k is not None and is_later(s, k) else []

        def is_later(s, k):
            return on(s, k) and not (s is not None and s + k == 0)

        def lo_splits(s, g):
            q, k = {7: (0, 3), 0: (1, 2), 1: (2, 2), 2: (3, 2)}.get(g, (0, None))
            return [(q, k)] if k is not None and is_later(s, k) else []

        def v_batch(s, n):
            if s == -2:
                return 0
            return n + 1 if on(s, 1) and s != -1 else None

        def v_bank(par, job):
            return ring[(par, par, 1 - par)[job]]

        def row_banks(s, p):
            return b_ps if s == 0 and p == 1 else a_ps

        def k_bank(par, job):
            return ring[(1 - par, par)[job]]

        wo_v = wo_t.rearrange("(c p) h -> c p h", p=P)
        NDEN = NDB * Q // 4
        DEN_PARTS = 3
        den = spare[:, 2 * D:2 * D + NDEN]
        o_tok = o_scr.rearrange("v g r b q -> v g r (b q)")

        with nc.Block() as block:
            @block.sync
            def _(sp):
                def prefetch(s, g):
                    if s == B - 2 and g == 7:
                        sp.wait_ge(k_mm, 2 * B)
                        sp.wait_ge(v_mm, KC * B)
                    if s == B - 2 and g == 1:
                        for i in range(OB):
                            sp.wait_ge(o_out[i], 16 * NDB * NG // OB)
                        sp.dma_start(den, denominators(o_tok, 2 * HD, 0, NDB)).then_inc(den_in, 16)
                    if s == B - 1 and g == 2:
                        sp.wait_ge(den_rec, DEN_PARTS)
                        sp.dma_start(denominators(r_scr, 0, 0, NDB), den).then_inc(r_out, 16)
                    if s == B - 1 and g >= 4:
                        if g == 4:
                            sp.wait_ge(r_out, 16)
                        load_attention(sp, tile_views(spare), o_tok, r_scr, 0, at_in, [g - 4])
                    step = {(B - 2, 7): 0, (B - 1, 0): 1, (B - 1, 1): 2, (B - 1, 2): 3}.get((s, g))
                    for c in range(2 * step, 2 * step + 2) if step is not None else ():
                        sp.dma_start(wo_raw[:, c, :], wo_v[c]).then_inc(w_in[c], 16)

                def load_q(b, par, h):
                    g0 = 4 * h
                    for rep, hl in enumerate((0, 1, 0)):
                        dst = f(q_st[par][HD * rep:HD * rep + HD, g0:g0 + 4, :])
                        src = q_scr[hl, :, b, g0:g0 + 4, :, :].rearrange("d g r t -> d g (r t)")
                        sp.dma_start(dst, src).then_inc(q_in[par][h], 16)

                def stack_k(par, c):
                    for rep, tile in enumerate((k_hi, k_hi, k_lo)):
                        for i in range(4):
                            sp.dma_start(f(k_st[par][HD * rep:HD * rep + HD, 4 * c + i, :]),
                                         f(tile[HD * i:HD * i + HD, c, :])).then_inc(k_in[par][c], 16)

                def shift(par, h):
                    for hl in range(2):
                        dst = f(q_st[par][96 + hl:97 + hl, 4 * h:4 * h + 4, :]).rearrange("p g (r t) -> p (g r) t", t=Q)
                        sp.dma_start(dst, f(max_t[h][16 * hl:16 * hl + 16, :])).then_inc(shift_in[h], 16)

                def store_o(b, g):
                    src = o_sb[g % OB][:].rearrange("p (r t) -> p r t", r=REP)
                    sp.dma_start(o_scr[:, g, :, b, :], src).then_inc(o_out[g % OB], 16)

                def emit(s, n, par, j):
                    for g in range(NG):
                        if g >= 2 and on(s, 0):
                            sp.wait_ge(o_ready, NG * n + g - 1)
                            store_o(n, g - 2)
                        if g < 2 and on(s, -1):
                            sp.wait_ge(o_ready, NG * n + g - 1)
                            store_o(n - 1, NG - 2 + g)
                        if g == 0 and on(s, 1):
                            if on(s, -1):
                                sp.wait_ge(b_mm, NG * n)
                            load_q(n + 1, 1 - par, 1)
                            sp.wait_ge(k_lo_ready, 2 * (n + 1) + 2)
                            stack_k(1 - par, 1)
                        if g == 2 and on(s, 3):
                            sp.wait_ge(c_hi_ready, 4 * (n + 3))
                            sp.wait_ge(c_lo_ready, 4 * (n + 3))
                            sp.dma_start(c_raw, ctx_t[n + 3]).then_inc(c_in, 16)
                        if g == 1 and on(s, 0):
                            sp.wait_ge(t_ready, 2 * (n + 1))
                            shift(par, 1)
                        if g == 0 and s == -2:
                            for slot in q_out:
                                sp.wait_ge(slot, NOUT * (NQG * NG // 4))
                        if g == 4 and on(s, 2):
                            if on(s, 0):
                                sp.wait_ge(b_mm, NG * n + 4)
                            load_q(n + 2, par, 0)
                            sp.wait_ge(k_lo_ready, 2 * (n + 2) + 1)
                            stack_k(par, 0)
                        if g == 6 and on(s, 1):
                            sp.wait_ge(t_ready, 2 * (n + 1) + 1)
                            shift(1 - par, 0)
                        prefetch(s, g)

                schedule(sp, emit)
                for g in (NG - 2, NG - 1):
                    sp.wait_ge(o_ready, NG * (B - 1) + g + 1)
                    store_o(B - 1, g)
                for i in range(OB):
                    sp.wait_ge(o_out[i], 16 * B * NG // OB)

            @block.tensor
            def _(pe):
                def scores_rows(s, b, par, jj, g, p):
                    if p == 0 and g % 4 == 0:
                        pe.wait_ge(k_in[par][g // 4], NKD * (jj + 1))
                        pe.wait_ge(q_in[par][g // 4], NQD * (jj + 1))
                    if s is None or s > 0:
                        pe.wait_ge(a_max, 16 * b + 2 * g + p)
                    elif g > 0:
                        pe.wait_ge(a_max, 2 * g + p - 1)
                    for i in range(2):
                        r = 2 * p + i
                        mm = pe.matmul(row_banks(s, p)[0:Q, i, 0:KP], q_st[par][0:96, g, r * Q:(r + 1) * Q],
                                       k_st[par][0:96, g, :], start=True, stop=True)
                    mm.then_inc(a_mm, 1)

                def scores_cols(s, b, par, g):
                    if g % 4 == 0:
                        pe.wait_ge(shift_in[g // 4], NSD * (b + 1))
                    if s is None or s > 0 or g > 0:
                        pe.wait_ge(exp_ready, NG * b + g)
                    else:
                        pe.wait_ge(a_max, 16)
                    for c in range(KC):
                        mm = pe.matmul(b_ps[0:KCS, c, 0:REP * Q], k_st[par][:, g, c * KCS:(c + 1) * KCS],
                                       q_st[par][:, g, :], start=True, stop=True)
                    mm.then_inc(b_mm, 1)

                def pv(s, b, par, g):
                    pe.wait_ge(p_lo_ready, NG * b + g + 1)
                    if s == B - 1:
                        pe.wait_ge(p_lo_rest, g + 1)
                    if g % NG == 0:
                        pe.wait_ge(v_lo_ready, KC * (b + 1))
                    if s is None or s > 0 or g > 0:
                        pe.wait_ge(o_ready, NG * b + g)
                    for c in range(KC):
                        w = v_st[par][:, c, g, :]
                        pe.matmul(o_ps[0:VW, 0:REP * Q], w, p_hi[g % 2][:, c, :], start=(c == 0), stop=False)
                        mm = pe.matmul(o_ps[0:VW, 0:REP * Q], w, p_lo[g % 2][:, c, :], start=False, stop=(c == KC - 1))
                    mm.then_inc(pv_mm, 1)

                def max_turn(s, b, h, bank):
                    pe.wait_ge(neg_ready, 2 * b + h + 1)
                    pe.transpose(bank[0:32, 0:Q], neg_max[:, h, :], ident[0:Q, 0:Q]).then_inc(t_mm, 1)

                def v_part(s, n, par, job, part):
                    b = v_batch(s, n)
                    if b is None:
                        return
                    if part == 0:
                        if job == 0 and s == 0:
                            pe.wait_ge(k_lo_ready, 2 * (n + 1) + 1)
                        elif job == 0 and s != -2:
                            pe.wait_ge(v_lo_ready, KC * b)
                        if job == 1:
                            pe.wait_ge(v_lo_ready, KC * b + 1)
                        if job == 2 and on(s, 2):
                            pe.wait_ge(k_lo_ready, 2 * (n + 2) + 1)
                        elif job == 2:
                            pe.wait_ge(t_ready, 2 * n + 2)
                    cpar = 0 if s == -2 else 1 - par
                    for st in range(8 * part, 8 * part + 8):
                        c, pas = divmod(st, 3)
                        if s == -2 and job == 0 and st % 6 == 0:
                            pe.wait_ge(c_lo_ready, c // 2 + 1)
                        a = (c_hi, c_lo, c_hi)[pas][cpar][:, c, job * KCS:(job + 1) * KCS]
                        w = (w_hi, w_hi, w_lo)[pas][:, c, NG * HD:]
                        mm = pe.matmul(v_bank(par, job)[0:KCS, 0:NG * HD], a, w, start=(st == 0), stop=(st == 23))
                    if part == 2:
                        mm.then_inc(v_mm, 1)

                def k_part(s, n, par, job, part):
                    if not on(s, 2):
                        return
                    if part == 0 and job == 0:
                        if on(s, 0):
                            pe.wait_ge(t_ready, 2 * n + 2)
                        elif s == -1:
                            pe.wait_ge(k_lo_ready, 2)
                    if part == 0 and job == 1:
                        if on(s, 1):
                            pe.wait_ge(t_ready, 2 * (n + 1) + 1)
                        else:
                            pe.wait_ge(v_lo_ready, 2)
                    for st in range(8 * part, 8 * part + 8):
                        c, pas = divmod(st, 3)
                        if job == 0 and st % 6 == 0:
                            pe.wait_ge(c_lo_ready, 4 * (n + 2) + c // 2 + 1)
                        a = (c_hi, c_lo, c_hi)[pas][par][:, c, :]
                        w = (w_hi, w_hi, w_lo)[pas][:, c, job * P:(job + 1) * P]
                        mm = pe.matmul(k_bank(par, job)[:, 0:KP], w, a, start=(st == 0), stop=(st == 23))
                    if part == 2:
                        mm.then_inc(k_mm, 1)

                def kv_piece(s, n, par, i):
                    for first, part_of, job in ((0, v_part, 0), (4, k_part, 0), (7, v_part, 1),
                                                (10, v_part, 2), (13, k_part, 1)):
                        if first <= i < first + 3:
                            part_of(s, n, par, job, i - first)

                def emit(s, n, par, j):
                    if s == -1:
                        pe.wait_ge(ones_ready, 4)
                    for g in range(NG):
                        if on(s, 1) and not on(s, 0):
                            scores_rows(None if s is None else s + 1, n + 1, 1 - par, pair(s, par, j, 1), g, 0)
                        if g == 1 and on(s, 0):
                            pe.wait_ge(k_lo_ready, 2 * (n + 2) if on(s, 1) else 2 * B)
                            pe.wait_ge(t_ready, 2 * n + 1)
                            max_turn(s, n, 1, ring[1 - par])
                        if g == 6 and on(s, 1):
                            pe.wait_ge(v_lo_ready, KC if s == -1 else KC * (n + 1) + 2)
                            max_turn(s, n + 1, 0, ring[par])
                        if on(s, 0):
                            scores_cols(s, n, par, g)
                            if on(s, 1) and g != 2:
                                scores_rows(None if s is None else s + 1, n + 1, 1 - par, pair(s, par, j, 1), g, 0)
                        if g >= 2 and on(s, 0):
                            pv(s, n, par, g - 2)
                        if g < 2 and on(s, -1):
                            pv(None if s is None else s - 1, n - 1, 1 - par, NG - 2 + g)
                        if on(s, 0) and on(s, 1) and g == 2:
                            scores_rows(None if s is None else s + 1, n + 1, 1 - par, pair(s, par, j, 1), g, 0)
                        kv_piece(s, n, par, 2 * g)
                        if on(s, 1):
                            scores_rows(None if s is None else s + 1, n + 1, 1 - par, pair(s, par, j, 1), g, 1)
                        kv_piece(s, n, par, 2 * g + 1)

                schedule(pe, emit)
                pv(B - 1, B - 1, (B - 1) % 2, NG - 2)
                pv(B - 1, B - 1, (B - 1) % 2, NG - 1)

            @block.vector
            def _(dve):
                for i in range(2):
                    dve.memset(f(v_st[i][:, :, :, 2 * HD:VW]), 1.0).then_inc(ones_ready, 1)

                def row_maxima(s, b, g, p):
                    dve.wait_ge(a_mm, 16 * b + 2 * g + p + 1)
                    dve.tensor_reduce(row_max[:, g // 4, (g % 4) * 4 + 2 * p:(g % 4) * 4 + 2 * p + 2],
                                      row_banks(s, p)[0:Q, 0:2, 0:K], AX, ALU.max).then_inc(a_max, 1)

                def negate(s, b, h):
                    dve.wait_ge(a_max, 16 * b + 8 * h + 8)
                    if s is None or s > 0:
                        dve.wait_ge(t_mm, 2 * b + h - 1)
                    dve.tensor_scalar(neg_max[:, h, 0:16].bitcast(F32R), row_max[:, h, :], -1.0, None, ALU.mult).then_inc(neg_step, 1)
                    dve.wait_ge(neg_step, 2 * b + h + 1)
                    dve.scalar_tensor_tensor(out=neg_max[:, h, 16:32], in0=row_max[:, h, :], scalar=-1.0,
                                             in1=neg_max[:, h, 0:16], op0=ALU.mult, op1=ALU.subtract).then_inc(neg_ready, 1)

                def take_turned(s, b, h, bank):
                    dve.wait_ge(t_mm, 2 * b + h + 1)
                    if s is None or s > 0:
                        dve.wait_ge(shift_in[h], NSD * b)
                    dve.tensor_copy(max_t[h][:], bank[0:32, 0:Q]).then_inc(t_ready, 1)

                def split_p(s, b, g):
                    dve.wait_ge(exp_ready, NG * b + g + 1)
                    if s is None or s > 0 or g >= 2:
                        dve.wait_ge(pv_mm, NG * b + g - 1)
                    dve.tensor_copy(p_hi[g % 2][:], p_f[g % 2][:]).then_inc(p_hi_ready, 1)
                    if s == B - 1:
                        dve.wait_ge(p_hi_ready, NG * b + g + 1)
                        if g == 0:
                            dve.wait_ge(p_lo_ready, NG * b)
                        dve.tensor_tensor(p_lo[g % 2][:, 0:2, :], p_f[g % 2][:, 0:2, :], f(p_hi[g % 2][:, 0:2, :]),
                                          ALU.subtract).then_inc(p_lo_ready, 1)

                def split_v(s, n, par, job):
                    b = v_batch(s, n)
                    if b is not None:
                        v = v_st[0 if s == -2 else 1 - par]
                        dve.wait_ge(v_hi_ready, KC * b + job + 1)
                        src = v_bank(par, job)[0:KCS, 0:NG * HD].rearrange("p (g d) -> p g d", g=NG)
                        dve.tensor_tensor(v[:, job, :, HD:2 * HD], src, f(v[:, job, :, 0:HD]),
                                          ALU.subtract).then_inc(v_lo_ready, 1)

                def split_k(b, bank, job):
                    dve.wait_ge(k_hi_ready, 2 * b + job + 1)
                    dve.tensor_tensor(k_lo[:, job, :], bank[:, 0:KP], f(k_hi[:, job, :]),
                                      ALU.subtract).then_inc(k_lo_ready, 1)

                def split_ctx(b, par, h):
                    dve.wait_ge(c_hi_ready, 4 * b + h + 1)
                    cs = slice(2 * h, 2 * h + 2)
                    dve.tensor_tensor(c_lo[par][:, cs, :], c_raw[:, cs, :], f(c_hi[par][:, cs, :]), ALU.subtract).then_inc(c_lo_ready, 1)

                def emit(s, n, par, j):
                    for g in range(NG):
                        if g == 0 and s == -1:
                            split_k(n + 1, k_bank(1 - par, 1), 1)
                        if g == 2:
                            for q, k in lo_splits(s, g):
                                split_ctx(n + k, (par + k) % 2, q)
                        if on(s, 1):
                            row_maxima(None if s is None else s + 1, n + 1, g, 0)
                        if g == 0 and on(s, 1) and s != -1:
                            split_k(n + 1, k_bank(1 - par, 1), 1)
                        if g == 1 and on(s, 0):
                            take_turned(s, n, 1, ring[1 - par])
                        if g == 6 and on(s, 1):
                            take_turned(None if s is None else s + 1, n + 1, 0, ring[par])
                        if s == B - 2 and g >= NG - DEN_PARTS:
                            i = g - (NG - DEN_PARTS)
                            part = den[:, i * NDEN // DEN_PARTS:(i + 1) * NDEN // DEN_PARTS]
                            dve.wait_ge(den_in, 16)
                            dve.reciprocal(part, part).then_inc(den_rec, 1)
                        if g == 5:
                            split_v(s, n, par, 1)
                        for q, k in lo_splits(s, g) if g != 2 else []:
                            split_ctx(n + k, (par + k) % 2, q)
                        if on(s, 0):
                            split_p(s, n, g)
                        if on(s, 1):
                            row_maxima(None if s is None else s + 1, n + 1, g, 1)
                            if g == 3:
                                negate(None if s is None else s + 1, n + 1, 0)
                            if g == 7:
                                negate(None if s is None else s + 1, n + 1, 1)
                        if g == 1:
                            split_v(s, n, par, 0)
                        if g == 3 and on(s, 2):
                            split_k(n + 2, k_bank(par, 0), 0)
                        if g == 6:
                            split_v(s, n, par, 2)

                schedule(dve, emit)

            @block.gpsimd
            def _(pool):
                for i in range(2):
                    pool.memset(f(k_st[i][96:98, :, :]), 1.0).then_inc(ones_ready, 1)

                def emit(s, n, par, j):
                    for g in range(NG):
                        if s == B - 1:
                            pool.wait_ge(p_hi_ready, NG * n + g + 1)
                            pool.tensor_tensor(p_lo[g % 2][:, 2, :], p_f[g % 2][:, 2, :], f(p_hi[g % 2][:, 2, :]),
                                               ALU.subtract).then_inc(p_lo_rest, 1)
                        elif on(s, 0):
                            pool.wait_ge(p_hi_ready, NG * n + g + 1)
                            pool.tensor_tensor(p_lo[g % 2][:], p_f[g % 2][:], f(p_hi[g % 2][:]), ALU.subtract).then_inc(p_lo_ready, 1)

                schedule(pool, emit)

            @block.scalar
            def _(act):
                def exponentials(s, b, g):
                    act.wait_ge(b_mm, NG * b + g + 1)
                    if s is None or s > 0 or g >= 2:
                        act.wait_ge(p_lo_ready, NG * b + g - 1)
                    if s == B - 1 and g >= 2:
                        act.wait_ge(p_lo_rest, g - 1)
                    act.activation(p_f[g % 2][:], b_ps[0:KCS, :, 0:REP * Q], ACT.Exp, scale=SCALE).then_inc(exp_ready, 1)

                def take_o(s, b, g):
                    act.wait_ge(pv_mm, NG * b + g + 1)
                    if s is None or s > 0 or g >= OB:
                        act.wait_ge(o_out[g % OB], 16 * (NG // OB * b + g // OB))
                    act.copy(o_sb[g % OB][:], o_ps[0:VW, 0:REP * Q]).then_inc(o_ready, 1)

                def take_v(s, n, par, job):
                    b = v_batch(s, n)
                    if b is not None:
                        act.wait_ge(v_mm, KC * b + job + 1)
                        if s is None or s >= 1:
                            act.wait_ge(pv_mm, NG * (b - 1))
                        src = v_bank(par, job)[0:KCS, 0:NG * HD].rearrange("p (g d) -> p g d", g=NG)
                        act.copy(v_st[0 if s == -2 else 1 - par][:, job, :, 0:HD], src).then_inc(v_hi_ready, 1)

                def take_k(s, b, par, jj, job):
                    act.wait_ge(k_mm, 2 * b + job + 1)
                    if s is None or s >= 1:
                        act.wait_ge(k_in[1 - par][job], NKD * jj)
                    act.copy(k_hi[:, job, :], k_bank(par, job)[:, 0:KP]).then_inc(k_hi_ready, 1)

                def split_ctx(s, b, par, h):
                    act.wait_ge(c_in, 16 * (b + 1))
                    if s is None or s >= 2:
                        act.wait_ge(v_mm, KC * (b - 1))
                    cs = slice(2 * h, 2 * h + 2)
                    act.copy(c_hi[par][:, cs, :], c_raw[:, cs, :]).then_inc(c_hi_ready, 1)

                def emit(s, n, par, j):
                    ahead = lambda k: None if s is None else s + k
                    for g in range(NG):
                        if on(s, 0):
                            exponentials(s, n, g)
                        if g >= 2 and on(s, 0):
                            take_o(s, n, g - 2)
                        if g < 2 and on(s, -1):
                            take_o(ahead(-1), n - 1, NG - 2 + g)
                        if g in (1, 4, 6):
                            take_v(s, n, par, (1, 4, 6).index(g))
                        if g in (3, 7) and on(s, 2):
                            take_k(ahead(2), n + 2, par, pair(s, par, j, 3), (3, 7).index(g))
                        for q, k in ctx_splits(s, g):
                            split_ctx(ahead(k), n + k, (par + k) % 2, q)

                schedule(act, emit)
                take_o(B - 1, B - 1, NG - 2)
                take_o(B - 1, B - 1, NG - 1)


def phase_output(nc, x, wf_t, bias, gate_t, in_scale, out_scale, o_scr, r_scr, out, ident, wo_raw, spare,
                 w_in, at_in):
    with ExitStack() as ctx:
        sb = lambda n, s, d=F32: ctx.enter_context(nc.sbuf_tensor(n, s, d))
        ps = lambda n, s: ctx.enter_context(nc.psum_tensor(n, s, F32))
        sem = lambda n: ctx.enter_context(nc.semaphore(n))
        two = range(2)
        wo_hi = sb("o_wo_hi", [P, NC, D], F32R)
        wo_lo = sb("o_wo_lo", [P, NC, D], F32R)
        sign = sb("o_sign", [P, NC, D], F32R)
        gate = sb("o_gate", [P, NC, NE])
        gate_hl = sb("o_gate_hl", [P, NC, 2 * NE], F32R)
        s_in = sb("o_s_in", [EROWS, D], F32R)
        s_out = sb("o_s_out", [EROWS, D], F32R)
        bias_b = sb("o_bias", [P, D])
        a_first, b_t, r_t = tile_views(spare)
        a_t = [a_first, sb("o_a_t1", [P, NC, TT])]
        den = sb("o_den_last", [P, (B - NDB) * Q // 4])
        a_hi = [sb(f"o_a_hi{i}", [P, NC, TT], F32R) for i in two]
        a_lo = [sb(f"o_a_lo{i}", [P, NC, TT], F32R) for i in two]
        x_in = [sb(f"o_x_in{i}", [TT, D]) for i in two]
        x1 = [sb(f"o_x1{i}", [TT, D]) for i in two]
        s_raw = [x1[1][0:EROWS, :], x1[0][0:EROWS, :]]
        raw = [wo_raw[:, c, :] for c in range(NC)]
        x1b = raw[1:3]
        x_n = raw[0]
        x_hi = sb("o_x_hi", [P, NC, TT], F32R)
        x_lo = sb("o_x_lo", [P, NC, TT], F32R)
        x_t = [raw[i].rearrange("p (c t) -> p c t", c=NC) for i in (5, 6)]
        xs = raw[4].rearrange("p (c t) -> p c t", c=NC)
        xs_hi = sb("o_xs_hi", [P, NC, TT], F32R)
        xs_lo = sb("o_xs_lo", [P, NC, TT], F32R)
        osc, y = raw[7], raw[3]
        stats = sb("o_stats", [TT, 12])
        mv = sb("o_mv", [TT, 2])
        var = sb("o_var", [TT, 1])
        rstd = sb("o_rstd", [TT, 1])
        half_pow = sb("o_half_pow", [TT, 1])
        lg_t = sb("o_lg_t", [2 * NE, TT])
        lg = sb("o_lg", [TT, NE])
        neg = sb("o_neg", [TT, 1])
        ex = sb("o_ex", [TT, NE])
        esum = sb("o_esum", [TT, 1])
        rden = sb("o_rden", [TT, 1])
        route = sb("o_route", [TT, EROWS])
        route_t = sb("o_route_t", [EROWS, TT], F32R)
        w_ps = ps("o_w_ps", [P, 2, HALF])
        x_ps = ps("o_x_ps", [P, 2, HALF])
        f_ps = ps("o_f_ps", [P, 2, HALF])
        o_ps = ps("o_o_ps", [P, HALF])
        s_ps = ps("o_s_ps", [P, HALF])

        names = """w_hi_ready w_lo_ready sign_ready small_in zero_ready scale_hi scale_ready
            sum_ready den_in den_rec r_out at_ready ahi_ready alo_ready w_mm x1_ready stat_step var_ready rstd_ready
            xn_ready x1b_ready gate_hi gate_ready xt_mm xhi_ready xlo_ready xt_ready lgsum_ready lg_mm lg_ready lt_mm neg_ready ex_ready rden_ready route_hi
            route_ready rt_mm rt_ready is_mm xs_ready xshi_ready xslo_ready os_mm osc_ready f_mm y_ready
            yout_ready const_ready waited_sp waited_pe waited_dve""".split()
        S = {k: sem("o_" + k) for k in names}
        scales_in = [sem(f"o_scales_in{i}") for i in two]
        xin = [sem(f"o_xin{i}") for i in two]
        out_done = sem("o_out_done")
        wf_v = wf_t.rearrange("(c p) h -> c p h", p=P)

        PEEL, LOOPS = 3, 5

        def schedule(eng, emit, first=-1):
            for n in range(first, PEEL):
                emit(n, n, n % 2)
            with eng.Fori(PEEL // 2, PEEL // 2 + LOOPS) as j:
                emit(None, 2 * j + 1, 1)
                emit(None, 2 * j + 2, 0)
            for n in range(PEEL + 2 * LOOPS, NT + 2):
                emit(n, n, n % 2)

        def on(static, ahead):
            return static is None or 0 <= static + ahead < NT

        def past(static, ahead, least):
            return static is None or static + ahead >= least

        def slot(static, n, par, ahead):
            return (static + ahead) // 2 if static is not None else None

        chunks = lambda ap: ap.rearrange("p k (c t) -> p (k c) t", c=NC // 2)

        with nc.Block() as block:
            @block.sync
            def _(sp):
                sp.dma_start(gate[:], gate_t).then_inc(S["small_in"], 16)
                sp.dma_start(bias_b[:], bias.rearrange("(a d) -> a d", a=1).broadcast_to([P, D])).then_inc(S["small_in"], 16)

                def load_wf(c):
                    sp.wait_ge(S["w_lo_ready"], c + 1)
                    sp.dma_start(raw[c], wf_v[c]).then_inc(w_in[c], 16)

                def load_scales(i, src):
                    sp.wait_ge(S["zero_ready"], i + 1)
                    for r in range(3):
                        sp.dma_start(s_raw[i][32 * r:32 * r + NE, :], src).then_inc(scales_in[i], 16)

                def emit(s, n, par):
                    if on(s, 1):
                        if past(s, 0, 0):
                            sp.wait_ge(S["at_ready"], n + 1)
                            sp.sem_inc(S["waited_sp"], 1)
                        if past(s, -1, 0):
                            sp.wait_ge(S["alo_ready"], n)
                        t0 = (n + 1) * TT
                        if s != -1:
                            load_attention(sp, (a_t[1 - par], b_t, r_t), o_scr, r_scr, t0, at_in)
                        if past(s, -1, 0):
                            sp.wait_ge(S["x1_ready"], 2 * n)
                        sp.dma_start(x_in[1 - par][:], x[bass.ds(t0, TT), :]).then_inc(xin[1 - par], 16)

                emit(-1, -1, 1)
                sp.dma_start(den[:], denominators(o_scr, 2 * HD, NDB, B)).then_inc(S["den_in"], 16)
                load_scales(0, in_scale)
                load_scales(1, out_scale)
                emit(0, 0, 0)
                for c in range(NC):
                    if c == 5:
                        emit(1, 1, 1)
                    load_wf(c)
                    if c == 4:
                        sp.wait_ge(S["den_rec"], 1)
                        sp.dma_start(denominators(r_scr, 0, NDB, B), den[:]).then_inc(S["r_out"], 16)
                sp.wait_ge(S["r_out"], 16)
                schedule(sp, emit, 2)

            @block.gpsimd
            def _(pool):
                pool.memset(s_raw[0], 0.0).then_inc(S["zero_ready"], 1)
                pool.wait_ge(S["zero_ready"], 1)
                pool.memset(s_raw[1], 0.0).then_inc(S["zero_ready"], 1)
                pool.wait_ge(S["zero_ready"], 2)
                for i, st in enumerate((s_in, s_out)):
                    pool.wait_ge(S["scale_hi"], i + 1)
                    pool.tensor_tensor(st[64:EROWS, :], s_raw[i][64:EROWS, :], f(st[64:EROWS, :]),
                                       ALU.subtract).then_inc(S["scale_ready"], 1)
                    pool.wait_ge(S["scale_ready"], i + 1)
                pool.wait_ge(S["const_ready"], 1)
                pool.wait_ge(S["small_in"], 2 * 16)

                def emit(s, n, par):
                    if on(s, 1) and s != -1:
                        pool.wait_ge(S["ahi_ready"], n + 2)
                        if past(s, 0, 1):
                            pool.wait_ge(S["w_mm"], 2 * n)
                        pool.tensor_tensor(a_lo[1 - par][:], a_t[1 - par][:], f(a_hi[1 - par][:]),
                                           ALU.subtract).then_inc(S["alo_ready"], 1)
                    if on(s, 0):
                        pool.wait_ge(S["var_ready"], n + 1)
                        pool.tensor_tensor(rstd[:], var[:], half_pow[:], ALU.pow).then_inc(S["rstd_ready"], 1)
                    if on(s, -2):
                        for h in range(2):
                            hs = slice(HALF * h, HALF * (h + 1))
                            pool.wait_ge(S["y_ready"], 2 * (n - 2) + h + 1)
                            pool.tensor_tensor(y[:, hs], y[:, hs], x1b[par][:, hs], ALU.add).then_inc(S["yout_ready"], 1)
                        pool.wait_ge(S["yout_ready"], 2 * (n - 1))
                        pool.dma_start(out[bass.ds((n - 2) * TT, TT), :], y).then_inc(out_done, 16)
                    if on(s, 0):
                        pool.wait_ge(S["x1_ready"], 2 * n + 2)
                        if s == 0:
                            pool.wait_ge(S["sign_ready"], 3)
                        if past(s, 0, 2):
                            pool.wait_ge(S["yout_ready"], 2 * (n - 1))
                        pool.tensor_tensor(x1b[par][:], x1[par][:], bias_b[:], ALU.add).then_inc(S["x1b_ready"], 1)

                schedule(pool, emit)
                pool.wait_ge(out_done, 16 * NT)

            @block.tensor
            def _(pe):
                def wo_chunk(par, c, h):
                    hs = slice(HALF * h, HALF * (h + 1))
                    pe.matmul(w_ps[:, h, :], a_hi[par][:, c, :], wo_hi[:, c, hs], start=(c == 0), stop=False)
                    pe.matmul(w_ps[:, h, :], a_hi[par][:, c, :], wo_lo[:, c, hs], start=False, stop=False)
                    return pe.matmul(w_ps[:, h, :], a_lo[par][:, c, :], wo_hi[:, c, hs], start=False, stop=(c == NC - 1))

                def wo(s, n, par, h, between=None):
                    if h == 0:
                        pe.wait_ge(S["alo_ready"], n + 1)
                    if past(s, 0, 1):
                        pe.wait_ge(S["x1_ready"], 2 * n - 1 + h)
                    for c in range(NC):
                        if c == NC // 2 and between:
                            between()
                        mm = wo_chunk(par, c, h)
                    mm.then_inc(S["w_mm"], 1)

                def wo_first():
                    pe.wait_ge(S["alo_ready"], 1)
                    for c in range(NC):
                        pe.wait_ge(S["w_lo_ready"], c + 1)
                        for h in range(2):
                            mm = wo_chunk(0, c, h)
                            if c == NC - 1:
                                mm.then_inc(S["w_mm"], 1)

                def turn_routes(s, m):
                    pe.wait_ge(S["route_ready"], m + 1)
                    pe.transpose(s_ps[0:EROWS, 0:TT], route[:], ident[:]).then_inc(S["rt_mm"], 1)

                def scale_in(s, m):
                    pe.wait_ge(S["rt_ready"], m + 1)
                    pe.wait_ge(S["xt_ready"], m + 1)
                    for c in range(NC):
                        mm = pe.matmul(x_ps[:, c // 4, (c % 4) * TT:(c % 4 + 1) * TT], s_in[:, c * P:(c + 1) * P],
                                       route_t[:], start=True, stop=True)
                    mm.then_inc(S["is_mm"], 1)

                def scale_out(s, m, h):
                    if not (h == 0 and s is not None and s == 2):
                        pe.wait_ge(S["osc_ready"], 2 * m + h)
                    pe.matmul(o_ps[:], route_t[:], s_out[:, HALF * h:HALF * (h + 1)], start=True, stop=True).then_inc(S["os_mm"], 1)

                def turn_x(s, m):
                    pe.wait_ge(S["xn_ready"], m + 1)
                    if s is None or s >= 2:
                        pe.wait_ge(S["xs_ready"], m)
                    for c in range(NC):
                        mm = pe.transpose(x_ps[:, c // 4, (c % 4) * TT:(c % 4 + 1) * TT], x_n[:, c * P:(c + 1) * P], ident[:])
                    mm.then_inc(S["xt_mm"], 1)

                def logits(s, m, par):
                    pe.wait_ge(S["xlo_ready"], m + 1)
                    if s == 1:
                        pe.wait_ge(S["gate_ready"], 1)
                    if s is None or s >= 2:
                        pe.wait_ge(S["rt_ready"], m)
                    for c in range(NC):
                        pe.matmul(s_ps[0:2 * NE, 0:TT], gate_hl[:, c, :], x_hi[:, c, :], start=(c == 0), stop=False)
                        mm = pe.matmul(s_ps[0:2 * NE, 0:TT], gate_hl[:, c, :], x_lo[:, c, :], start=False, stop=(c == NC - 1))
                    mm.then_inc(S["lg_mm"], 1)

                def ffn(s, m, h, between=None):
                    if h == 0:
                        pe.wait_ge(S["xslo_ready"], m + 1)
                    if s is None or s > 2:
                        pe.wait_ge(S["y_ready"], 2 * m - 1 + h)
                    hs = slice(HALF * h, HALF * (h + 1))
                    for c in range(NC):
                        if c == NC // 2 and between:
                            between()
                        if s == 2 and h == 0:
                            pe.wait_ge(S["sign_ready"], c + 1)
                        pe.matmul(f_ps[:, h, :], xs_hi[:, c, :], sign[:, c, hs], start=(c == 0), stop=False)
                        mm = pe.matmul(f_ps[:, h, :], xs_lo[:, c, :], sign[:, c, hs], start=False, stop=(c == NC - 1))
                    mm.then_inc(S["f_mm"], 1)

                def turn_logits(s, m):
                    pe.wait_ge(S["lg_ready"], m + 1)
                    pe.sem_inc(S["waited_pe"], 1)
                    pe.transpose(s_ps[0:TT, 0:2 * NE], lg_t[:], ident[0:2 * NE, 0:2 * NE]).then_inc(S["lt_mm"], 1)

                def emit(s, n, par):
                    routes = (lambda: turn_routes(s, n - 2)) if on(s, -2) else None
                    turned = (lambda: turn_logits(s, n - 1)) if on(s, -1) else None
                    if s == 0:
                        wo_first()
                    elif on(s, 0):
                        wo(s, n, par, 0, routes)
                    elif routes:
                        routes()
                    if on(s, -2):
                        if s == 2:
                            pe.wait_ge(S["scale_ready"], 2)
                        scale_in(s, n - 2)
                        scale_out(s, n - 2, 0)
                    if on(s, 0) and s != 0:
                        wo(s, n, par, 1)
                    if on(s, -1):
                        turn_x(s, n - 1)
                    if on(s, -2):
                        scale_out(s, n - 2, 1)
                        ffn(s, n - 2, 0)
                    if on(s, -1):
                        logits(s, n - 1, 1 - par)
                    if on(s, -2):
                        ffn(s, n - 2, 1, turned)
                    elif turned:
                        turned()

                pe.wait_ge(S["small_in"], 2 * 16)
                schedule(pe, emit)

            @block.scalar
            def _(act):
                def signs(half):
                    for c in range(4 * half, 4 * half + 4):
                        act.wait_ge(w_in[c], 32)
                        act.activation(sign[:, c, :], raw[c], ACT.Sign).then_inc(S["sign_ready"], 1)

                def emit(s, n, par):
                    if on(s, 1):
                        act.wait_ge(S["at_ready"], n + 2)
                        if past(s, 0, 1):
                            act.wait_ge(S["w_mm"], 2 * n)
                            act.wait_ge(S["alo_ready"], n)
                        act.copy(a_hi[1 - par][:], a_t[1 - par][:]).then_inc(S["ahi_ready"], 1)
                    if s == 1:
                        signs(1)
                        act.wait_ge(S["sign_ready"], NC)
                    if on(s, -2):
                        act.wait_ge(S["os_mm"], 2 * (n - 2) + 1)
                        if past(s, -2, 1):
                            act.wait_ge(S["y_ready"], 2 * (n - 2))
                        act.copy(osc[:, 0:HALF], o_ps[:]).then_inc(S["osc_ready"], 1)
                        act.wait_ge(S["xs_ready"], n - 1)
                        if past(s, -2, 1):
                            act.wait_ge(S["f_mm"], 2 * (n - 2))
                        act.copy(xs_hi[:], xs[:]).then_inc(S["xshi_ready"], 1)
                    if on(s, -1):
                        act.wait_ge(S["xt_mm"], n)
                        if past(s, -1, 1):
                            act.wait_ge(S["lg_mm"], n - 1)
                        act.copy(x_t[1 - par][:], chunks(x_ps[:])).then_inc(S["xt_ready"], 1)
                        act.wait_ge(S["xt_ready"], n)
                        act.copy(x_hi[:], x_t[1 - par]).then_inc(S["xhi_ready"], 1)
                    if on(s, -2):
                        act.wait_ge(S["os_mm"], 2 * (n - 2) + 2)
                        act.copy(osc[:, HALF:D], o_ps[:]).then_inc(S["osc_ready"], 1)
                    if on(s, -1):
                        act.wait_ge(S["lg_mm"], n)
                        act.copy(lg_t[:], s_ps[0:2 * NE, 0:TT]).then_inc(S["lg_ready"], 1)
                        act.wait_ge(S["neg_ready"], n)
                        act.activation(ex[:], lg[:], ACT.Exp, bias=neg[:], accum_out=esum[:]).then_inc(S["ex_ready"], 1)

                for c in range(NC):
                    act.wait_ge(w_in[c], 16)
                    act.copy(wo_hi[:, c, :], raw[c]).then_inc(S["w_hi_ready"], 1)
                    if c == 1:
                        emit(-1, -1, 1)
                    if c == 3:
                        act.wait_ge(S["small_in"], 2 * 16)
                        act.copy(gate_hl[:, :, 0:NE], gate[:]).then_inc(S["gate_hi"], 1)
                    if c == 4:
                        for i, st in enumerate((s_in, s_out)):
                            act.wait_ge(scales_in[i], 3 * 16)
                            act.copy(st[:], s_raw[i]).then_inc(S["scale_hi"], 1)
                emit(0, 0, 0)
                signs(0)
                schedule(act, emit, 1)

            @block.vector
            def _(dve):
                def combine(s, m, par):
                    dve.wait_ge(at_in, 3 * REP * 16 * (m + 1))
                    dve.tensor_tensor(a_t[par][:], a_t[par][:], b_t[:], ALU.add).then_inc(S["sum_ready"], 1)

                def normalise_a(s, m, par):
                    dve.wait_ge(S["sum_ready"], m + 1)
                    dve.tensor_tensor(a_t[par][:], a_t[par][:], r_t[:], ALU.mult).then_inc(S["at_ready"], 1)

                def add_x(s, m, par, jj, h):
                    hs = slice(HALF * h, HALF * (h + 1))
                    dve.wait_ge(S["w_mm"], 2 * m + h + 1)
                    if s in (0, 1) and h == 0:
                        dve.wait_ge(S["scale_ready"], 2 - s)
                    if h == 0:
                        if s is None:
                            dve.wait_ge(xin[par], jj)
                        else:
                            dve.wait_ge(xin[par], 16 * (s // 2 + 1))
                        if past(s, 0, 2):
                            dve.wait_ge(S["x1b_ready"], m - 1)
                    dve.tensor_tensor(x1[par][:, hs], w_ps[:, h, :], x_in[par][:, hs], ALU.add).then_inc(S["x1_ready"], 1)

                def normalise(s, m, par):
                    if past(s, 0, 1):
                        dve.wait_ge(S["xt_mm"], m)
                    for h in range(2):
                        dve.wait_ge(S["x1_ready"], 2 * m + h + 1)
                        dve.bn_stats(stats[:, 6 * h:6 * h + 6], x1[par][:, HALF * h:HALF * (h + 1)]).then_inc(S["stat_step"], 1)
                    dve.wait_ge(S["stat_step"], 3 * m + 2)
                    dve.sem_inc(S["waited_dve"], 1)
                    dve.bn_aggr(mv[:], stats[:]).then_inc(S["stat_step"], 1)
                    dve.wait_ge(S["stat_step"], 3 * m + 3)
                    dve.tensor_scalar(var[:], mv[:, 1:2], 1.0, EPS, ALU.mult, ALU.add).then_inc(S["var_ready"], 1)
                    if on(s, -1):
                        split_x(m - 1, 1 - par)
                    dve.wait_ge(S["rstd_ready"], m + 1)
                    if s == 0:
                        dve.wait_ge(S["sign_ready"], 1)
                    dve.tensor_scalar(x_n, x1[par][:], mv[:, 0:1], rstd[:], ALU.subtract, ALU.mult).then_inc(S["xn_ready"], 1)

                def split_x(m, par):
                    dve.wait_ge(S["xhi_ready"], m + 1)
                    dve.tensor_tensor(x_lo[:], x_t[par], f(x_hi[:]), ALU.subtract).then_inc(S["xlo_ready"], 1)

                def scale_x(s, m, par):
                    dve.wait_ge(S["is_mm"], m + 1)
                    if s == 2:
                        dve.wait_ge(S["sign_ready"], NC)
                    if past(s, -2, 1):
                        dve.wait_ge(S["xslo_ready"], m)
                    dve.tensor_tensor(xs[:], chunks(x_ps[:]), x_t[par][:], ALU.mult).then_inc(S["xs_ready"], 1)
                    dve.wait_ge(S["xshi_ready"], m + 1)
                    dve.tensor_tensor(xs_lo[:], xs[:], f(xs_hi[:]), ALU.subtract).then_inc(S["xslo_ready"], 1)

                def scale_y(s, m, h):
                    hs = slice(HALF * h, HALF * (h + 1))
                    dve.wait_ge(S["f_mm"], 2 * m + h + 1)
                    dve.wait_ge(S["osc_ready"], 2 * m + h + 1)
                    if h == 0 and past(s, -2, 1):
                        dve.wait_ge(out_done, 16 * m)
                    dve.tensor_tensor(y[:, hs], f_ps[:, h, :], osc[:, hs], ALU.mult).then_inc(S["y_ready"], 1)

                def routing(s, m):
                    dve.wait_ge(S["lt_mm"], m + 1)
                    if past(s, -1, 1):
                        dve.wait_ge(S["ex_ready"], m)
                    dve.tensor_reduce(lg[:], s_ps[0:TT, 0:2 * NE].rearrange("t (k e) -> t e k", k=2), AX,
                                      ALU.add).then_inc(S["lgsum_ready"], 1)
                    dve.wait_ge(S["lgsum_ready"], m + 1)
                    dve.tensor_reduce(neg[:], lg[:], AX, ALU.max, negate=True).then_inc(S["neg_ready"], 1)
                    dve.wait_ge(S["ex_ready"], m + 1)
                    dve.reciprocal(rden[:], esum[:]).then_inc(S["rden_ready"], 1)
                    dve.wait_ge(S["rden_ready"], m + 1)
                    for k in (0, 64):
                        dve.tensor_scalar(route[:, k:k + NE].bitcast(F32R), ex[:], rden[:], None, ALU.mult).then_inc(S["route_hi"], 1)
                    dve.wait_ge(S["route_hi"], 2 * m + 2)
                    dve.scalar_tensor_tensor(out=route[:, 32:32 + NE], in0=ex[:], scalar=rden[:],
                                             in1=route[:, 0:NE], op0=ALU.mult, op1=ALU.subtract).then_inc(S["route_ready"], 1)

                def emit(s, n, par):
                    if on(s, 1) and s != 0:
                        combine(s, n + 1, 1 - par)
                    if on(s, -2):
                        dve.wait_ge(S["rt_mm"], n - 1)
                        dve.tensor_copy(route_t[:], s_ps[0:EROWS, 0:TT]).then_inc(S["rt_ready"], 1)
                    if on(s, 1) and s != 0:
                        normalise_a(s, n + 1, 1 - par)
                    if on(s, 0):
                        jj = None if s is not None else (8 * n + 16 if par == 0 else 8 * n + 8)
                        add_x(s, n, par, jj, 0)
                    if on(s, -2):
                        scale_x(s, n - 2, par)
                    if on(s, 0):
                        add_x(s, n, par, jj, 1)
                        normalise(s, n, par)
                    elif on(s, -1):
                        split_x(n - 1, 1 - par)
                    if on(s, -2):
                        scale_y(s, n - 2, 0)
                    if on(s, -1):
                        routing(s, n - 1)
                    if on(s, -2):
                        scale_y(s, n - 2, 1)

                emit(-1, -1, 1)
                dve.memset(half_pow[:], -0.5).then_inc(S["const_ready"], 1)
                dve.memset(route[:], 0.0).then_inc(S["const_ready"], 1)
                for c in range(NC):
                    if c == 6:
                        combine(0, 1, 1)
                        normalise_a(0, 1, 1)
                    dve.wait_ge(S["w_hi_ready"], c + 1)
                    dve.tensor_tensor(wo_lo[:, c, :], raw[c], f(wo_hi[:, c, :]), ALU.subtract).then_inc(S["w_lo_ready"], 1)
                    if c == 0:
                        dve.wait_ge(S["ahi_ready"], 1)
                        dve.tensor_tensor(a_lo[0][:], a_t[0], f(a_hi[0][:]), ALU.subtract).then_inc(S["alo_ready"], 1)
                    if c == 4:
                        dve.wait_ge(S["den_in"], 16)
                        dve.reciprocal(den[:], den[:]).then_inc(S["den_rec"], 1)
                        dve.wait_ge(S["gate_hi"], 1)
                        dve.tensor_tensor(gate_hl[:, :, NE:2 * NE], gate[:], f(gate_hl[:, :, 0:NE]),
                                          ALU.subtract).then_inc(S["gate_ready"], 1)
                emit(0, 0, 0)
                schedule(dve, emit, 1)


def build(nc, x, ctx_t, wq_t, wkv_t, wo_t, ln_w, wf_t, bias, gate_t, in_scale, out_scale, out):
    q_scr = nc.dram_tensor("q_scratch", (2, HD, B, NG, REP, Q), F32).ap()
    o_scr = nc.dram_tensor("o_scratch", (VW, NG, REP, B, Q), F32).ap()
    r_scr = nc.dram_tensor("r_scratch", (1, NG, REP, T), F32).ap()
    with ExitStack() as ctx:
        ident = ctx.enter_context(nc.sbuf_tensor("ident", [P, P], F32))
        zeroed = ctx.enter_context(nc.semaphore("ident_zeroed"))
        with nc.Block() as block:
            @block.gpsimd
            def _(pool):
                pool.memset(ident[:], 0.0).then_inc(zeroed, 1)
                pool.wait_ge(zeroed, 1)
                pool.affine_select(out=ident[:], in_=ident[:], compare_op=ALU.not_equal, fill=1.0, base=0,
                                   pattern=[[-1, P]], channel_multiplier=1).then_inc(zeroed, 1)
                pool.wait_ge(zeroed, 2)
        kv_at = nc.sbuf_base
        kv_hi = ctx.enter_context(nc.sbuf_tensor("kv_hi", [P, NC, 2 * NG * HD], F32R))
        kv_lo = ctx.enter_context(nc.sbuf_tensor("kv_lo", [P, NC, 2 * NG * HD], F32R))
        wo_raw = nc.alloc_sbuf_tensor_at("wo_raw", [P, NC, D], F32, offset=kv_at)
        spare = ctx.enter_context(nc.sbuf_tensor("spare", [P, 3 * D], F32))
        c_in = ctx.enter_context(nc.semaphore("c_in"))
        w_in = [ctx.enter_context(nc.semaphore(f"o_w_in{i}")) for i in range(NC)]
        at_in = ctx.enter_context(nc.semaphore("o_at_in"))
        early = ctx.enter_context(ExitStack())
        xc = [early.enter_context(nc.sbuf_tensor(f"x_or_context_{n}", [P, NC, QG], F32R)) for n in ("hi", "lo")]
        p_bufs = [early.enter_context(nc.sbuf_tensor(f"p_buf{i}", [P, KC, REP * Q], F32R)) for i in range(3)]
        c_ready = [ctx.enter_context(nc.semaphore(f"c_{n}_ready")) for n in ("hi", "lo")]
        q_out = [ctx.enter_context(nc.semaphore(f"q_out{i}")) for i in range(4)]
        phase_queries(nc, x, wq_t, ln_w, wkv_t, ctx_t, q_scr, ident, kv_hi, kv_lo, spare, c_in, c_ready, xc, p_bufs, q_out)
        phase_attention(nc, ctx_t, q_scr, o_scr, ident, kv_hi, kv_lo, wo_raw, spare, c_in, c_ready, xc, p_bufs, q_out,
                        wo_t, r_scr, w_in, at_in)
        early.close()
        phase_output(nc, x.rearrange("b q d -> (b q) d"), wf_t, bias, gate_t, in_scale, out_scale,
                     o_scr.rearrange("v g r b q -> v g r (b q)"), r_scr, out, ident, wo_raw, spare, w_in, at_in)


def kernel(x, ctx_4096, L0_xattn_wq, L0_xattn_wk, L0_xattn_wv, L0_xattn_wo, L0_xattn_ln_w, L0_ffn_weight,
           L0_ffn_bias, L0_ffn_gate_w, L0_ffn_in_channel_scale, L0_ffn_out_channel_scale):
    import concourse.bacc as bacc
    from concourse.bass_utils import run_bass_kernel_spmd

    lay = lambda a: np.ascontiguousarray(a)
    ctx = np.zeros((B, NC, P, KP), np.float32)
    ctx[:, :, :, :K] = np.asarray(ctx_4096).transpose(0, 2, 1).reshape(B, NC, P, K)
    wkv = np.concatenate([np.asarray(L0_xattn_wk).T, np.asarray(L0_xattn_wv).T], axis=1)
    arrays = {
        "x": lay(x),
        "ctx_t": lay(ctx.transpose(0, 2, 1, 3)),
        "wq_t": lay(np.asarray(L0_xattn_wq).T),
        "wkv_t": lay(wkv.reshape(NC, P, 2 * NG * HD)),
        "wo_t": lay(np.asarray(L0_xattn_wo).T),
        "ln_w": lay(np.asarray(L0_xattn_ln_w).reshape(NC, P).T),
        "wf_t": lay(np.asarray(L0_ffn_weight).T),
        "bias": lay(L0_ffn_bias),
        "gate_t": lay(np.asarray(L0_ffn_gate_w).T.reshape(NC, P, NE).transpose(1, 0, 2)),
        "in_scale": lay(L0_ffn_in_channel_scale),
        "out_scale": lay(L0_ffn_out_channel_scale),
    }
    nc = bacc.Bacc("TRN2", target_bir_lowering=False, num_devices=1)
    args = [nc.dram_tensor(f"in_{n}", a.shape, mybir.dt.from_np(a.dtype), kind="ExternalInput").ap()
            for n, a in arrays.items()]
    out = nc.dram_tensor("out", (T, D), F32, kind="ExternalOutput").ap()
    build(nc, *args, out)
    got = run_bass_kernel_spmd(nc, [{f"in_{n}": a for n, a in arrays.items()}], core_ids=[0])
    return got.results[0]["out"].reshape(B, Q, D)
```
